# Optimizing a Trainium2 kernel written in Bass

```python
import numpy as np
import jax
import jax.numpy as jnp

def _softmax(x, axis=-1):
    return jax.nn.softmax(x, axis=axis)

def _gelu(x):
    return jax.nn.gelu(x, approximate=True)

def _silu(x):
    return jax.nn.silu(x)

def _sigmoid(x):
    return jax.nn.sigmoid(x)

def _layernorm(x, axis=-1, eps=1e-05):
    m = jnp.mean(x, axis=axis, keepdims=True)
    v = jnp.var(x, axis=axis, keepdims=True)
    return (x - m) / jnp.sqrt(v + eps)

def _scatter_add(tgt, idx, src, axis=0):
    return tgt.at[idx].add(src)

def _segment_sum(src, seg, n):
    return jax.ops.segment_sum(src, seg, n)
kernel_name = 'mk_decoder_preln_d2_seqx_r8_1df8b4'

def setup_inputs(seed: int=0):
    np.random.seed(seed)
    _w = jnp.asarray

    def _rec_inputs():
        import jax
        import jax.numpy as jnp
        _rk = jax.random.key(seed)
        x = 0.002226 + 0.9996 * jax.random.normal(jax.random.fold_in(_rk, 1), (4, 256, 128), jnp.float32)
        _lenS = 256 - jax.random.randint(jax.random.fold_in(_rk, 7), (4,), 0, max(1, 256 // 4) + 1, jnp.int32)
        _lenS2 = 512 - jax.random.randint(jax.random.fold_in(_rk, 8), (4,), 0, max(1, 512 // 4) + 1, jnp.int32)
        _ctx_1024P = jax.random.normal(jax.random.fold_in(_rk, 11), (4, 16, 128), jnp.float32)
        _ctx_1024c = jax.random.dirichlet(jax.random.fold_in(_rk, 511), 0.3 * jnp.ones((16,), jnp.float32), (4, 512))
        _ctx_1024t = jnp.einsum('bsk,bkd->bsd', _ctx_1024c, _ctx_1024P)
        _ctx_1024t = _ctx_1024t * jax.lax.rsqrt(jnp.mean(jnp.square(_ctx_1024t)) + 1e-12) * 0.953939
        ctx_1024 = -0.000125008 + 0.999885 * (_ctx_1024t + 0.3 * jax.random.normal(jax.random.fold_in(_rk, 611), (4, 512, 128), jnp.float32))
        _validS = jnp.arange(256)[None, :] < _lenS[:, None]
        _validS2 = jnp.arange(512)[None, :] < _lenS2[:, None]
        _causal = jnp.tril(jnp.ones((256, 256), dtype=bool))
        mask_1xSxS2_ff0 = jnp.where(jnp.ones((1, 256, 512), dtype=bool), 0.0, -1000000000.0).astype(jnp.float32)
        return (x, ctx_1024, mask_1xSxS2_ff0)
    x, ctx_1024, mask_1xSxS2_ff0 = _rec_inputs()

    def _L0_attn_setup():
        import jax, jax.numpy as jnp
        import numpy as np
        B, T, C, H = (2, 256, 128, 16)
        R = 32
        LORA_SCALE = 0.5
        HD = C // H

        def lora_linear(x, w, b, la, lb):
            return x @ w.T + b + LORA_SCALE * (x @ la.T @ lb.T)
        key = jax.random.key(seed)
        ks = jax.random.split(key, 8)
        std = 0.02
        return {'x': jax.random.normal(ks[0], (B, T, C), jnp.float32), 'w_attn': jax.random.normal(ks[1], (3 * C, C), jnp.float32) * std, 'b_attn': jnp.zeros((3 * C,), jnp.float32), 'la_attn': jax.random.normal(ks[2], (R, C), jnp.float32) * std, 'lb_attn': jax.random.normal(ks[3], (3 * C, R), jnp.float32) * std, 'w_proj': jax.random.normal(ks[4], (C, C), jnp.float32) * std, 'b_proj': jnp.zeros((C,), jnp.float32), 'la_proj': jax.random.normal(ks[5], (R, C), jnp.float32) * std, 'lb_proj': jax.random.normal(ks[6], (C, R), jnp.float32) * std}
    _L0_attn_all = _L0_attn_setup()
    _L0_attn_in = {k: v for k, v in _L0_attn_all.items() if k in ('w_attn', 'b_attn', 'la_attn', 'lb_attn', 'w_proj', 'b_proj', 'la_proj', 'lb_proj')}
    del _L0_attn_all

    def _L0_xattn_setup():
        import jax, jax.numpy as jnp
        import numpy as np
        EPS = 1e-05

        def layer_norm(x, g, b):
            mu = jnp.mean(x, axis=-1, keepdims=True)
            var = jnp.var(x, axis=-1, keepdims=True)
            return (x - mu) * jax.lax.rsqrt(var + EPS) * g + b
        key = jax.random.key(seed)
        ks = jax.random.split(key, 8)
        dim, heads, dim_head = (128, 16, 64)
        inner = heads * dim_head
        b, n, m = (8, 512, 64)
        s = dim ** (-0.5)
        return {'x': jax.random.normal(ks[0], (b, n, dim), jnp.float32), 'latents': jax.random.normal(ks[1], (b, m, dim), jnp.float32), 'ln_m_g': jnp.ones((dim,), jnp.float32), 'ln_m_b': jnp.zeros((dim,), jnp.float32), 'ln_l_g': jnp.ones((dim,), jnp.float32), 'ln_l_b': jnp.zeros((dim,), jnp.float32), 'Wq': jax.random.normal(ks[2], (dim, inner), jnp.float32) * s, 'Wkv': jax.random.normal(ks[3], (dim, 2 * inner), jnp.float32) * s, 'Wout': jax.random.normal(ks[4], (inner, dim), jnp.float32) * s}
    _L0_xattn_all = _L0_xattn_setup()
    _L0_xattn_in = {k: v for k, v in _L0_xattn_all.items() if k in ('ln_m_g', 'ln_m_b', 'ln_l_g', 'ln_l_b', 'Wq', 'Wkv', 'Wout')}
    del _L0_xattn_all

    def _L0_ffn_setup():
        import jax, jax.numpy as jnp
        import numpy as np
        DIM, HEADS, FFN, E = (128, 16, 512, 8)
        B, S = (2, 128)
        EPS = 1e-05

        def _ln(x, g, b):
            mu = jnp.mean(x, axis=-1, keepdims=True)
            var = jnp.mean((x - mu) ** 2, axis=-1, keepdims=True)
            return (x - mu) * jax.lax.rsqrt(var + EPS) * g + b
        key = jax.random.key(seed)
        ks = jax.random.split(key, 20)
        sd = 0.02
        d, f = (DIM, FFN)
        return {'x': jax.random.normal(ks[0], (B, S, d), jnp.float32), 'ln1_g': jnp.ones((d,), jnp.float32), 'ln1_b': jnp.zeros((d,), jnp.float32), 'Wqkv': jax.random.normal(ks[1], (d, 3 * d), jnp.float32) * sd, 'bqkv': jnp.zeros((3 * d,), jnp.float32), 'Wo': jax.random.normal(ks[2], (d, d), jnp.float32) * sd, 'bo': jnp.zeros((d,), jnp.float32), 'ln2_g': jnp.ones((d,), jnp.float32), 'ln2_b': jnp.zeros((d,), jnp.float32), 'gate_w': jax.random.normal(ks[3], (d, E), jnp.float32) * sd, 'W1': jax.random.normal(ks[4], (E, d, f), jnp.float32) * sd, 'b1': jnp.zeros((E, f), jnp.float32), 'W2': jax.random.normal(ks[5], (E, f, d), jnp.float32) * sd, 'b2': jnp.zeros((E, d), jnp.float32), 'rW1': jax.random.normal(ks[6], (d, f), jnp.float32) * sd, 'rb1': jnp.zeros((f,), jnp.float32), 'rW2': jax.random.normal(ks[7], (f, d), jnp.float32) * sd, 'rb2': jnp.zeros((d,), jnp.float32), 'coef_w': jax.random.normal(ks[8], (d, 2), jnp.float32) * sd, 'coef_b': jnp.zeros((2,), jnp.float32)}
    _L0_ffn_all = _L0_ffn_setup()
    _L0_ffn_in = {k: v for k, v in _L0_ffn_all.items() if k in ('ln1_g', 'ln1_b', 'Wqkv', 'bqkv', 'Wo', 'bo', 'ln2_g', 'ln2_b', 'gate_w', 'W1', 'b1', 'W2', 'b2', 'rW1', 'rb1', 'rW2', 'rb2', 'coef_w', 'coef_b')}
    del _L0_ffn_all

    def _L1_attn_setup():
        import jax, jax.numpy as jnp
        import numpy as np
        B, T, DIM, H = (2, 256, 128, 16)
        HD = DIM // H

        def _custom_softmax(a):
            a = jnp.clip(a, -100.0, 100.0)
            m = jnp.max(a, axis=-1, keepdims=True)
            e = jnp.exp(a - m)
            p = e / (jnp.sum(e, axis=-1, keepdims=True) + 1e-06)
            p = p + 1e-08
            return p / jnp.sum(p, axis=-1, keepdims=True)
        key = jax.random.key(seed)
        k1, k2, k3 = jax.random.split(key, 3)
        x = jax.random.normal(k1, (B, T, DIM), dtype=jnp.float32)
        w_qkv = jax.random.normal(k2, (3 * DIM, DIM), dtype=jnp.float32) / np.sqrt(DIM)
        w_proj = jax.random.normal(k3, (DIM, DIM), dtype=jnp.float32) / np.sqrt(DIM)
        return {'x': x, 'w_qkv': w_qkv, 'w_proj': w_proj}
    _L1_attn_all = _L1_attn_setup()
    _L1_attn_in = {k: v for k, v in _L1_attn_all.items() if k in ('w_qkv', 'w_proj')}
    del _L1_attn_all

    def _L1_xattn_setup():
        import jax, jax.numpy as jnp
        import numpy as np
        INP_SIZE = 128
        D_MODEL = 128
        B, S = (4, 256)
        key = jax.random.key(seed)
        ks = jax.random.split(key, 9)
        q = jax.random.normal(ks[0], (B, S, INP_SIZE), dtype=jnp.float32)
        k = jax.random.normal(ks[1], (B, S, INP_SIZE), dtype=jnp.float32)
        v = jax.random.normal(ks[2], (B, S, INP_SIZE), dtype=jnp.float32)
        mask = jnp.zeros((1, S, S), dtype=jnp.float32)
        kernel_q = jax.random.normal(ks[3], (INP_SIZE, D_MODEL), dtype=jnp.float32) * 0.05
        kernel_k = jax.random.normal(ks[4], (INP_SIZE, D_MODEL), dtype=jnp.float32) * 0.05
        kernel_v = jax.random.normal(ks[5], (INP_SIZE, D_MODEL), dtype=jnp.float32) * 0.05
        bias_q = jax.random.normal(ks[6], (D_MODEL,), dtype=jnp.float32) * 0.05
        bias_k = jax.random.normal(ks[7], (D_MODEL,), dtype=jnp.float32) * 0.05
        bias_v = jax.random.normal(ks[8], (D_MODEL,), dtype=jnp.float32) * 0.05
        return {'q': q, 'k': k, 'v': v, 'mask': mask, 'kernel_q': kernel_q, 'bias_q': bias_q, 'kernel_k': kernel_k, 'bias_k': bias_k, 'kernel_v': kernel_v, 'bias_v': bias_v}
    _L1_xattn_all = _L1_xattn_setup()
    _L1_xattn_in = {k: v for k, v in _L1_xattn_all.items() if k in ('kernel_q', 'bias_q', 'kernel_k', 'bias_k', 'kernel_v', 'bias_v')}
    del _L1_xattn_all

    def _L1_ffn_setup():
        import jax, jax.numpy as jnp
        import numpy as np
        B, S, D = (8, 512, 128)
        E, R, K = (6, 16, 2)
        key = jax.random.key(seed)
        ks = jax.random.split(key, 9)
        sc = 0.02
        return {'x': jax.random.normal(ks[0], (B, S, D), jnp.float32), 'base_W': jax.random.normal(ks[1], (D, D), jnp.float32) * sc, 'base_b': jax.random.normal(ks[2], (D,), jnp.float32) * sc, 'shared_A': jax.random.normal(ks[3], (R, D), jnp.float32) * sc, 'shared_B': jax.random.normal(ks[4], (D, R), jnp.float32) * sc, 'routed_A': jax.random.normal(ks[5], (E, R, D), jnp.float32) * sc, 'routed_B': jax.random.normal(ks[6], (E, D, R), jnp.float32) * sc, 'router_W': jax.random.normal(ks[7], (E, D), jnp.float32) * sc, 'router_b': jax.random.normal(ks[8], (E,), jnp.float32) * sc}
    _L1_ffn_all = _L1_ffn_setup()
    _L1_ffn_in = {k: v for k, v in _L1_ffn_all.items() if k in ('base_W', 'base_b', 'shared_A', 'shared_B', 'routed_A', 'routed_B', 'router_W', 'router_b')}
    del _L1_ffn_all
    return {'x': x, 'ctx_1024': ctx_1024, 'mask_1xSxS2_ff0': mask_1xSxS2_ff0, 'L0_attn_w_attn': _L0_attn_in['w_attn'], 'L0_attn_b_attn': _L0_attn_in['b_attn'], 'L0_attn_la_attn': _L0_attn_in['la_attn'], 'L0_attn_lb_attn': _L0_attn_in['lb_attn'], 'L0_attn_w_proj': _L0_attn_in['w_proj'], 'L0_attn_b_proj': _L0_attn_in['b_proj'], 'L0_attn_la_proj': _L0_attn_in['la_proj'], 'L0_attn_lb_proj': _L0_attn_in['lb_proj'], 'L0_xattn_ln_m_g': _L0_xattn_in['ln_m_g'], 'L0_xattn_ln_m_b': _L0_xattn_in['ln_m_b'], 'L0_xattn_ln_l_g': _L0_xattn_in['ln_l_g'], 'L0_xattn_ln_l_b': _L0_xattn_in['ln_l_b'], 'L0_xattn_Wq': _L0_xattn_in['Wq'], 'L0_xattn_Wkv': _L0_xattn_in['Wkv'], 'L0_xattn_Wout': _L0_xattn_in['Wout'], 'L0_ffn_ln1_g': _L0_ffn_in['ln1_g'], 'L0_ffn_ln1_b': _L0_ffn_in['ln1_b'], 'L0_ffn_Wqkv': _L0_ffn_in['Wqkv'], 'L0_ffn_bqkv': _L0_ffn_in['bqkv'], 'L0_ffn_Wo': _L0_ffn_in['Wo'], 'L0_ffn_bo': _L0_ffn_in['bo'], 'L0_ffn_ln2_g': _L0_ffn_in['ln2_g'], 'L0_ffn_ln2_b': _L0_ffn_in['ln2_b'], 'L0_ffn_gate_w': _L0_ffn_in['gate_w'], 'L0_ffn_W1': _L0_ffn_in['W1'], 'L0_ffn_b1': _L0_ffn_in['b1'], 'L0_ffn_W2': _L0_ffn_in['W2'], 'L0_ffn_b2': _L0_ffn_in['b2'], 'L0_ffn_rW1': _L0_ffn_in['rW1'], 'L0_ffn_rb1': _L0_ffn_in['rb1'], 'L0_ffn_rW2': _L0_ffn_in['rW2'], 'L0_ffn_rb2': _L0_ffn_in['rb2'], 'L0_ffn_coef_w': _L0_ffn_in['coef_w'], 'L0_ffn_coef_b': _L0_ffn_in['coef_b'], 'L1_attn_w_qkv': _L1_attn_in['w_qkv'], 'L1_attn_w_proj': _L1_attn_in['w_proj'], 'L1_xattn_kernel_q': _L1_xattn_in['kernel_q'], 'L1_xattn_bias_q': _L1_xattn_in['bias_q'], 'L1_xattn_kernel_k': _L1_xattn_in['kernel_k'], 'L1_xattn_bias_k': _L1_xattn_in['bias_k'], 'L1_xattn_kernel_v': _L1_xattn_in['kernel_v'], 'L1_xattn_bias_v': _L1_xattn_in['bias_v'], 'L1_ffn_base_W': _L1_ffn_in['base_W'], 'L1_ffn_base_b': _L1_ffn_in['base_b'], 'L1_ffn_shared_A': _L1_ffn_in['shared_A'], 'L1_ffn_shared_B': _L1_ffn_in['shared_B'], 'L1_ffn_routed_A': _L1_ffn_in['routed_A'], 'L1_ffn_routed_B': _L1_ffn_in['routed_B'], 'L1_ffn_router_W': _L1_ffn_in['router_W'], 'L1_ffn_router_b': _L1_ffn_in['router_b']}

def reference(x, ctx_1024, mask_1xSxS2_ff0, L0_attn_w_attn, L0_attn_b_attn, L0_attn_la_attn, L0_attn_lb_attn, L0_attn_w_proj, L0_attn_b_proj, L0_attn_la_proj, L0_attn_lb_proj, L0_xattn_ln_m_g, L0_xattn_ln_m_b, L0_xattn_ln_l_g, L0_xattn_ln_l_b, L0_xattn_Wq, L0_xattn_Wkv, L0_xattn_Wout, L0_ffn_ln1_g, L0_ffn_ln1_b, L0_ffn_Wqkv, L0_ffn_bqkv, L0_ffn_Wo, L0_ffn_bo, L0_ffn_ln2_g, L0_ffn_ln2_b, L0_ffn_gate_w, L0_ffn_W1, L0_ffn_b1, L0_ffn_W2, L0_ffn_b2, L0_ffn_rW1, L0_ffn_rb1, L0_ffn_rW2, L0_ffn_rb2, L0_ffn_coef_w, L0_ffn_coef_b, L1_attn_w_qkv, L1_attn_w_proj, L1_xattn_kernel_q, L1_xattn_bias_q, L1_xattn_kernel_k, L1_xattn_bias_k, L1_xattn_kernel_v, L1_xattn_bias_v, L1_ffn_base_W, L1_ffn_base_b, L1_ffn_shared_A, L1_ffn_shared_B, L1_ffn_routed_A, L1_ffn_routed_B, L1_ffn_router_W, L1_ffn_router_b):
    import jax
    import jax.numpy as jnp

    def _L0_attn_ref(x, w_attn, b_attn, la_attn, lb_attn, w_proj, b_proj, la_proj, lb_proj):
        import jax, jax.numpy as jnp
        import numpy as np
        B, T, C, H = (2, 256, 128, 16)
        R = 32
        LORA_SCALE = 0.5
        HD = C // H

        def lora_linear(x, w, b, la, lb):
            return x @ w.T + b + LORA_SCALE * (x @ la.T @ lb.T)
        Bsz, Tlen, Cdim = x.shape
        qkv = lora_linear(x, w_attn, b_attn, la_attn, lb_attn)
        q, k, v = jnp.split(qkv, 3, axis=2)
        rs = lambda t: t.reshape(Bsz, Tlen, H, HD).transpose(0, 2, 1, 3)
        q, k, v = (rs(q), rs(k), rs(v))
        att = jnp.einsum('bhqd,bhkd->bhqk', q, k) * (1.0 / np.sqrt(HD))
        causal = jnp.tril(jnp.ones((Tlen, Tlen), dtype=bool))
        att = jnp.where(causal[None, None], att, -jnp.inf)
        att = jax.nn.softmax(att, axis=-1)
        y = jnp.einsum('bhqk,bhkd->bhqd', att, v)
        y = y.transpose(0, 2, 1, 3).reshape(Bsz, Tlen, Cdim)
        return lora_linear(y, w_proj, b_proj, la_proj, lb_proj)

    def _L0_xattn_ref(x, latents, ln_m_g, ln_m_b, ln_l_g, ln_l_b, Wq, Wkv, Wout):
        import jax, jax.numpy as jnp
        import numpy as np
        EPS = 1e-05

        def layer_norm(x, g, b):
            mu = jnp.mean(x, axis=-1, keepdims=True)
            var = jnp.var(x, axis=-1, keepdims=True)
            return (x - mu) * jax.lax.rsqrt(var + EPS) * g + b
        heads, dim_head = (16, 64)
        scale = dim_head ** (-0.5)
        x = layer_norm(x, ln_m_g, ln_m_b)
        lat = layer_norm(latents, ln_l_g, ln_l_b)
        b, m, _ = lat.shape
        q = lat @ Wq
        kv_input = jnp.concatenate([x, lat], axis=1)
        kv = kv_input @ Wkv
        k, v = jnp.split(kv, 2, axis=-1)

        def split_heads(t):
            return t.reshape(t.shape[0], t.shape[1], heads, dim_head).transpose(0, 2, 1, 3)
        q, k, v = (split_heads(q), split_heads(k), split_heads(v))
        dots = jnp.einsum('bhid,bhjd->bhij', q, k) * scale
        attn = jax.nn.softmax(dots, axis=-1)
        out = jnp.einsum('bhij,bhjd->bhid', attn, v)
        out = out.transpose(0, 2, 1, 3).reshape(b, m, heads * dim_head)
        return out @ Wout

    def _L0_ffn_ref(x, ln1_g, ln1_b, Wqkv, bqkv, Wo, bo, ln2_g, ln2_b, gate_w, W1, b1, W2, b2, rW1, rb1, rW2, rb2, coef_w, coef_b):
        import jax, jax.numpy as jnp
        import numpy as np
        DIM, HEADS, FFN, E = (128, 16, 512, 8)
        B, S = (2, 128)
        EPS = 1e-05

        def _ln(x, g, b):
            mu = jnp.mean(x, axis=-1, keepdims=True)
            var = jnp.mean((x - mu) ** 2, axis=-1, keepdims=True)
            return (x - mu) * jax.lax.rsqrt(var + EPS) * g + b
        b, s, d = x.shape
        h, dh = (HEADS, d // HEADS)
        xn = _ln(x, ln1_g, ln1_b)
        qkv = xn @ Wqkv + bqkv
        q, k, v = jnp.split(qkv, 3, axis=-1)
        q = q.reshape(b, s, h, dh)
        k = k.reshape(b, s, h, dh)
        v = v.reshape(b, s, h, dh)
        scores = jnp.einsum('bqhd,bkhd->bhqk', q, k) / jnp.sqrt(jnp.float32(dh))
        attn = jax.nn.softmax(scores, axis=-1)
        ctx = jnp.einsum('bhqk,bkhd->bqhd', attn, v).reshape(b, s, d)
        x = x + ctx @ Wo + bo
        xn2 = _ln(x, ln2_g, ln2_b)
        xt = xn2.reshape(b * s, d)
        probs = jax.nn.softmax(xt @ gate_w, axis=-1)
        gate_val = jnp.max(probs, axis=-1, keepdims=True)
        expert_idx = jnp.argmax(probs, axis=-1)
        oh = jax.nn.one_hot(expert_idx, E, dtype=xt.dtype)
        xe = jnp.einsum('te,td->etd', oh, xt)
        he = jax.nn.gelu(jnp.einsum('etd,edf->etf', xe, W1) + b1[:, None, :], approximate=False)
        ye = jnp.einsum('etf,efd->etd', he, W2) + b2[:, None, :]
        moe_out = jnp.einsum('te,etd->td', oh, ye) * gate_val
        rm = jax.nn.gelu(xt @ rW1 + rb1, approximate=False) @ rW2 + rb2
        coef = jax.nn.softmax(xt @ coef_w + coef_b, axis=-1)
        ff = moe_out * coef[:, 0:1] + rm * coef[:, 1:2]
        return x + ff.reshape(b, s, d)

    def _L1_attn_ref(x, w_qkv, w_proj):
        import jax, jax.numpy as jnp
        import numpy as np
        B, T, DIM, H = (2, 256, 128, 16)
        HD = DIM // H

        def _custom_softmax(a):
            a = jnp.clip(a, -100.0, 100.0)
            m = jnp.max(a, axis=-1, keepdims=True)
            e = jnp.exp(a - m)
            p = e / (jnp.sum(e, axis=-1, keepdims=True) + 1e-06)
            p = p + 1e-08
            return p / jnp.sum(p, axis=-1, keepdims=True)
        b, t, c = x.shape
        scale = HD ** (-0.5)
        qkv = jnp.einsum('btc,oc->bto', x, w_qkv)
        qkv = qkv.reshape(b, t, 3, H, HD)
        q = jnp.transpose(qkv[:, :, 0], (0, 2, 1, 3))
        k = jnp.transpose(qkv[:, :, 1], (0, 2, 1, 3))
        v = jnp.transpose(qkv[:, :, 2], (0, 2, 1, 3))
        attn = jnp.einsum('bhqd,bhkd->bhqk', q, k) * scale
        causal = jnp.tril(jnp.ones((t, t), dtype=bool))
        attn = jnp.where(causal, attn, -jnp.inf)
        attn = _custom_softmax(attn)
        out = jnp.einsum('bhqk,bhkd->bhqd', attn, v)
        out = jnp.transpose(out, (0, 2, 1, 3)).reshape(b, t, c)
        return jnp.einsum('btc,oc->bto', out, w_proj)

    def _L1_xattn_ref(q, k, v, mask, kernel_q, bias_q, kernel_k, bias_k, kernel_v, bias_v):
        import jax, jax.numpy as jnp
        import numpy as np
        INP_SIZE = 128
        D_MODEL = 128
        B, S = (4, 256)
        qp = jnp.einsum('bsi,id->bsd', q, kernel_q) + bias_q
        kp = jnp.einsum('bsi,id->bsd', k, kernel_k) + bias_k
        vp = jnp.einsum('bsi,id->bsd', v, kernel_v) + bias_v
        dk = jnp.asarray(kp.shape[-1], dtype=jnp.float32)
        logits = jnp.einsum('bqd,bkd->bqk', qp, kp) / jnp.sqrt(dk)
        logits = logits + mask
        attn = jax.nn.softmax(logits, axis=-1)
        out = jnp.einsum('bqk,bkd->bqd', attn, vp)
        return out

    def _L1_ffn_ref(x, base_W, base_b, shared_A, shared_B, routed_A, routed_B, router_W, router_b):
        import jax, jax.numpy as jnp
        import numpy as np
        B, S, D = (8, 512, 128)
        E, R, K = (6, 16, 2)
        base_out = jax.lax.stop_gradient(jnp.einsum('bsi,oi->bso', x, base_W) + base_b)
        shared_out = jnp.einsum('bsr,or->bso', jnp.einsum('bsi,ri->bsr', x, shared_A), shared_B)
        logits = jnp.einsum('bsi,ei->bse', x, router_W) + router_b
        gate = jax.nn.softmax(logits, axis=-1)
        topk_w, topk_i = jax.lax.top_k(gate, K)
        sparse_w = jnp.sum(jax.nn.one_hot(topk_i, E, dtype=gate.dtype) * topk_w[..., None], axis=-2)
        sparse_w = sparse_w / (jnp.sum(sparse_w, axis=-1, keepdims=True) + 1e-06)
        h = jnp.einsum('bsi,eri->bser', x, routed_A)
        routed_outs = jnp.einsum('bser,eor->bseo', h, routed_B)
        routed_out = jnp.einsum('bseo,bse->bso', routed_outs, sparse_w)
        return base_out + shared_out + routed_out
    x = x + _L0_attn_ref(_layernorm(x, axis=-1), L0_attn_w_attn, L0_attn_b_attn, L0_attn_la_attn, L0_attn_lb_attn, L0_attn_w_proj, L0_attn_b_proj, L0_attn_la_proj, L0_attn_lb_proj)
    x = x + _L0_xattn_ref(ctx_1024, _layernorm(x, axis=-1), L0_xattn_ln_m_g, L0_xattn_ln_m_b, L0_xattn_ln_l_g, L0_xattn_ln_l_b, L0_xattn_Wq, L0_xattn_Wkv, L0_xattn_Wout)
    x = x + _L0_ffn_ref(_layernorm(x, axis=-1), L0_ffn_ln1_g, L0_ffn_ln1_b, L0_ffn_Wqkv, L0_ffn_bqkv, L0_ffn_Wo, L0_ffn_bo, L0_ffn_ln2_g, L0_ffn_ln2_b, L0_ffn_gate_w, L0_ffn_W1, L0_ffn_b1, L0_ffn_W2, L0_ffn_b2, L0_ffn_rW1, L0_ffn_rb1, L0_ffn_rW2, L0_ffn_rb2, L0_ffn_coef_w, L0_ffn_coef_b)
    x = x + _L1_attn_ref(_layernorm(x, axis=-1), L1_attn_w_qkv, L1_attn_w_proj)
    x = x + _L1_xattn_ref(_layernorm(x, axis=-1), ctx_1024, ctx_1024, mask_1xSxS2_ff0, L1_xattn_kernel_q, L1_xattn_bias_q, L1_xattn_kernel_k, L1_xattn_bias_k, L1_xattn_kernel_v, L1_xattn_bias_v)
    x = x + _L1_ffn_ref(_layernorm(x, axis=-1), L1_ffn_base_W, L1_ffn_base_b, L1_ffn_shared_A, L1_ffn_shared_B, L1_ffn_routed_A, L1_ffn_routed_B, L1_ffn_router_W, L1_ffn_router_b)
    return x

_drawn_inputs = setup_inputs


def setup_inputs(seed=0):
    import zlib

    import numpy as np

    out = dict(_drawn_inputs(seed))
    spreads = {'L0_attn_b_attn': (0.0, 0.351),
     'L0_attn_b_proj': (0.0, 0.1),
     'L0_xattn_ln_m_g': (1.0, 0.2),
     'L0_xattn_ln_m_b': (0.0, 0.1),
     'L0_xattn_ln_l_g': (1.0, 0.2),
     'L0_xattn_ln_l_b': (0.0, 0.1),
     'L0_ffn_ln1_g': (1.0, 0.6),
     'L0_ffn_ln1_b': (0.0, 0.8),
     'L0_ffn_bqkv': (0.0, 0.8),
     'L0_ffn_bo': (0.0, 0.1),
     'L0_ffn_ln2_g': (1.0, 0.6),
     'L0_ffn_ln2_b': (0.0, 0.8),
     'L0_ffn_b1': (0.0, 0.8),
     'L0_ffn_b2': (0.0, 0.8),
     'L0_ffn_rb1': (0.0, 0.8),
     'L0_ffn_rb2': (0.0, 0.354),
     'L0_ffn_coef_b': (0.0, 0.8)}
    factors = {'L0_attn_w_attn': 7.355,
     'L0_attn_la_attn': 8.0,
     'L0_attn_lb_attn': 8.0,
     'L0_attn_la_proj': 8.0,
     'L0_attn_lb_proj': 8.0,
     'L0_ffn_Wqkv': 4.165,
     'L0_ffn_Wo': 3.375,
     'L0_ffn_gate_w': 8.0,
     'L0_ffn_W1': 8.0,
     'L0_ffn_W2': 8.0,
     'L0_ffn_rW1': 4.641,
     'L0_ffn_rW2': 4.284,
     'L0_ffn_coef_w': 8.0,
     'L1_xattn_kernel_q': 4.309,
     'L1_xattn_bias_q': 8.0,
     'L1_xattn_kernel_k': 4.096,
     'L1_xattn_bias_k': 8.0,
     'L1_xattn_bias_v': 2.75,
     'L1_ffn_base_b': 7.371,
     'L1_ffn_shared_A': 7.654,
     'L1_ffn_shared_B': 8.0,
     'L1_ffn_routed_A': 8.0,
     'L1_ffn_routed_B': 8.0,
     'L1_ffn_router_W': 8.0,
     'L1_ffn_router_b': 8.0}
    for name, (base, spread) in spreads.items():
        noise = np.random.default_rng([zlib.crc32(name.encode()), seed]).standard_normal(out[name].shape)
        drawn = base * np.exp(spread * noise) if base else spread * noise
        out[name] = jnp.asarray(drawn.astype(out[name].dtype))
    for name, factor in factors.items():
        out[name] = (out[name] * factor).astype(out[name].dtype)
    return out
```

```python
from contextlib import ExitStack

import numpy as np
import concourse.bass as bass
from concourse import mybir

P = 128
D = 128
B = 4
T = 256
S2 = 512
NT = B * T // P
NC = B * S2 // P
BANK = 512
EPS = 1e-5

H = 16
HD = D // H
G = 4
HG = H // G
ROWS = P // HG

XH = 16
XD = 64
XP = XH // 2
KEYS = S2 + T
KT = KEYS // P

E = 8
F = 512
FT = F // P
E2 = 6
R2 = 16
RU = (E2 + 1) * R2
RL = 32
MASKED = -1e30
CLIP = 100.0
TINY = 1e-6
FLOOR = 1e-8

LAYOUT = {
    "a": [("ident", P), ("headmask", H), ("causal", P), ("la0", D), ("lb0", 3 * D), ("w0", 3 * D),
          ("bq0", 1), ("bk0", 1), ("bv0", D), ("lap0", G * P), ("lbp0", D), ("wp0", G * D),
          ("lnm_g", 1), ("lnm_b", 1), ("lnl_g", 1), ("lnl_b", 1)],
    "q": [("wqT", XP * D), ("wkT", XP * D)],
    "v": [("wv", (XP + 1) * P), ("wout", XP * D)],
    "f": [("ln1_g", 1), ("ln1_b", 1), ("w2", 3 * D), ("bq2", 1), ("bk2", 1), ("bv2", D), ("wp2", G * D),
          ("ln2_g", 1), ("ln2_b", 1), ("gate", E + 2), ("coef_b", 2), ("ramp", E), ("sel", E + 1),
          ("b1", (E + 1) * 2 * FT), ("b2", D)],
    "l": [("w3", 3 * D), ("zero", 1), ("zeros", D), ("wp3", G * D), ("wq4", D), ("wk4", D), ("wv4", D), ("bq4", 1), ("bk4", 1),
          ("bv4", D), ("base", D), ("lowA", RU), ("lowB", D), ("base_b", D), ("router", E2), ("router_b", E2),
          ("sel7", RU)],
}


class Chain:

    def __init__(self, sem):
        self.sem, self.base, self.n = sem, 0, 0

    def did(self, instruction):
        instruction.then_inc(self.sem, 1)
        self.n += 1

    def wait(self, engine):
        engine.wait_ge(self.sem, self.base + self.n)

    def enter(self, iteration, first, each):
        self.start = self.n
        self.base, self.n, self.each = iteration * each + (self.start - first * each), 0, each

    def leave(self, iterations):
        assert self.n == self.each, (self.n, self.each)
        self.base, self.n = 0, self.start + iterations * self.each


def decoder(nc, x_d, ctx_d, mask_d, packs_d, w1_d, w2_d, out_d, stages=6):
    f32, bf16 = mybir.dt.float32, mybir.dt.bfloat16
    ALU, ACT, AX = mybir.AluOpType, mybir.ActivationFunctionType, mybir.AxisListType

    ctx = ExitStack()
    with ctx:
        def sb(name, shape, dt=f32):
            return ctx.enter_context(nc.sbuf_tensor(name, shape, dt))

        def sem(name):
            return ctx.enter_context(nc.semaphore(name))

        x = sb("x", [P, NT, D])
        z = sb("z", [P, NT, D])
        z2 = sb("z2", [P, NT, D])
        zT = sb("zT", [P, NT * P])
        ctx_x = sb("ctx_x", [P, NC, D])
        ctx_z = sb("ctx_z", [P, NC, D])
        centred = sb("centred", [P, 4, 4, D])
        squares = sb("squares", [P, 2, 4, D])
        stat = sb("stat", [P, 4, 4, 4])
        half = sb("half", [P, 4])
        ctxT = sb("ctxT", [P, NC * P])
        kvT = sb("kvT", [P, B, KEYS])
        packs = {key: sb(f"pack_{key}", [P, sum(w for _, w in columns)]) for key, columns in LAYOUT.items()}
        identb = sb("identb", [P, P], bf16)
        causalb = sb("causalb", [P, P], bf16)
        ones = sb("ones_", [P, T])
        A_all = sb("A_all", [P, XH + 2, P])
        A_flat = A_all[:, :, :].rearrange("p h c -> p (h c)")
        low_bias = sb("low_bias", [P, 1])
        weff = sb("weff", [P, 3 * D])
        wpeff = sb("wpeff", [P, G * D])

        ARENA = 17664
        arena = sb("arena", [P, ARENA])

        class Area:
            def __init__(self):
                self.at = 0

            def __call__(self, *dims):
                n = int(np.prod(dims))
                view = arena[:, self.at:self.at + n]
                self.at += n
                assert self.at <= ARENA, self.at
                if len(dims) == 2:
                    return view.rearrange("p (a b) -> p a b", a=dims[0])
                if len(dims) == 3:
                    return view.rearrange("p (a b c) -> p a b c", a=dims[0], b=dims[1])
                return view

        area = Area()
        qT, kT = area(NT * P), area(NT * P)
        v_tok = area(NT, D)
        qm = area(HG, T)
        v_aug = area(2, HG * ROWS)
        prob = area(HG, 2, T)
        eraw = area(HG, 2, T)
        pT = area(HG, 2 * T)
        yT = area(G, NT * P)
        sums = area(H, 2 * HG)
        negmax = area(HG, 2)
        low = area(HG, 2)
        small = area(8, 2 * HG)
        rbc = area(2, 2, P)
        rb = area(2, T)
        vsum = area(1)
        ytmp = area(T)

        area = Area()
        oT = area(XP, NT * P)
        xpT = area(2, 2, KT * T)
        xprob = area(2, 2 * KEYS)

        xv = sb("xv", [P, B, KT * P])
        xq = sb("xq", [P, 2, T])
        acur = sb("acur", [P, 2, P])
        xnegmax = sb("xnegmax", [P, 2, 2])
        xsums = sb("xsums", [P, 2, 2, 2])
        xr = sb("xr", [P, 4])
        xrbc = sb("xrbc", [P, 2, P])
        xrb = sb("xrb", [P, T])

        area = Area()
        xin = area(NT, D)
        w1b = area(2, F)
        w2b = area(2, FT * D)
        hid = area(4, BANK)
        hidm = area(4, BANK)
        mixsrc = area(2, NT * P)
        gates = area(NT, E + 2)
        probs = area(NT, E)
        pick = area(NT, E)
        coef = area(NT, 2)
        g1 = area(8, NT)
        route = area(NT, E + 1)
        routeT = area(NT * P)
        ffT = area(NT * P)

        area = Area()
        qx = area(NT * P)
        kx = area(NC * P)
        vx = area(NC, D)
        maskx = area(2, S2)
        sm = area(2, S2)
        px = area(2, S2)
        pxT = area(2, S2)
        nm1, sm1, r1 = area(NT), area(NT), area(NT)

        area = Area()
        lowT = area(NT * P)
        lowTm = area(NT * P)
        lg, lp, lpick, lsel, lw = area(NT, E2), area(NT, E2), area(NT, E2), area(NT, E2), area(NT, E2 + 1)
        l1 = area(8, NT)
        lwT = area(NT * P)

        psum = ctx.enter_context(nc.psum_tensor("psum", [P, 8, BANK], f32))
        bank = [psum[:, i, :] for i in range(8)]

        def col(key, name):
            at = 0
            for n, w in LAYOUT[key]:
                if n == name:
                    return packs[key][:, at:at + w]
                at += w
            raise KeyError(name)

        ident = col("a", "ident")

        def banks_pair(half):
            return psum[:, 2 * half:2 * half + 2, 0:KEYS // 2]

        def tiles(view):
            return view.rearrange("p (t c) -> p t c", c=D)

        def spread(view, n):
            return view.unsqueeze(2).broadcast_to([P, view.shape[1], n])

        loaded = {k: sem(f"loaded_{k}") for k in ("ctx", "a", "q", "v", "f", "l", "mask")}
        loaded_x = [sem("loaded_x0"), sem("loaded_x1")]
        stored = sem("stored")
        constants = sem("constants")
        dve_chain, pool_chain = sem("dve_chain"), sem("pool_chain")
        centred_ready, squared, rstd_ready = sem("centred_ready"), sem("squared"), sem("rstd_ready")
        normed = sem("normed")
        var_ready = sem("var_ready")
        prep_psum, prep_act, prep_dve = sem("prep_psum"), sem("prep_act"), sem("prep_dve")
        x_done, x_parts = sem("x_done"), sem("x_parts")
        CONSTANTS = 4

        class Attention:

            def __init__(self, tag, causal, clip, act_heads):
                self.causal, self.clip = causal, clip
                self.act_heads = act_heads
                self.dve_heads = [j for j in range(HG) if j not in act_heads]
                self.zT_psum = sem(f"{tag}_zT_psum")
                self.zT_act = sem(f"{tag}_zT_act")
                self.zT_dve = sem(f"{tag}_zT_dve")
                self.qkv_psum = sem(f"{tag}_qkv_psum")
                self.k_ready = sem(f"{tag}_k_ready")
                self.qv_ready = sem(f"{tag}_qv_ready")
                self.qm_ready = sem(f"{tag}_qm_ready")
                self.score_psum = sem(f"{tag}_score_psum")
                self.max_ready = sem(f"{tag}_max_ready")
                self.exp_done = sem(f"{tag}_exp_done")
                self.clip_done = sem(f"{tag}_clip_done")
                self.pT_psum = sem(f"{tag}_pT_psum")
                self.pT_act = sem(f"{tag}_pT_act")
                self.pT_dve = sem(f"{tag}_pT_dve")
                self.v_aug_ready = sem(f"{tag}_v_aug_ready")
                self.y_psum = sem(f"{tag}_y_psum")
                self.rbc_ready = sem(f"{tag}_rbc_ready")
                self.rb_psum = sem(f"{tag}_rb_psum")
                self.rb_ready = sem(f"{tag}_rb_ready")
                self.y_done = sem(f"{tag}_y_done")
                self.out_psum = sem(f"{tag}_out_psum")

            def evacuated(self, eng, it, j):
                if j in self.act_heads:
                    eng.wait_ge(self.pT_act, it * len(self.act_heads) + self.act_heads.index(j) + 1)
                else:
                    eng.wait_ge(self.pT_dve, it * len(self.dve_heads) + self.dve_heads.index(j) + 1)

            def probabilities(self, eng, n):
                if self.clip:
                    eng.wait_ge(self.clip_done, n * 2)
                else:
                    eng.wait_ge(self.exp_done, n)

            def blocks(self):
                return [(0, 0), (0, 1), (1, 1)] if self.causal and not self.clip else [(0, 0), (0, 1), (1, 0), (1, 1)]

        att0 = Attention("att0", True, False, [1])
        att1 = Attention("att1", False, False, [1])
        att2 = Attention("att2", True, True, [0, 1, 2, 3])

        def family(tag, *names):
            return {n: sem(f"{tag}_{n}") for n in names}

        sx = family("x", "zT_psum", "zT_act", "zT_dve", "acur_ready", "q_psum", "q_ready", "v_psum", "v_ready",
                    "score_psum", "max_ready", "exp_done", "pT_psum", "pT_act", "pT_dve", "y_psum", "rbc_ready",
                    "rb_psum", "rb_ready", "y_done", "out_psum")
        sf = family("f", "xin_ready", "zT_psum", "zT_act", "zT_dve", "gate_psum", "gate_shifted", "gate_exp",
                    "route_ready", "routeT_psum", "routeT_ready", "mixsrc_ready", "mix_psum", "hid_psum", "gelu_done",
                    "hid_ready", "down_done", "w_used", "out_psum", "out_ready", "ff_psum", "w_slot0", "w_slot1")
        sg = family("g", "zT_psum", "zT_act", "zT_dve", "proj_psum", "proj_act", "proj_dve", "score_psum",
                    "max_ready", "exp_done", "pT_psum", "pT_ready", "out_psum")
        sl = family("l", "zT_psum", "zT_act", "zT_dve", "low_psum", "low_ready", "gate_psum", "gate_shifted",
                    "gate_exp", "route_ready", "routeT_psum", "routeT_ready", "wide_psum", "mixed", "out_psum")

        jobs = {}

        def job(key, src, dst, after):
            jobs[key] = (len(jobs), src, dst, after)

        def quarter(view, h):
            return view[:, 4 * h:4 * h + 4, :]

        for h in range(2):
            job(("n0", h), quarter(x, h), quarter(z, h), (loaded_x[h], 16))
        for s in range(1, 6):
            for h in range(2):
                job((f"n{s}", h), quarter(x, h), quarter(z, h), (x_done, 2 * s - 1 + h))
            if s == 1:
                for c in range(2):
                    job(("ctx", c), quarter(ctx_x, c), quarter(ctx_z, c), (loaded["ctx"], 16))
                for h in range(2):
                    job(("lat", h), quarter(z, h), quarter(z2, h), (normed, jobs[("n1", h)][0] + 1))
                for c in range(2, 4):
                    job(("ctx", c), quarter(ctx_x, c), quarter(ctx_z, c), (loaded["ctx"], 16))
            if s == 2:
                for h in range(2):
                    job(("ln1", h), quarter(z, h), quarter(z2, h), (normed, jobs[("n2", h)][0] + 1))
                for h in range(2):
                    job(("ln2", h), quarter(xin, h), quarter(z2, h), (sf["xin_ready"], h + 1))
        FIRST_JOBS = [("n0", 0), ("n0", 1)]
        CROSS_JOBS = [[("n1", 0), ("n1", 1), ("ctx", 0), ("ctx", 1)], [("lat", 0), ("lat", 1), ("ctx", 2), ("ctx", 3)]]

        def wait_normed(eng, name, n=2):
            eng.wait_ge(normed, max(jobs[(name, h)][0] for h in range(n)) + 1)

        block = ctx.enter_context(nc.Block())


        @block.sync
        def _(sp):
            for h in range(2):
                sp.dma_start(quarter(x, h), x_d[2 * h:2 * h + 2].rearrange("b (u p) c -> p (b u) c", p=P))\
                    .then_inc(loaded_x[h], 16)
            sp.dma_start(packs["a"][:, :], packs_d["a"]).then_inc(loaded["a"], 16)
            sp.dma_start(packs["q"][:, :], packs_d["q"]).then_inc(loaded["q"], 16)
            sp.dma_start(ctx_x[:, :, :], ctx_d.rearrange("b (u p) c -> p (b u) c", p=P)).then_inc(loaded["ctx"], 16)
            sp.dma_start(packs["v"][:, :], packs_d["v"]).then_inc(loaded["v"], 16)
            sp.dma_start(packs["f"][:, :], packs_d["f"]).then_inc(loaded["f"], 16)
            sp.dma_start(packs["l"][:, :], packs_d["l"]).then_inc(loaded["l"], 16)
            if stages > 2:
                def expert(e, slot):
                    sp.dma_start(w1b[:, slot, :], w1_d[e]).then_inc(sf[f"w_slot{slot}"], 16)
                    sp.dma_start(w2b[:, slot, :], w2_d[e]).then_inc(sf[f"w_slot{slot}"], 16)

                sp.wait_ge(sf["xin_ready"], 1)
                expert(0, 0)
                expert(1, 1)
                sp.wait_ge(sf["w_used"], 1)
                expert(2, 0)
                with sp.Fori(1, E // 2) as i:
                    for k in range(2):
                        sp.wait_ge(sf["w_used"], i * 2 + k)
                        expert(i * 2 + k + 1, 1 - k)
            if stages > 4:
                sp.wait_ge(x_done, 8)
                sp.dma_start(maskx, mask_d[0].rearrange("(u p) k -> p u k", p=P)).then_inc(loaded["mask"], 16)
            for h in range(2):
                sp.wait_ge(x_done, 2 * stages - 1 + h)
                sp.dma_start(out_d[2 * h:2 * h + 2].rearrange("b (u p) c -> p (b u) c", p=P), quarter(x, h))\
                    .then_inc(stored, 16)
            sp.wait_ge(stored, 32)

        @block.tensor
        def _(pe):
            mm, transpose = nc.tensor.matmul, nc.tensor.transpose

            def transposes(src, done):
                for h in range(2):
                    for t in range(4):
                        last = transpose(bank[h][:, t * P:(t + 1) * P], src[:, 4 * h + t, :], ident)
                    last.then_inc(done, 1)

            def effective_weights():
                pe.wait_ge(loaded["a"], 16)
                mm(bank[0][:, 0:3 * D], col("a", "la0")[0:RL, :], col("a", "lb0")[0:RL, :], start=True, stop=True)\
                    .then_inc(prep_psum, 1)
                for g in range(G):
                    last = mm(bank[1][:, g * D:(g + 1) * D], col("a", "lap0")[0:RL, g * P:(g + 1) * P],
                              col("a", "lbp0")[0:RL, :], start=True, stop=True)
                last.then_inc(prep_psum, 1)
                pe.wait_ge(prep_dve, 2)

            def cross_operands():
                pe.wait_ge(loaded["q"], 16)
                for h in range(XH):
                    r = slice(XD * (h % 2), XD * (h % 2) + XD)
                    c = slice((h // 2) * D, (h // 2 + 1) * D)
                    bk, s = 2 + 2 * (h % 2) + h // 8, (h // 2) % 4
                    last = mm(bank[bk][:, s * P:(s + 1) * P], col("q", "wqT")[r, c], col("q", "wkT")[r, c],
                              start=True, stop=True)
                    if s == 3:
                        last.then_inc(prep_psum, 1)
                pe.wait_ge(loaded["ctx"], 16)
                for i in range(8):
                    c = i % 4
                    if i == 4:
                        wait_normed(pe, "lat")
                        transposes(z2, sx["zT_psum"])
                    if i >= 4:
                        pe.wait_ge(normed, jobs[("ctx", c)][0] + 1)
                    if i >= 2:
                        if i % 2:
                            pe.wait_ge(prep_dve, 2 + i // 2)
                        else:
                            pe.wait_ge(prep_act, 4 + i // 2)
                    src = ctx_x if i < 4 else ctx_z
                    for t in range(4):
                        last = transpose(bank[6 + c % 2][:, t * P:(t + 1) * P], src[:, 4 * c + t, :], ident)
                    last.then_inc(prep_psum, 1)

            def attention(a, src, name, w, wp):
                wait_normed(pe, name)
                transposes(src, a.zT_psum)
                pe.wait_ge(a.zT_act, 1)
                pe.wait_ge(a.zT_dve, 1)
                for h in range(2):
                    cols = slice(h * BANK, (h + 1) * BANK)
                    mm(bank[2 + h][:, :], w[:, 0:D], zT[:, cols], start=True, stop=True).then_inc(a.qkv_psum, 1)
                    mm(bank[4 + h][:, :], w[:, D:2 * D], zT[:, cols], start=True, stop=True).then_inc(a.qkv_psum, 1)
                    for t in range(4):
                        last = mm(bank[6 + h][:, t * P:(t + 1) * P], zT[:, (4 * h + t) * P:(4 * h + t + 1) * P],
                                  w[:, 2 * D:3 * D], start=True, stop=True)
                    last.then_inc(a.qkv_psum, 1)
                pe.wait_ge(a.k_ready, 2)
                pe.wait_ge(a.qv_ready, 4)

                def scores(it, b, j, prev):
                    pe.wait_ge(a.qm_ready, it * HG + j + 1)
                    if prev:
                        pe.wait_ge(a.exp_done, it * HG + j - 3)
                    for u in range(2):
                        keys = P if a.causal and u == 0 else T
                        last = mm(bank[j][:, u * T:u * T + keys], qm[:, j, u * P:(u + 1) * P],
                                  kT[:, bass.ds(b * T, keys)], start=True, stop=not a.causal)
                        if a.causal:
                            last = mm(bank[j][:, u * T + keys - P:u * T + keys], identb[:, :], causalb[:, :],
                                      start=False, stop=True)
                    last.then_inc(a.score_psum, 1)

                def transposed(it, j, prev=True):
                    a.probabilities(pe, it * HG + j + 1)
                    if j >= 2:
                        a.evacuated(pe, it, j - 2)
                    elif j == 0 and prev:
                        a.evacuated(pe, it - 1, 2)
                    for i, (k, u) in enumerate(a.blocks()):
                        last = transpose(bank[4 + j % 2][:, i * P:(i + 1) * P], prob[:, j, u, k * P:(k + 1) * P], ident)
                    last.then_inc(a.pT_psum, 1)

                def weighted(group):
                    for j in range(HG):
                        a.evacuated(pe, group, j)
                    pe.wait_ge(a.v_aug_ready, group + 1)
                    pe.wait_ge(a.y_done, group + 1)
                    for k in range(2):
                        dst, keys = slice(0, T), slice(k * T, (k + 1) * T)
                        if k and len(a.blocks()) == 3:
                            dst, keys = slice(P, T), slice(T, T + P)
                        for j in range(HG):
                            last = mm(bank[6][ROWS * j:ROWS * (j + 1), dst], v_aug[:, k, ROWS * j:ROWS * (j + 1)],
                                      pT[:, j, keys], start=(k == 0), stop=(k == 1))
                    if a.clip:
                        for k in range(2):
                            last = mm(bank[6][:, T:T + 1], v_aug[:, k, :], ones[:, 0:1], start=(k == 0), stop=(k == 1))
                    last.then_inc(a.y_psum, 1)
                    pe.wait_ge(a.rbc_ready, group + 1)
                    for k in range(2 if a.clip else 1):
                        for u in range(2):
                            last = transpose(bank[7][:, k * T + u * P:k * T + (u + 1) * P], rbc[:, k, u, :], ident)
                    last.then_inc(a.rb_psum, 1)

                def body(it, b, cur=True, prev=True, prev2=True):
                    for j in range(HG):
                        if cur:
                            scores(it, b, j, prev)
                        if prev:
                            transposed(it - 1, j, prev2)
                        if j == 0 and prev2:
                            weighted(it - 2)

                body(0, 0, prev=False, prev2=False)
                body(1, 0, prev2=False)
                with pe.Fori(2, H) as it:
                    body(it, it // G)
                body(H, 0, cur=False)
                body(H + 1, 0, cur=False, prev=False)

                pe.wait_ge(a.y_done, H + 1)
                for t in range(NT):
                    for g in range(G):
                        last = mm(bank[t // 4][:, (t % 4) * P:(t % 4 + 1) * P], yT[:, g, t * P:(t + 1) * P],
                                  wp[:, g * D:(g + 1) * D], start=(g == 0), stop=(g == G - 1))
                    if t % 4 == 3:
                        last.then_inc(a.out_psum, 1)

            def cross():
                cross_operands()
                pe.wait_ge(sx["zT_act"], 1)
                pe.wait_ge(sx["zT_dve"], 1)
                pe.wait_ge(prep_act, 9)
                pe.wait_ge(prep_dve, 6)
                pe.wait_ge(loaded["v"], 16)
                wv, wo = col("v", "wv"), col("v", "wout")
                W = KEYS // 2

                def queries(it, u):
                    pe.wait_ge(sx["acur_ready"], it * 2 + u % 2 + 1)
                    mm(bank[6][:, T:2 * T], acur[:, u % 2, :], kvT[:, u // 2, S2:KEYS], start=True, stop=True)\
                        .then_inc(sx["q_psum"], 1)

                def values(it, b, half):
                    for k in range(3):
                        kt = 3 * half + k
                        last = mm(bank[7][:, k * P:(k + 1) * P], kvT[:, b, kt * P:(kt + 1) * P],
                                  wv[:, bass.ds(it * P, P)], start=True, stop=True)
                    last.then_inc(sx["v_psum"], 1)

                def scores(u, half):
                    for c in range(2):
                        last = mm(bank[2 * half + c][:, 0:W], xq[:, u % 2, half * P:(half + 1) * P],
                                  kvT[:, u // 2, c * W:(c + 1) * W], start=True, stop=True)
                    last.then_inc(sx["score_psum"], 1)

                def transposed(m, u, chunks, first=False):
                    pe.wait_ge(sx["exp_done"], m * 2 + 2)
                    for c in chunks:
                        if c == 2:
                            pe.wait_ge(sx["pT_act"], m * 2 + 1)
                        elif not first:
                            if c:
                                pe.wait_ge(sx["pT_act"], m * 2)
                            else:
                                pe.wait_ge(sx["pT_dve"], m)
                        for i in range(2):
                            kt = 2 * c + i
                            for h in range(2):
                                last = transpose(bank[4 + (3 * u + c) % 2][:, (2 * i + h) * P:(2 * i + h + 1) * P],
                                                 xprob[:, u % 2, h * KEYS + kt * P:h * KEYS + (kt + 1) * P], ident)
                        last.then_inc(sx["pT_psum"], 1)

                def weighted(p, b):
                    pe.wait_ge(sx["pT_dve"], p * 2 + 2)
                    pe.wait_ge(sx["pT_act"], p * 4 + 4)
                    pe.wait_ge(sx["y_done"], p + 1)
                    for kt in range(KT):
                        for a in range(2):
                            last = mm(bank[6][XD * a:XD * (a + 1), 0:T], xv[:, b, kt * P + XD * a:kt * P + XD * (a + 1)],
                                      xpT[:, b % 2, a, kt * T:(kt + 1) * T], start=(kt == 0), stop=(kt == KT - 1))
                    last.then_inc(sx["y_psum"], 1)

                def factors(p):
                    pe.wait_ge(sx["rbc_ready"], p + 1)
                    for u in range(2):
                        last = transpose(bank[6][:, T + u * P:T + (u + 1) * P], xrbc[:, u, :], ident)
                    last.then_inc(sx["rb_psum"], 1)

                queries(0, 0)
                for half in range(2):
                    if half:
                        pe.wait_ge(sx["v_ready"], 1)
                    values(0, 0, half)

                def body(it, prev, cur):
                    for u in range(8):
                        n, b, odd = it * 8 + u, u // 2, u % 2
                        weigh = odd and (prev or u > 1)
                        behind = (prev and u == 0) or (cur and u)
                        if cur:
                            pe.wait_ge(sx["q_ready"], n + 1)
                            if prev or u:
                                pe.wait_ge(sx["exp_done"], n * 2 - 1)
                            scores(u, 0)
                            if odd:
                                queries(it + (u + 1) // 8, (u + 1) % 8)
                            pe.wait_ge(sx["v_ready"], n + 2)
                            values(it + (b + 1) // 4, (b + 1) % 4, odd)
                        if weigh:
                            if cur:
                                pe.wait_ge(sx["q_ready"], n + 2)
                            weighted(it * 4 + b - 1, (b - 1) % 4)
                        if behind:
                            transposed(n - 1, (u - 1) % 8, (0, 1), first=(not prev and u == 1))
                        if cur:
                            if not odd:
                                if prev or u >= 4:
                                    pe.wait_ge(sx["rb_ready"], it * 4 + b - 1)
                                    pe.wait_ge(sx["y_done"], it * 4 + b)
                                queries(it, u + 1)
                            if prev or u:
                                pe.wait_ge(sx["exp_done"], n * 2)
                            scores(u, 1)
                        if behind:
                            transposed(n - 1, (u - 1) % 8, (2,))
                        if weigh:
                            factors(it * 4 + b - 1)
                        if not cur and u == 1:
                            break

                body(0, False, True)
                with pe.Fori(1, XP) as it:
                    body(it, True, True)
                body(XP, True, False)

                pe.wait_ge(sx["y_done"], XP * B + 1)
                for t in range(NT):
                    for h in range(XP):
                        last = mm(bank[t // 4][:, (t % 4) * P:(t % 4 + 1) * P], oT[:, h, t * P:(t + 1) * P],
                                  wo[:, h * D:(h + 1) * D], start=(h == 0), stop=(h == XP - 1))
                    if t % 4 == 3:
                        last.then_inc(sx["out_psum"], 1)

            def experts():
                wait_normed(pe, "ln2")
                transposes(z2, sf["zT_psum"])
                pe.wait_ge(sf["zT_act"], 1)
                pe.wait_ge(sf["zT_dve"], 1)
                for t in range(NT):
                    last = mm(bank[2][:, t * (E + 2):(t + 1) * (E + 2)], zT[:, t * P:(t + 1) * P], col("f", "gate"),
                              start=True, stop=True)
                last.then_inc(sf["gate_psum"], 1)
                pe.wait_ge(sf["route_ready"], 1)
                for t in range(NT):
                    last = transpose(bank[3 + t // 4][0:E + 1, (t % 4) * P:(t % 4 + 1) * P], route[:, t, :], ident)
                last.then_inc(sf["routeT_psum"], 1)
                pe.wait_ge(sf["routeT_ready"], 2)
                def expert(e, slot, prev, cur):
                    for u in range(2 * FT):
                        n, c = e * (2 * FT) + u, u // FT
                        if cur:
                            if u == 0:
                                pe.wait_ge(sf[f"w_slot{slot}"], (e // 2) * 32 + 32)
                                pe.wait_ge(sf["mixsrc_ready"], e + 1)
                            if u % FT == 0:
                                if prev:
                                    pe.wait_ge(sf["hid_ready"], n - FT)
                                mm(bank[2 + c][:, :], ones[0:E + 1, 0:P], mixsrc[0:E + 1, slot, c * BANK:(c + 1) * BANK],
                                   start=True, stop=True).then_inc(sf["mix_psum"], 1)
                            if prev or u >= 4:
                                pe.wait_ge(sf["gelu_done"], n - 3)
                            mm(bank[4 + u % 4][:, :], w1b[:, slot, (u % FT) * P:(u % FT + 1) * P],
                               zT[:, c * BANK:(c + 1) * BANK], start=True, stop=True).then_inc(sf["hid_psum"], 1)
                        m = u - 2
                        if (m >= 0 and cur) or (m < 0 and prev):
                            pe.wait_ge(sf["hid_ready"], n - 1)
                            ms, mu = (slot, m) if m >= 0 else (1 - slot, m + 2 * FT)
                            mm(bank[mu // FT][:, :], w2b[:, ms, (mu % FT) * D:(mu % FT + 1) * D], hidm[:, mu % 4, :],
                               start=not prev and mu % FT == 0, stop=False).then_inc(sf["down_done"], 1)
                            if m == -1:
                                pe.wait_ge(sf["down_done"], n - 1)
                                pe.sem_inc(sf["w_used"], 1)
                                if not cur:
                                    break

                expert(0, 0, False, True)
                with pe.Fori(0, E // 2) as i:
                    for k in range(2):
                        expert(i * 2 + k + 1, 1 - k, True, True)
                expert(E + 1, 1, True, False)
                for c in range(2):
                    mm(bank[c][:, :], col("f", "b2")[0:E + 1, :], routeT[0:E + 1, c * BANK:(c + 1) * BANK],
                       start=False, stop=True).then_inc(sf["out_psum"], 1)
                pe.wait_ge(sf["out_ready"], 2)
                for t in range(NT):
                    last = transpose(bank[2 + t // 4][:, (t % 4) * P:(t % 4 + 1) * P], ffT[:, t * P:(t + 1) * P], ident)
                    if t % 4 == 3:
                        last.then_inc(sf["ff_psum"], 1)

            def single():
                for c in range(4):
                    mm(bank[2 + c][:, :], col("l", "wk4"), ctxT[:, c * BANK:(c + 1) * BANK], start=True, stop=True)\
                        .then_inc(sg["proj_psum"], 1)
                for c in range(4):
                    bk = bank[(6, 7, 2, 3)[c]]
                    if c >= 2:
                        pe.wait_ge(sg["proj_act"], c - 1)
                    for t in range(4):
                        last = mm(bk[:, t * P:(t + 1) * P], ctxT[:, (4 * c + t) * P:(4 * c + t + 1) * P],
                                  col("l", "wv4"), start=True, stop=True)
                    last.then_inc(sg["proj_psum"], 1)
                wait_normed(pe, "n4")
                transposes(z, sg["zT_psum"])
                pe.wait_ge(sg["zT_act"], 1)
                pe.wait_ge(sg["zT_dve"], 1)
                for c in range(2):
                    pe.wait_ge(sg["proj_act"], 3 + c)
                    mm(bank[4 + c][:, :], col("l", "wq4"), zT[:, c * BANK:(c + 1) * BANK], start=True, stop=True)\
                        .then_inc(sg["proj_psum"], 1)
                pe.wait_ge(sg["proj_dve"], 6)
                for n in range(NT + 2):
                    if n < NT:
                        if n >= 2:
                            pe.wait_ge(sg["max_ready"], n - 1)
                        mm(bank[n % 2][:, :], qx[:, n * P:(n + 1) * P], kx[:, (n // 2) * S2:(n // 2 + 1) * S2],
                           start=True, stop=True).then_inc(sg["score_psum"], 1)
                    if 1 <= n <= NT:
                        m = n - 1
                        pe.wait_ge(sg["exp_done"], m + 1)
                        if m >= 2:
                            pe.wait_ge(sg["pT_ready"], m - 1)
                        for k in range(4):
                            last = transpose(bank[2 + m % 2][:, k * P:(k + 1) * P], px[:, m % 2, k * P:(k + 1) * P], ident)
                        last.then_inc(sg["pT_psum"], 1)
                    if n >= 2:
                        m = n - 2
                        pe.wait_ge(sg["pT_ready"], m + 1)
                        if m >= 2:
                            pe.wait_ge(x_parts, m - 1)
                        for k in range(4):
                            last = mm(bank[4 + m % 2][:, 0:D], pxT[:, m % 2, k * P:(k + 1) * P],
                                      vx[:, (m // 2) * 4 + k, :], start=(k == 0), stop=(k == 3))
                        last.then_inc(sg["out_psum"], 1)

            def mixture():
                wait_normed(pe, "n5")
                transposes(z, sl["zT_psum"])
                pe.wait_ge(sl["zT_act"], 1)
                pe.wait_ge(sl["zT_dve"], 1)
                for t in range(NT):
                    last = mm(bank[4][:, t * E2:(t + 1) * E2], zT[:, t * P:(t + 1) * P], col("l", "router"),
                              start=True, stop=True)
                last.then_inc(sl["gate_psum"], 1)
                for c in range(2):
                    mm(bank[2 + c][0:RU, :], col("l", "lowA"), zT[:, c * BANK:(c + 1) * BANK], start=True, stop=True)\
                        .then_inc(sl["low_psum"], 1)
                pe.wait_ge(sl["route_ready"], 1)
                for t in range(NT):
                    last = transpose(bank[5 + t // 4][0:E2 + 1, (t % 4) * P:(t % 4 + 1) * P], lw[:, t, :], ident)
                last.then_inc(sl["routeT_psum"], 1)
                pe.wait_ge(sl["routeT_ready"], 2)
                for c in range(2):
                    mm(bank[7 * c][0:RU, :], col("l", "sel7")[0:E2 + 1, :], lwT[0:E2 + 1, c * BANK:(c + 1) * BANK],
                       start=True, stop=True).then_inc(sl["wide_psum"], 1)
                pe.wait_ge(sl["mixed"], 2)
                for t in range(NT):
                    out = bank[2 + t // 4][:, (t % 4) * P:(t % 4 + 1) * P]
                    mm(out, zT[:, t * P:(t + 1) * P], col("l", "base"), start=True, stop=False)
                    mm(out, lowTm[0:RU, t * P:(t + 1) * P], col("l", "lowB")[0:RU, :], start=False, stop=False)
                    last = mm(out, ones[0:1, 0:P], col("l", "base_b")[0:1, :], start=False, stop=True)
                    if t % 4 == 3:
                        last.then_inc(sl["out_psum"], 1)

            pe.wait_ge(constants, CONSTANTS)
            effective_weights()
            attention(att0, z, "n0", weff, wpeff)
            if stages > 1:
                cross()
            if stages > 2:
                pe.wait_ge(loaded["f"], 16)
                attention(att1, z2, "ln1", col("f", "w2"), col("f", "wp2"))
                experts()
            if stages > 3:
                pe.wait_ge(loaded["l"], 16)
                attention(att2, z, "n3", col("l", "w3"), col("l", "wp3"))
            if stages > 4:
                single()
            if stages > 5:
                mixture()

        @block.scalar
        def _(act):
            activation = nc.scalar.activation

            def square_jobs(keys):
                for key in keys:
                    k = jobs[key][0]
                    act.wait_ge(centred_ready, k + 1)
                    if k >= 2:
                        act.wait_ge(var_ready, k - 1)
                    activation(squares[:, k % 2, :, :], centred[:, k % 4, :, :], ACT.Square).then_inc(squared, 1)

            def affine(out, in_, g, b, done):
                activation(out, in_, ACT.Identity, bias=b, scale=g).then_inc(done, 1)

            def attention(a, g, b, bias_k):
                act.wait_ge(a.zT_psum, 1)
                if g is None:
                    activation(zT[:, 0:BANK], bank[0][:, :], ACT.Copy).then_inc(a.zT_act, 1)
                else:
                    affine(zT[:, 0:BANK], bank[0][:, :], g, b, a.zT_act)
                for h in range(2):
                    act.wait_ge(a.qkv_psum, 3 * h + 2)
                    activation(kT[:, h * BANK:(h + 1) * BANK], bank[4 + h][:, :], ACT.Identity, bias=bias_k)\
                        .then_inc(a.k_ready, 1)

                def exponentials(it, j, prev):
                    n = it * HG + j
                    act.wait_ge(a.max_ready, n + 1)
                    if prev:
                        if a.clip:
                            a.probabilities(act, n - 3)
                        else:
                            act.wait_ge(a.pT_psum, n - 3)
                    if a.clip:
                        activation(low[:, j, :], negmax[:, j, :], ACT.Exp, bias=low_bias[:, :])
                    for u in range(2):
                        keys = P if a.causal and u == 0 else T
                        if a.clip:
                            last = activation(eraw[:, j, u, 0:keys], bank[j][:, u * T:u * T + keys], ACT.Exp,
                                              bias=negmax[:, j, u:u + 1])
                        else:
                            last = activation(prob[:, j, u, 0:keys], bank[j][:, u * T:u * T + keys], ACT.Exp,
                                              bias=negmax[:, j, u:u + 1], accum_out=sums[:, it, u * HG + j:u * HG + j + 1])
                    last.then_inc(a.exp_done, 1)

                def evacuate(it, j, prev):
                    if j in a.act_heads:
                        act.wait_ge(a.pT_psum, it * HG + j + 1)
                        if j == 0 and prev:
                            act.wait_ge(a.y_psum, it)
                        w = len(a.blocks()) * P
                        activation(pT[:, j, 0:w], bank[4 + j % 2][:, 0:w], ACT.Copy).then_inc(a.pT_act, 1)

                def body(it, cur=True, prev=True, prev2=True):
                    for j in range(HG):
                        if cur:
                            exponentials(it, j, prev)
                        if prev:
                            evacuate(it - 1, j, prev2)
                        if j == 0 and prev2:
                            act.wait_ge(a.rb_psum, it - 1)
                            w = 2 if a.clip else 1
                            activation(rb[:, 0:w, :], bank[7][:, 0:w * T].rearrange("p (k t) -> p k t", k=w), ACT.Copy)\
                                .then_inc(a.rb_ready, 1)

                body(0, prev=False, prev2=False)
                body(1, prev2=False)
                with act.Fori(2, H) as it:
                    body(it)
                body(H, cur=False)
                body(H + 1, cur=False, prev=False)

            def cross():
                for i in range(4):
                    odd, late = i % 2, i // 2
                    act.wait_ge(prep_psum, 3 + i)
                    activation(A_all[:, 8 * late + odd:8 * late + odd + 7:2, :], tiles(bank[2 + 2 * odd + late][:, :]),
                               ACT.Copy, scale=XD ** -0.5).then_inc(prep_act, 1)
                for i in (0, 2):
                    act.wait_ge(prep_psum, 7 + i)
                    activation(ctxT[:, i * BANK:(i + 1) * BANK], bank[6][:, :], ACT.Copy).then_inc(prep_act, 1)
                square_jobs(CROSS_JOBS[1])
                act.wait_ge(sx["zT_psum"], 1)
                affine(kvT[:, 0:2, S2:KEYS], bank[0][:, :].rearrange("p (b t) -> p b t", b=2), col("a", "lnl_g"),
                       col("a", "lnl_b"), sx["zT_act"])

            def cross_context():
                for i in (0, 2):
                    act.wait_ge(prep_psum, 11 + i)
                    affine(kvT[:, i, 0:S2], bank[6][:, :], col("a", "lnm_g"), col("a", "lnm_b"), prep_act)
                activation(A_all[:, XH:XH + 2, :], psum[:, 2:5:2, 0:P], ACT.Copy, scale=XD ** -0.5)\
                    .then_inc(prep_act, 1)

            def cross_units():
                def body(it, prev, cur):
                    for u in range(8):
                        n, b, odd = it * 8 + u, u // 2, u % 2
                        behind = (prev and u == 0) or (cur and u)
                        if cur:
                            if odd:
                                queries(n, u)
                            exponentials(it, n, u, 0, prev)
                        if behind:
                            evacuate(n - 1, (u - 1) % 8, 0)
                        if cur:
                            if not odd:
                                queries(n, u)
                            exponentials(it, n, u, 1, prev)
                        if behind:
                            evacuate(n - 1, (u - 1) % 8, 2)
                        if odd and (prev or u > 1):
                            act.wait_ge(sx["rb_psum"], it * 4 + b)
                            activation(xrb[:, :], bank[6][:, T:2 * T], ACT.Copy).then_inc(sx["rb_ready"], 1)
                        if not cur and u == 1:
                            break

                def queries(n, u):
                    act.wait_ge(sx["q_psum"], n + 2)
                    activation(xq[:, (u + 1) % 2, :], bank[6][:, T:2 * T], ACT.Copy).then_inc(sx["q_ready"], 1)

                def evacuate(m, mu, c):
                    act.wait_ge(sx["pT_psum"], m * 3 + c + 1)
                    activation(xpT[:, (mu // 2) % 2, mu % 2, 2 * c * T:2 * (c + 1) * T], bank[4 + (3 * mu + c) % 2][:, :],
                               ACT.Copy).then_inc(sx["pT_act"], 1)

                def exponentials(it, n, u, half, prev):
                    act.wait_ge(sx["max_ready"], n * 2 + half + 1)
                    if half == 0 and (prev or u >= 2):
                        act.wait_ge(sx["pT_psum"], n * 3 - 3)
                    src = banks_pair(half)
                    activation(xprob[:, u % 2, half * KEYS:(half + 1) * KEYS].rearrange("p (c w) -> p c w", c=2), src,
                               ACT.Exp, bias=xnegmax[:, u % 2, half:half + 1],
                               accum_out=xsums[:, (u // 2) % 2, half, u % 2:u % 2 + 1]).then_inc(sx["exp_done"], 1)

                act.wait_ge(sx["q_psum"], 1)
                activation(xq[:, 0, :], bank[6][:, T:2 * T], ACT.Copy).then_inc(sx["q_ready"], 1)
                body(0, False, True)
                with act.Fori(1, XP) as it:
                    body(it, True, True)
                body(XP, True, False)

            def experts():
                square_jobs([("ln2", 0), ("ln2", 1)])
                act.wait_ge(sf["zT_psum"], 1)
                affine(zT[:, 0:BANK], bank[0][:, :], col("f", "ln2_g"), col("f", "ln2_b"), sf["zT_act"])
                act.wait_ge(sf["gate_shifted"], 1)
                activation(gates[:, :, :], gates[:, :, :], ACT.Exp).then_inc(sf["gate_exp"], 1)
                act.wait_ge(sf["routeT_psum"], 1)
                activation(routeT[0:E + 1, 0:BANK], bank[3][0:E + 1, :], ACT.Copy).then_inc(sf["routeT_ready"], 1)
                b1 = col("f", "b1")

                def expert(e, prev):
                    for u in range(2 * FT):
                        n = e * (2 * FT) + u
                        act.wait_ge(sf["hid_psum"], n + 1)
                        if prev or u >= 4:
                            act.wait_ge(sf["hid_ready"], n - 3)
                        activation(hid[:, u % 4, :], bank[4 + u % 4][:, :], ACT.Gelu,
                                   bias=b1[:, bass.ds(e * 2 * FT + u, 1)]).then_inc(sf["gelu_done"], 1)

                expert(0, False)
                with act.Fori(1, E + 1) as e:
                    expert(e, True)
                act.wait_ge(sf["out_psum"], 1)
                activation(ffT[:, 0:BANK], bank[0][:, :], ACT.Copy).then_inc(sf["out_ready"], 1)

            def single():
                for c in range(4):
                    act.wait_ge(sg["proj_psum"], c + 1)
                    activation(kx[:, c * BANK:(c + 1) * BANK], bank[2 + c][:, :], ACT.Identity, bias=col("l", "bk4"))\
                        .then_inc(sg["proj_act"], 1)
                square_jobs([("n4", 0), ("n4", 1)])
                act.wait_ge(sg["zT_psum"], 1)
                activation(zT[:, 0:BANK], bank[0][:, :], ACT.Copy).then_inc(sg["zT_act"], 1)
                for n in range(NT):
                    act.wait_ge(sg["max_ready"], n + 1)
                    if n >= 2:
                        act.wait_ge(sg["pT_psum"], n - 1)
                    activation(px[:, n % 2, :], sm[:, n % 2, :], ACT.Exp, bias=nm1[:, n:n + 1],
                               accum_out=sm1[:, n:n + 1]).then_inc(sg["exp_done"], 1)

            def mixture():
                square_jobs([("n5", 0), ("n5", 1)])
                act.wait_ge(sl["zT_psum"], 1)
                activation(zT[:, 0:BANK], bank[0][:, :], ACT.Copy).then_inc(sl["zT_act"], 1)
                for c in range(2):
                    act.wait_ge(sl["low_psum"], c + 1)
                    activation(lowT[0:RU, c * BANK:(c + 1) * BANK], bank[2 + c][0:RU, :], ACT.Copy)\
                        .then_inc(sl["low_ready"], 1)
                act.wait_ge(sl["gate_shifted"], 1)
                activation(lp, lg, ACT.Exp).then_inc(sl["gate_exp"], 1)
                act.wait_ge(sl["routeT_psum"], 1)
                activation(lwT[0:E2 + 1, 0:BANK], bank[5][0:E2 + 1, :], ACT.Copy).then_inc(sl["routeT_ready"], 1)

            square_jobs(FIRST_JOBS)
            act.wait_ge(constants, CONSTANTS)
            act.wait_ge(loaded["a"], 16)
            attention(att0, None, None, col("a", "bk0"))
            if stages > 1:
                square_jobs(CROSS_JOBS[0])
                cross()
                cross_context()
                cross_units()
            if stages > 2:
                act.wait_ge(loaded["f"], 16)
                square_jobs([("n2", 0), ("n2", 1)])
                square_jobs([("ln1", 0), ("ln1", 1)])
                attention(att1, col("f", "ln1_g"), col("f", "ln1_b"), col("f", "bk2"))
                experts()
            if stages > 3:
                act.wait_ge(loaded["l"], 16)
                square_jobs([("n3", 0), ("n3", 1)])
                attention(att2, None, None, col("l", "zero"))
            if stages > 4:
                single()
            if stages > 5:
                mixture()

        @block.vector
        def _(dve):
            v = nc.vector
            chain = Chain(dve_chain)

            def link(instruction):
                chain.did(instruction)
                chain.wait(dve)

            def normalise(keys):
                for key in keys:
                    k, src, _, (after, value) = jobs[key]
                    dve.wait_ge(after, value)
                    link(v.tensor_reduce(stat[:, k % 4, 0, :], src, AX.X, ALU.add))
                    v.scalar_tensor_tensor(centred[:, k % 4, :, :], spread(stat[:, k % 4, 0, :], D), -1.0 / D, src,
                                           ALU.mult, ALU.add).then_inc(centred_ready, 1)
                for key in keys:
                    k = jobs[key][0]
                    dve.wait_ge(squared, k + 1)
                    v.tensor_reduce(stat[:, k % 4, 1, :], squares[:, k % 2, :, :], AX.X, ALU.add).then_inc(var_ready, 1)
                for key in keys:
                    k, _, dst, _ = jobs[key]
                    dve.wait_ge(rstd_ready, k + 1)
                    v.tensor_tensor(dst, centred[:, k % 4, :, :], spread(stat[:, k % 4, 3, :], D), ALU.mult)\
                        .then_inc(normed, 1)

            def add_to_x(psum, banks):
                for h in range(2):
                    dve.wait_ge(psum, h + 1)
                    v.tensor_tensor(quarter(x, h), quarter(x, h), tiles(bank[banks[h]][:, :]), ALU.add)\
                        .then_inc(x_done, 1)

            def effective_weights():
                dve.wait_ge(prep_psum, 1)
                v.scalar_tensor_tensor(weff[:, :], bank[0][:, 0:3 * D], 0.5, col("a", "w0"), ALU.mult, ALU.add)\
                    .then_inc(prep_dve, 1)
                dve.wait_ge(prep_psum, 2)
                v.scalar_tensor_tensor(wpeff[:, :], bank[1][:, :], 0.5, col("a", "wp0"), ALU.mult, ALU.add)\
                    .then_inc(prep_dve, 1)

            def attention(a, g, b, bias_q, bias_v):
                link(v.memset(v_aug, 0.0))
                link(v.memset(v_aug.rearrange("p k (j r) -> p k j r", j=HG)[:, :, :, HD:HD + 1], 1.0))
                if a.clip:
                    link(v.memset(eraw, 0.0))
                dve.wait_ge(a.zT_psum, 2)
                if g is None:
                    v.tensor_copy(zT[:, BANK:2 * BANK], bank[1][:, :]).then_inc(a.zT_dve, 1)
                else:
                    v.tensor_scalar(zT[:, BANK:2 * BANK], bank[1][:, :], g, b, ALU.mult, ALU.add).then_inc(a.zT_dve, 1)
                for h in range(2):
                    dve.wait_ge(a.qkv_psum, 3 * h + 1)
                    v.tensor_scalar(qT[:, h * BANK:(h + 1) * BANK], bank[2 + h][:, :], bias_q, HD ** -0.5,
                                    ALU.add, ALU.mult).then_inc(a.qv_ready, 1)
                    dve.wait_ge(a.qkv_psum, 3 * h + 3)
                    v.tensor_tensor(quarter(v_tok, h), tiles(bank[6 + h][:, :]),
                                    bias_v.unsqueeze(1).broadcast_to([P, 4, D]), ALU.add).then_inc(a.qv_ready, 1)
                chain.did(v.memset(ytmp, 0.0))
                chain.wait(dve)
                v.memset(ytmp, 0.0).then_inc(a.y_done, 1)
                dve.wait_ge(a.qv_ready, 4)

                def maxima(it, j):
                    dve.wait_ge(a.score_psum, it * HG + j + 1)
                    if a.causal:
                        last = v.tensor_reduce(negmax[:, j, 0:1], bank[j][:, 0:P], AX.X, ALU.max, negate=True)
                        if a.clip:
                            chain.did(last)
                        last = v.tensor_reduce(negmax[:, j, 1:2], bank[j][:, T:2 * T], AX.X, ALU.max, negate=True)
                    else:
                        last = v.tensor_reduce(negmax[:, j, :], bank[j][:, :].rearrange("p (u k) -> p u k", u=2), AX.X,
                                               ALU.max, negate=True)
                    if a.clip:
                        chain.did(last)
                    else:
                        last.then_inc(a.max_ready, 1)

                def clipped_maxima(j):
                    chain.wait(dve)
                    v.tensor_scalar(negmax[:, j, :], negmax[:, j, :], -CLIP, CLIP, ALU.max, ALU.min)\
                        .then_inc(a.max_ready, 1)

                def clipped(it, j, u, prev):
                    if u == 0:
                        dve.wait_ge(a.exp_done, it * HG + j + 1)
                        if prev:
                            dve.wait_ge(a.pT_psum, it * HG + j - 3)
                    v.scalar_tensor_tensor(prob[:, j, u, :], eraw[:, j, u, :], low[:, j, u:u + 1], ones[:, :], ALU.max,
                                           ALU.min, accum_out=sums[:, it, u * HG + j:u * HG + j + 1])\
                        .then_inc(a.clip_done, 1)

                def evacuate(it, j, prev):
                    if j in a.dve_heads:
                        dve.wait_ge(a.pT_psum, it * HG + j + 1)
                        if j == 0 and prev:
                            dve.wait_ge(a.y_psum, it)
                        w = len(a.blocks()) * P
                        v.tensor_copy(pT[:, j, 0:w], bank[4 + j % 2][:, 0:w]).then_inc(a.pT_dve, 1)

                r, t, den, w = small[:, 0, :], small[:, 1, :], small[:, 2, :], small[:, 3, :]

                def over_rows(k, factor):
                    return v.tensor_copy(rbc[:, k, :, :].rearrange("p u (j r) -> p (u j) r", j=HG), spread(factor, ROWS))

                def factors(it):
                    dve.wait_ge(a.exp_done, it * HG + HG)
                    link(v.reciprocal(r, sums[:, it, :]))
                    over_rows(0, r).then_inc(a.rbc_ready, 1)

                def floored_factors(it, step):
                    if step == 0:
                        dve.wait_ge(a.clip_done, (it * HG + HG) * 2)
                        chain.did(v.tensor_scalar(t, sums[:, it, :], FLOOR, FLOOR * TINY, ALU.mult, ALU.add))
                    else:
                        chain.wait(dve)
                    if step == 1:
                        chain.did(v.scalar_tensor_tensor(den, t, float(T), sums[:, it, :], ALU.mult, ALU.add))
                    if step == 2:
                        chain.did(v.reciprocal(r, den))
                    if step == 3:
                        chain.did(v.tensor_tensor(w, t, r, ALU.mult))
                    if step == 4:
                        chain.did(over_rows(1, w))
                        over_rows(0, r).then_inc(a.rbc_ready, 1)

                def values(it, b, g):
                    v.tensor_copy(v_aug.rearrange("p k (j r) -> p k j r", j=HG)[:, :, :, 0:HD],
                                  v_tok[:, bass.ds(b * 2, 2), bass.ds(g * HG * HD, HG * HD)]
                                  .rearrange("p k (j r) -> p k j r", j=HG)).then_inc(a.v_aug_ready, 1)

                def results(group, b, g):
                    dve.wait_ge(a.rb_ready, group + 1)
                    out = yT[:, g, bass.ds(b * T, T)]
                    if a.clip:
                        chain.did(v.tensor_copy(vsum, bank[6][:, T:T + 1]))
                        link(v.tensor_tensor(ytmp, bank[6][:, 0:T], rb[:, 0, :], ALU.mult))
                        v.scalar_tensor_tensor(out, rb[:, 1, :], vsum, ytmp, ALU.mult, ALU.add).then_inc(a.y_done, 1)
                    else:
                        v.tensor_tensor(out, bank[6][:, 0:T], rb[:, 0, :], ALU.mult).then_inc(a.y_done, 1)

                def body(it, cur=True, prev=True, prev2=True):
                    for j in range(HG):
                        if cur:
                            maxima(it, j)
                        if a.clip:
                            behind = (it - 1, HG - 1, prev) if j == 0 else (it, j - 1, cur)
                            if j in (1, 2) and prev:
                                floored_factors(it - 1, 2 * j - 2)
                            if behind[2]:
                                clipped(behind[0], behind[1], 0, prev)
                            if cur:
                                clipped_maxima(j)
                            if behind[2]:
                                clipped(behind[0], behind[1], 1, prev)
                            if j in (1, 2) and prev:
                                floored_factors(it - 1, 2 * j - 1)
                        if j == 1 and prev2:
                            results(it - 2, (it - 2) // G, (it - 2) % G)
                        if prev:
                            evacuate(it - 1, j, prev2)
                            if j == 1:
                                values(it - 1, (it - 1) // G, (it - 1) % G)
                                if not a.clip:
                                    factors(it - 1)
                            if j == 3 and a.clip:
                                floored_factors(it - 1, 4)

                body(0, prev=False, prev2=False)
                body(1, prev2=False)
                each = 2 * HG + 5 + 2 if a.clip else 1
                with dve.Fori(2, H) as it:
                    chain.enter(it, 2, each)
                    body(it)
                    chain.leave(H - 2)
                body(H, cur=False)
                body(H + 1, cur=False, prev=False)

            def cross_context():
                for i in (1, 3):
                    dve.wait_ge(prep_psum, 7 + i)
                    v.tensor_copy(ctxT[:, i * BANK:(i + 1) * BANK], bank[7][:, :]).then_inc(prep_dve, 1)

            def cross_context_normed():
                dve.wait_ge(sx["zT_psum"], 2)
                v.tensor_scalar(kvT[:, 2:4, S2:KEYS], bank[1][:, :].rearrange("p (b t) -> p b t", b=2),
                                col("a", "lnl_g"), col("a", "lnl_b"), ALU.mult, ALU.add).then_inc(sx["zT_dve"], 1)
                for i in (1, 3):
                    dve.wait_ge(prep_psum, 11 + i)
                    v.tensor_scalar(kvT[:, i, 0:S2], bank[7][:, :], col("a", "lnm_g"), col("a", "lnm_b"),
                                    ALU.mult, ALU.add).then_inc(prep_dve, 1)

            def cross_units():
                W3 = 3 * P

                def maxima(n, u, half):
                    dve.wait_ge(sx["score_psum"], n * 2 + half + 1)
                    v.tensor_reduce(xnegmax[:, u % 2, half:half + 1], banks_pair(half), AX.XY, ALU.max, negate=True)\
                        .then_inc(sx["max_ready"], 1)

                def values(count, b, half):
                    dve.wait_ge(sx["v_psum"], count)
                    v.tensor_copy(xv[:, b, half * W3:(half + 1) * W3], bank[7][:, 0:W3]).then_inc(sx["v_ready"], 1)

                def results(p, hp, b):
                    dve.wait_ge(sx["rb_ready"], p + 1)
                    v.tensor_tensor(oT[:, hp, b * T:(b + 1) * T], bank[6][:, 0:T], xrb[:, :], ALU.mult)\
                        .then_inc(sx["y_done"], 1)

                def body(it, prev, cur):
                    for u in range(8):
                        n, b, odd = it * 8 + u, u // 2, u % 2
                        if cur:
                            maxima(n, u, 0)
                            values(n + 3, (b + 1) % 4, odd)
                        if not odd and (prev or u >= 4):
                            results(it * 4 + b - 2, it - (u < 4), (b - 2) % 4)
                        if (prev and u == 0) or (cur and u):
                            m, mu = n - 1, (u - 1) % 8
                            dve.wait_ge(sx["pT_psum"], m * 3 + 2)
                            v.tensor_copy(xpT[:, (mu // 2) % 2, mu % 2, 2 * T:4 * T], bank[4 + (3 * mu + 1) % 2][:, :])\
                                .then_inc(sx["pT_dve"], 1)
                        if not odd and ((prev and u == 0) or (cur and u)):
                            dve.wait_ge(sx["exp_done"], n * 2)
                            link(v.reciprocal(xr[:, :], xsums[:, ((u - 2) % 8 // 2) % 2, :, :].rearrange("p h a -> p (h a)")))
                            v.tensor_copy(xrbc[:, :, :].rearrange("p h (a r) -> p (h a) r", a=2), spread(xr[:, :], XD))\
                                .then_inc(sx["rbc_ready"], 1)
                        if cur:
                            maxima(n, u, 1)
                        if not cur and u == 2:
                            break

                v.memset(xrb[:, 0:1], 0.0).then_inc(sx["y_done"], 1)
                values(1, 0, 0)
                values(2, 0, 1)
                body(0, False, True)
                with dve.Fori(1, XP) as it:
                    chain.enter(it, 1, 4)
                    body(it, True, True)
                    chain.leave(XP - 1)
                body(XP, True, False)

            def top(src, out, value, key, shape_e, ramp):
                link(v.tensor_reduce(value, src, AX.X, ALU.max))
                link(v.tensor_tensor(out, src, spread(value, shape_e), ALU.is_equal))
                link(v.tensor_tensor(out, out, ramp.unsqueeze(1).broadcast_to([P, NT, shape_e]), ALU.mult))
                link(v.tensor_reduce(key, out, AX.X, ALU.max))
                link(v.tensor_tensor(out, out, spread(key, shape_e), ALU.is_equal))

            def experts():
                for h in range(2):
                    dve.wait_ge(att1.out_psum, h + 1)
                    v.tensor_tensor(quarter(xin, h), quarter(z, h), tiles(bank[h][:, :]), ALU.add)\
                        .then_inc(sf["xin_ready"], 1)
                normalise([("ln2", 0), ("ln2", 1)])
                link(v.tensor_tensor(x[:, :, :], x[:, :, :], xin, ALU.add))
                dve.wait_ge(sf["zT_psum"], 2)
                v.tensor_scalar(zT[:, BANK:2 * BANK], bank[1][:, :], col("f", "ln2_g"), col("f", "ln2_b"),
                                ALU.mult, ALU.add).then_inc(sf["zT_dve"], 1)
                dve.wait_ge(sf["gate_psum"], 1)
                link(v.tensor_copy(gates, bank[2][:, 0:NT * (E + 2)].rearrange("p (t e) -> p t e", t=NT)))
                ge, gc = gates[:, :, 0:E], gates[:, :, E:E + 2]
                link(v.tensor_tensor(gc, gc, col("f", "coef_b").unsqueeze(1).broadcast_to([P, NT, 2]), ALU.add))
                link(v.tensor_reduce(g1[:, 0, :], ge, AX.X, ALU.max))
                link(v.tensor_reduce(g1[:, 1, :], gc, AX.X, ALU.max))
                link(v.tensor_tensor(ge, ge, spread(g1[:, 0, :], E), ALU.subtract))
                v.tensor_tensor(gc, gc, spread(g1[:, 1, :], 2), ALU.subtract).then_inc(sf["gate_shifted"], 1)
                dve.wait_ge(sf["gate_exp"], 1)
                link(v.tensor_reduce(g1[:, 2, :], ge, AX.X, ALU.add))
                link(v.tensor_reduce(g1[:, 3, :], gc, AX.X, ALU.add))
                link(v.reciprocal(g1[:, 2:4, :], g1[:, 2:4, :]))
                link(v.tensor_tensor(probs, ge, spread(g1[:, 2, :], E), ALU.mult))
                link(v.tensor_tensor(coef, gc, spread(g1[:, 3, :], 2), ALU.mult))
                top(probs, pick, g1[:, 4, :], g1[:, 5, :], E, col("f", "ramp"))
                link(v.tensor_tensor(g1[:, 6, :], g1[:, 4, :], coef[:, :, 0:1].rearrange("p t a -> p (t a)"), ALU.mult))
                link(v.tensor_tensor(route[:, :, 0:E], pick, spread(g1[:, 6, :], E), ALU.mult))
                v.tensor_copy(route[:, :, E:E + 1], coef[:, :, 1:2]).then_inc(sf["route_ready"], 1)
                dve.wait_ge(sf["routeT_psum"], 1)
                v.tensor_copy(routeT[0:E + 1, BANK:2 * BANK], bank[4][0:E + 1, :]).then_inc(sf["routeT_ready"], 1)

                def expert(e, prev):
                    for u in range(2 * FT):
                        n, c = e * (2 * FT) + u, u // FT
                        if u % FT == 0:
                            dve.wait_ge(sf["mix_psum"], e * 2 + c + 1)
                        dve.wait_ge(sf["gelu_done"], n + 1)
                        if prev or u >= 4:
                            dve.wait_ge(sf["down_done"], n - 3)
                        v.tensor_tensor(hidm[:, u % 4, :], hid[:, u % 4, :], bank[2 + c][:, :], ALU.mult)\
                            .then_inc(sf["hid_ready"], 1)

                expert(0, False)
                with dve.Fori(1, E + 1) as e:
                    expert(e, True)
                dve.wait_ge(sf["out_psum"], 2)
                v.tensor_copy(ffT[:, BANK:2 * BANK], bank[1][:, :]).then_inc(sf["out_ready"], 1)
                add_to_x(sf["ff_psum"], (2, 3))

            def single():
                for c in range(4):
                    dve.wait_ge(sg["proj_psum"], 5 + c)
                    v.tensor_tensor(quarter(vx, c), tiles(bank[(6, 7, 2, 3)[c]][:, :]),
                                    col("l", "bv4").unsqueeze(1).broadcast_to([P, 4, D]), ALU.add)\
                        .then_inc(sg["proj_dve"], 1)
                normalise([("n4", 0), ("n4", 1)])
                dve.wait_ge(sg["zT_psum"], 2)
                v.tensor_copy(zT[:, BANK:2 * BANK], bank[1][:, :]).then_inc(sg["zT_dve"], 1)
                for c in range(2):
                    dve.wait_ge(sg["proj_psum"], 9 + c)
                    v.tensor_scalar(qx[:, c * BANK:(c + 1) * BANK], bank[4 + c][:, :], col("l", "bq4"), D ** -0.5,
                                    ALU.add, ALU.mult).then_inc(sg["proj_dve"], 1)
                dve.wait_ge(loaded["mask"], 16)
                for n in range(NT + 2):
                    if n < NT:
                        dve.wait_ge(sg["score_psum"], n + 1)
                        if n >= 2:
                            dve.wait_ge(sg["exp_done"], n - 1)
                        link(v.tensor_tensor(sm[:, n % 2, :], bank[n % 2][:, :], maskx[:, n % 2, :], ALU.add))
                        v.tensor_reduce(nm1[:, n:n + 1], sm[:, n % 2, :], AX.X, ALU.max, negate=True)\
                            .then_inc(sg["max_ready"], 1)
                    if 1 <= n <= NT:
                        m = n - 1
                        dve.wait_ge(sg["pT_psum"], m + 1)
                        v.tensor_copy(pxT[:, m % 2, :], bank[2 + m % 2][:, :]).then_inc(sg["pT_ready"], 1)
                    if n >= 2:
                        m = n - 2
                        link(v.reciprocal(r1[:, m:m + 1], sm1[:, m:m + 1]))
                        dve.wait_ge(sg["out_psum"], m + 1)
                        last = v.scalar_tensor_tensor(x[:, m, :], bank[4 + m % 2][:, 0:D], r1[:, m:m + 1], x[:, m, :],
                                                      ALU.mult, ALU.add)
                        last.then_inc(x_parts, 1)
                        if m % 4 == 3:
                            dve.wait_ge(x_parts, m + 1)
                            dve.sem_inc(x_done, 1)

            def mixture():
                normalise([("n5", 0), ("n5", 1)])
                dve.wait_ge(sl["zT_psum"], 2)
                v.tensor_copy(zT[:, BANK:2 * BANK], bank[1][:, :]).then_inc(sl["zT_dve"], 1)
                dve.wait_ge(sl["gate_psum"], 1)
                link(v.tensor_tensor(lg, bank[4][:, 0:NT * E2].rearrange("p (t e) -> p t e", t=NT),
                                     col("l", "router_b").unsqueeze(1).broadcast_to([P, NT, E2]), ALU.add))
                link(v.tensor_reduce(l1[:, 0, :], lg, AX.X, ALU.max))
                v.tensor_tensor(lg, lg, spread(l1[:, 0, :], E2), ALU.subtract).then_inc(sl["gate_shifted"], 1)
                dve.wait_ge(sl["gate_exp"], 1)
                link(v.tensor_reduce(l1[:, 1, :], lp, AX.X, ALU.add))
                link(v.reciprocal(l1[:, 1, :], l1[:, 1, :]))
                link(v.tensor_tensor(lp, lp, spread(l1[:, 1, :], E2), ALU.mult))
                ramp = col("f", "ramp")[:, 0:E2]
                top(lp, lpick, l1[:, 2, :], l1[:, 3, :], E2, ramp)
                link(v.scalar_tensor_tensor(lg, lpick, -2.0, lp, ALU.mult, ALU.add))
                top(lg, lsel, l1[:, 4, :], l1[:, 5, :], E2, ramp)
                link(v.tensor_tensor(lsel, lsel, lpick, ALU.add))
                link(v.tensor_tensor(lsel, lsel, lp, ALU.mult))
                link(v.tensor_reduce(l1[:, 6, :], lsel, AX.X, ALU.add))
                link(v.tensor_scalar(l1[:, 6, :], l1[:, 6, :], TINY, None, ALU.add))
                link(v.reciprocal(l1[:, 6, :], l1[:, 6, :]))
                link(v.memset(lw[:, :, 0:1], 1.0))
                v.tensor_tensor(lw[:, :, 1:E2 + 1], lsel, spread(l1[:, 6, :], E2), ALU.mult).then_inc(sl["route_ready"], 1)
                dve.wait_ge(sl["routeT_psum"], 1)
                v.tensor_copy(lwT[0:E2 + 1, BANK:2 * BANK], bank[6][0:E2 + 1, :]).then_inc(sl["routeT_ready"], 1)
                dve.wait_ge(sl["low_ready"], 2)
                for c in range(2):
                    dve.wait_ge(sl["wide_psum"], c + 1)
                    v.tensor_tensor(lowTm[0:RU, c * BANK:(c + 1) * BANK], lowT[0:RU, c * BANK:(c + 1) * BANK],
                                    bank[7 * c][0:RU, :], ALU.mult).then_inc(sl["mixed"], 1)
                add_to_x(sl["out_psum"], (2, 3))

            v.memset(ones[:, :], 1.0).then_inc(constants, 1)
            v.memset(low_bias[:, :], -CLIP).then_inc(constants, 1)
            normalise(FIRST_JOBS)
            dve.wait_ge(loaded["a"], 16)
            v.tensor_copy(identb[:, :], ident).then_inc(constants, 1)
            v.tensor_copy(causalb[:, :], col("a", "causal")).then_inc(constants, 1)
            effective_weights()
            attention(att0, None, None, col("a", "bq0"), col("a", "bv0"))
            add_to_x(att0.out_psum, (0, 1))
            if stages > 1:
                normalise(CROSS_JOBS[0])
                cross_context()
                normalise(CROSS_JOBS[1])
                cross_context_normed()
                cross_units()
                add_to_x(sx["out_psum"], (0, 1))
            if stages > 2:
                dve.wait_ge(loaded["f"], 16)
                normalise([("n2", 0), ("n2", 1)])
                normalise([("ln1", 0), ("ln1", 1)])
                attention(att1, col("f", "ln1_g"), col("f", "ln1_b"), col("f", "bq2"), col("f", "bv2"))
                experts()
            if stages > 3:
                dve.wait_ge(loaded["l"], 16)
                normalise([("n3", 0), ("n3", 1)])
                attention(att2, None, None, col("l", "zero"), col("l", "zeros"))
                add_to_x(att2.out_psum, (0, 1))
            if stages > 4:
                single()
            if stages > 5:
                mixture()

        @block.gpsimd
        def _(pool):
            done = [0]

            def link(instruction):
                instruction.then_inc(pool_chain, 1)
                done[0] += 1
                pool.wait_ge(pool_chain, done[0])

            def rstd_jobs(keys):
                for key in keys:
                    k = jobs[key][0]
                    pool.wait_ge(var_ready, k + 1)
                    link(pool.tensor_scalar(stat[:, k % 4, 2, :], stat[:, k % 4, 1, :], 1.0 / D, EPS, ALU.mult, ALU.add))
                    pool.tensor_tensor(stat[:, k % 4, 3, :], stat[:, k % 4, 2, :], half[:, :], ALU.pow)\
                        .then_inc(rstd_ready, 1)

            def attention(a):
                pool.wait_ge(a.qv_ready, 4)
                headmask = col("a", "headmask")

                def body(it, b, g, prev):
                    for j in range(HG):
                        if prev:
                            pool.wait_ge(a.score_psum, it * HG + j - 3)
                        pool.tensor_tensor(qm[:, j, :], qT[:, bass.ds(b * T, T)],
                                           headmask[:, bass.ds(g * HG + j, 1)].broadcast_to([P, T]), ALU.mult)\
                            .then_inc(a.qm_ready, 1)

                body(0, 0, 0, False)
                with pool.Fori(1, H) as it:
                    body(it, it // G, it % G, True)

            def cross():
                def pair(it, prev):
                    for u in range(2):
                        if prev:
                            pool.wait_ge(sx["q_psum"], it * 8 - 1 + u)
                        pool.tensor_copy(acur[:, u, :], A_flat[:, bass.ds(it * 2 * P + u * P, P)])\
                            .then_inc(sx["acur_ready"], 1)

                pool.wait_ge(prep_act, 9)
                pair(0, False)
                with pool.Fori(1, XP + 1) as it:
                    pair(it, True)

            def experts():
                pool.wait_ge(sf["routeT_ready"], 2)
                sel = col("f", "sel")

                def source(e, slot, prev):
                    if prev:
                        pool.wait_ge(sf["mix_psum"], e * 2 - 2)
                    pool.tensor_tensor(mixsrc[0:E + 1, slot, :], routeT[0:E + 1, :],
                                       sel[0:E + 1, bass.ds(e, 1)].broadcast_to([E + 1, B * T]), ALU.mult)\
                        .then_inc(sf["mixsrc_ready"], 1)

                source(0, 0, False)
                source(1, 1, False)
                source(2, 0, True)
                with pool.Fori(1, E // 2) as i:
                    for k in range(2):
                        source(i * 2 + k + 1, 1 - k, True)

            pool.memset(half[:, :], -0.5).then_inc(pool_chain, 1)
            done[0] += 1
            pool.wait_ge(pool_chain, 1)
            rstd_jobs(FIRST_JOBS)
            pool.wait_ge(loaded["a"], 16)
            attention(att0)
            if stages > 1:
                rstd_jobs(CROSS_JOBS[0])
                rstd_jobs(CROSS_JOBS[1])
                cross()
            if stages > 2:
                rstd_jobs([("n2", 0), ("n2", 1), ("ln1", 0), ("ln1", 1)])
                attention(att1)
                rstd_jobs([("ln2", 0), ("ln2", 1)])
                pool.wait_ge(loaded["f"], 16)
                experts()
            if stages > 3:
                rstd_jobs([("n3", 0), ("n3", 1)])
                attention(att2)
            if stages > 4:
                rstd_jobs([("n4", 0), ("n4", 1)])
            if stages > 5:
                rstd_jobs([("n5", 0), ("n5", 1)])


def _arrange(inputs):
    f = lambda n: np.asarray(inputs[n])

    def rows(a, n=P):
        out = np.zeros((n,) + a.shape[1:], np.float32)
        out[:a.shape[0]] = a
        return out

    def column(v):
        return np.ascontiguousarray(v).reshape(-1, 1)

    def repeated(v):
        return np.broadcast_to(v.reshape(1, -1), (P, v.size))

    def grouped(w, bias=None):
        out = np.zeros((HG, ROWS, G, w.shape[1]), np.float32)
        out[:, :HD] = w.reshape(G, HG, HD, -1).transpose(1, 2, 0, 3)
        if bias is not None:
            out[0, HD, 0] = bias
        return out.reshape(P, G * w.shape[1])

    qkv = f("L0_attn_b_attn").reshape(3, D)
    b2 = f("L0_ffn_bqkv").reshape(3, D)
    wx = f("L0_xattn_Wkv")
    wv = np.concatenate([wx[:, XH * XD:], wx[:, XH * XD:XH * XD + P]], 1)

    def pairs(w):
        return np.ascontiguousarray(w.T).reshape(XP, P, D).transpose(1, 0, 2).reshape(P, XP * D)

    low_rows = np.concatenate([f("L1_ffn_shared_A")[None], f("L1_ffn_routed_A")]).reshape(RU, D)
    low_cols = np.concatenate([f("L1_ffn_shared_B").T[None], f("L1_ffn_routed_B").transpose(0, 2, 1)]).reshape(RU, D)
    c = {
        "ident": np.eye(P, dtype=np.float32),
        "headmask": (np.arange(P)[:, None] // HD == np.arange(H)[None]).astype(np.float32),
        "causal": np.where(np.arange(P)[None] <= np.arange(P)[:, None], 0.0, MASKED).astype(np.float32),
        "la0": rows(f("L0_attn_la_attn")), "lb0": rows(f("L0_attn_lb_attn").T), "w0": f("L0_attn_w_attn").T,
        "bq0": column(qkv[0]), "bk0": column(qkv[1]), "bv0": repeated(qkv[2]),
        "lap0": rows(grouped(f("L0_attn_la_proj").T).reshape(P, G, RL).transpose(2, 1, 0).reshape(RL, G * P)),
        "lbp0": rows(f("L0_attn_lb_proj").T), "wp0": grouped(f("L0_attn_w_proj").T, f("L0_attn_b_proj")),
        "lnm_g": column(f("L0_xattn_ln_m_g")), "lnm_b": column(f("L0_xattn_ln_m_b")),
        "lnl_g": column(f("L0_xattn_ln_l_g")), "lnl_b": column(f("L0_xattn_ln_l_b")),
        "wqT": pairs(f("L0_xattn_Wq")), "wkT": pairs(wx[:, :XH * XD]), "wv": wv,
        "wout": f("L0_xattn_Wout").reshape(XP, P, D).transpose(1, 0, 2).reshape(P, XP * D),
        "ln1_g": column(f("L0_ffn_ln1_g")), "ln1_b": column(f("L0_ffn_ln1_b")), "w2": f("L0_ffn_Wqkv"),
        "bq2": column(b2[0]), "bk2": column(b2[1]), "bv2": repeated(b2[2]),
        "wp2": grouped(f("L0_ffn_Wo"), f("L0_ffn_bo")),
        "ln2_g": column(f("L0_ffn_ln2_g")), "ln2_b": column(f("L0_ffn_ln2_b")),
        "gate": np.concatenate([f("L0_ffn_gate_w"), f("L0_ffn_coef_w")], 1), "coef_b": repeated(f("L0_ffn_coef_b")),
        "ramp": np.broadcast_to(np.arange(E, 0, -1, dtype=np.float32), (P, E)),
        "sel": rows(np.eye(E + 1, dtype=np.float32)),
        "b1": np.concatenate([f("L0_ffn_b1"), f("L0_ffn_rb1")[None]]).reshape(E + 1, 1, FT, P).repeat(2, 1)
        .reshape((E + 1) * 2 * FT, P).T,
        "b2": rows(np.concatenate([f("L0_ffn_b2"), f("L0_ffn_rb2")[None]])),
        "w3": f("L1_attn_w_qkv").T, "zero": np.zeros((P, 1), np.float32), "zeros": np.zeros((P, D), np.float32),
        "wp3": grouped(f("L1_attn_w_proj").T),
        "wq4": f("L1_xattn_kernel_q"), "wk4": f("L1_xattn_kernel_k"), "wv4": f("L1_xattn_kernel_v"),
        "bq4": column(f("L1_xattn_bias_q")), "bk4": column(f("L1_xattn_bias_k")), "bv4": repeated(f("L1_xattn_bias_v")),
        "base": f("L1_ffn_base_W").T, "lowA": low_rows.T, "lowB": rows(low_cols),
        "base_b": rows(f("L1_ffn_base_b").reshape(1, D)), "router": f("L1_ffn_router_W").T,
        "router_b": repeated(f("L1_ffn_router_b")),
        "sel7": rows((np.arange(E2 + 1)[:, None] == np.arange(RU)[None] // R2).astype(np.float32)),
    }
    arrays = {f"pack_{key}": np.concatenate([c[n] for n, _ in columns], 1) for key, columns in LAYOUT.items()}
    arrays["x"] = f("x")
    arrays["ctx"] = f("ctx_1024")
    arrays["mask"] = f("mask_1xSxS2_ff0")
    arrays["w1"] = np.concatenate([f("L0_ffn_W1"), f("L0_ffn_rW1")[None]])
    arrays["w2"] = np.concatenate([f("L0_ffn_W2"), f("L0_ffn_rW2")[None]]).reshape(E + 1, FT, P, D)\
        .transpose(0, 2, 1, 3).reshape(E + 1, P, FT * D)
    return arrays


def kernel(**inputs):
    import concourse.bacc as _bacc
    from concourse.bass_utils import run_bass_kernel_spmd as _run

    nc = _bacc.Bacc("TRN2", target_bir_lowering=False, num_devices=1)
    arrays = {f"in_{n}": np.ascontiguousarray(a) for n, a in _arrange(inputs).items()}
    d = {n[3:]: nc.dram_tensor(n, a.shape, mybir.dt.from_np(a.dtype), kind="ExternalInput").ap() for n, a in arrays.items()}
    out = nc.dram_tensor("out", (B, T, D), mybir.dt.float32, kind="ExternalOutput").ap()
    decoder(nc, d["x"], d["ctx"], d["mask"], {k: d[f"pack_{k}"] for k in LAYOUT}, d["w1"], d["w2"], out)
    return _run(nc, [arrays], core_ids=[0]).results[0]["out"]
```

```python
from contextlib import ExitStack

import numpy as np
import concourse.bass as bass
from concourse import mybir

P = 128
D = 128
B = 4
T = 256
S2 = 512
NT = B * T // P
NC = B * S2 // P
BANK = 512
EPS = 1e-5

H = 16
HD = D // H
G = 4
HG = H // G
ROWS = P // HG

XH = 16
XD = 64
XP = XH // 2
KEYS = S2 + T
KT = KEYS // P

E = 8
F = 512
FT = F // P
E2 = 6
R2 = 16
RU = (E2 + 1) * R2
RL = 32
MASKED = -1e30
CLIP = 100.0
TINY = 1e-6
FLOOR = 1e-8

LAYOUT = {
    "a": [("ident", P), ("headmask", H), ("causal", P), ("la0", D), ("lb0", 3 * D), ("w0", 3 * D),
          ("bq0", 1), ("bk0", 1), ("bv0", D)],
    "b": [("lap0", G * P), ("lbp0", D), ("wp0", G * D), ("lnm_g", 1), ("lnm_b", 1), ("lnl_g", 1), ("lnl_b", 1)],
    "q": [("wqT", XP * D), ("wkT", XP * D)],
    "v": [("wv", (XP + 1) * P), ("wout", XP * D)],
    "f": [("ln1_g", 1), ("ln1_b", 1), ("w2", 3 * D), ("bq2", 1), ("bk2", 1), ("bv2", D), ("wp2", G * D),
          ("ln2_g", 1), ("ln2_b", 1), ("gate", E + 2), ("coef_b", 2), ("ramp", E),
          ("b1", (E + 1) * 2 * FT), ("b2", D)],
    "l": [("w3", 3 * D), ("zero", 1), ("zeros", D), ("wp3", G * D), ("wq4", D), ("wk4", D), ("wv4", D), ("bq4", 1), ("bk4", 1),
          ("bv4", D), ("base", D), ("lowA", RU), ("lowB", D), ("base_b", D), ("router", E2), ("router_b", E2),
          ("sel7", RU)],
}


class Chain:

    def __init__(self, sem):
        self.sem, self.base, self.n = sem, 0, 0

    def did(self, instruction):
        instruction.then_inc(self.sem, 1)
        self.n += 1

    def wait(self, engine):
        engine.wait_ge(self.sem, self.base + self.n)

    def enter(self, iteration, first, each):
        self.start = self.n
        self.base, self.n, self.each = iteration * each + (self.start - first * each), 0, each

    def leave(self, iterations):
        assert self.n == self.each, (self.n, self.each)
        self.base, self.n = 0, self.start + iterations * self.each


def decoder(nc, x_d, ctx_d, mask_d, packs_d, w1_d, w2_d, out_d, stages=6):
    f32, f32r, bf16 = mybir.dt.float32, mybir.dt.float32r, mybir.dt.bfloat16
    ALU, ACT, AX = mybir.AluOpType, mybir.ActivationFunctionType, mybir.AxisListType

    ctx = ExitStack()
    with ctx:
        def sb(name, shape, dt=f32):
            return ctx.enter_context(nc.sbuf_tensor(name, shape, dt))

        def sem(name):
            return ctx.enter_context(nc.semaphore(name))

        x = sb("x", [P, NT, D])
        z = sb("z", [P, NT, D])
        z2 = sb("z2", [P, NT, D])
        zT = sb("zT", [P, NT * P])
        with nc.sbuf_tensor("ctx_x", [P, NC, D], f32) as ctx_x, nc.sbuf_tensor("ctx_z", [P, NC, D], f32) as ctx_z, \
                nc.sbuf_tensor("centred", [P, 4, 4, D], f32) as centred, \
                nc.sbuf_tensor("squares", [P, 2, 4, D], f32) as squares:
            pass
        kv_high = sb("kv_high", [P, B, KEYS], f32r)
        kv_low = sb("kv_low", [P, B, KEYS], f32r)
        sb("behind_kv_low", [P, 2 * NC * D + 6 * 4 * D - 2 * B * KEYS])
        stat = sb("stat", [P, 4, 4, 4])
        half = sb("half", [P, 4])
        ctxT = sb("ctxT", [P, NC * P])
        kvT = sb("kvT", [P, B, KEYS])
        packs = {key: sb(f"pack_{key}", [P, sum(w for _, w in columns)]) for key, columns in LAYOUT.items()}
        identb = sb("identb", [P, P], bf16)
        causalb = sb("causalb", [P, P], bf16)
        ones = sb("ones_", [P, T])
        A_all = sb("A_all", [P, XH + 2, P])
        A_flat = A_all[:, :, :].rearrange("p h c -> p (h c)")
        low_bias = sb("low_bias", [P, 1])
        weff = sb("weff", [P, 3 * D])
        wpeff = sb("wpeff", [P, G * D])

        ARENA = 17664
        arena = sb("arena", [P, ARENA])

        class Area:
            def __init__(self):
                self.at = 0

            def __call__(self, *dims):
                n = int(np.prod(dims))
                view = arena[:, self.at:self.at + n]
                self.at += n
                assert self.at <= ARENA, self.at
                if len(dims) == 2:
                    return view.rearrange("p (a b) -> p a b", a=dims[0])
                if len(dims) == 3:
                    return view.rearrange("p (a b c) -> p a b c", a=dims[0], b=dims[1])
                return view

        area = Area()
        qT, kT = area(NT * P), area(NT * P)
        v_tok = area(NT, D)
        qm = area(HG, T)
        v_aug = area(2, HG * ROWS)
        prob = area(HG, 2, T)
        eraw = area(HG, 2, T)
        pT = area(HG, 2 * (T + 1))
        yT = area(G, NT * P)
        sums = area(H, 2 * HG)
        negmax = area(HG, 2)
        low = area(HG, 2)
        small = area(8, 2 * HG)
        rbc = area(2, 2, P)
        rb = area(2, T)
        vsum = area(1)
        ytmp = area(T)

        area = Area()
        oT = area(XP, NT * P)
        xpT = area(2, 2, KT * T)
        xprob = area(2, 2 * KEYS)

        xv = sb("xv", [P, B, KT * P])
        xq_high = sb("xq_high", [P, 2, T], f32r)
        xq_low = sb("xq_low", [P, 2, T], f32r)
        acur = sb("acur", [P, 2, P])
        xnegmax = sb("xnegmax", [P, 2, 2])
        xsums = sb("xsums", [P, 2, 2, 2])
        xr = sb("xr", [P, 4])
        xrbc = sb("xrbc", [P, 2, P])
        xrb = sb("xrb", [P, T])

        area = Area()
        xin = area(NT, D)
        w1b = area(2, F)
        w2b = area(2, FT * D)
        hid = area(2 * FT, BANK)
        gates = area(NT, E + 2)
        probs = area(NT, E)
        pick = area(NT, E)
        coef = area(NT, 2)
        g1 = area(8, NT)
        route = area(NT, E + 1)
        routeT = area(NT * P)

        area = Area()
        qx = area(NT * P)
        kx = area(NC * P)
        vx = area(NC, D)
        maskx = area(2, S2)
        sm = area(2, S2)
        px = area(2, S2)
        pxT = area(2, S2)
        nm1, sm1, r1 = area(NT), area(NT), area(NT)

        area = Area()
        lowT = area(NT * P)
        lowTm = area(NT * P)
        lg, lp, lpick, lsel, lw = area(NT, E2), area(NT, E2), area(NT, E2), area(NT, E2), area(NT, E2 + 1)
        l1 = area(8, NT)
        lwT = area(NT * P)

        psum = ctx.enter_context(nc.psum_tensor("psum", [P, 8, BANK], f32))
        bank = [psum[:, i, :] for i in range(8)]

        def col(key, name):
            at = 0
            for n, w in LAYOUT[key]:
                if n == name:
                    return packs[key][:, at:at + w]
                at += w
            raise KeyError(name)

        ident = col("a", "ident")

        def banks_pair(half):
            return psum[:, 2 * half:2 * half + 2, 0:KEYS // 2]

        def tiles(view):
            return view.rearrange("p (t c) -> p t c", c=D)

        def spread(view, n):
            return view.unsqueeze(2).broadcast_to([P, view.shape[1], n])

        loaded = {k: sem(f"loaded_{k}") for k in ("ctx", "a", "b", "q", "v", "f", "l", "mask")}
        loaded_x = [sem("loaded_x0"), sem("loaded_x1")]
        stored = sem("stored")
        constants = sem("constants")
        dve_chain, pool_chain = sem("dve_chain"), sem("pool_chain")
        centred_ready, squared, rstd_ready = sem("centred_ready"), sem("squared"), sem("rstd_ready")
        normed = sem("normed")
        var_ready = sem("var_ready")
        prep_psum, prep_act, prep_dve = sem("prep_psum"), sem("prep_act"), sem("prep_dve")
        x_done, x_parts = sem("x_done"), sem("x_parts")
        CONSTANTS = 4

        class Attention:

            def __init__(self, tag, causal, clip, act_heads):
                self.causal, self.clip = causal, clip
                self.evacuations = [(), (0, 1), (2,), (3,)]
                self.act_heads = act_heads
                self.dve_heads = [j for j in range(HG) if j not in act_heads]
                self.zT_psum = sem(f"{tag}_zT_psum")
                self.zT_act = sem(f"{tag}_zT_act")
                self.qkv_psum = sem(f"{tag}_qkv_psum")
                self.k_ready = sem(f"{tag}_k_ready")
                self.qv_ready = sem(f"{tag}_qv_ready")
                self.qm_ready = sem(f"{tag}_qm_ready")
                self.score_psum = sem(f"{tag}_score_psum")
                self.max_ready = sem(f"{tag}_max_ready")
                self.exp_done = sem(f"{tag}_exp_done")
                self.clip_done = sem(f"{tag}_clip_done")
                self.pT_psum = sem(f"{tag}_pT_psum")
                self.pT_act = sem(f"{tag}_pT_act")
                self.pT_dve = sem(f"{tag}_pT_dve")
                self.v_aug_ready = sem(f"{tag}_v_aug_ready")
                self.y_psum = sem(f"{tag}_y_psum")
                self.rbc_ready = sem(f"{tag}_rbc_ready")
                self.rb_psum = sem(f"{tag}_rb_psum")
                self.rb_ready = sem(f"{tag}_rb_ready")
                self.y_done = sem(f"{tag}_y_done")
                self.out_psum = sem(f"{tag}_out_psum")

            def evacuated(self, eng, it, j):
                if j in self.act_heads:
                    eng.wait_ge(self.pT_act, it * len(self.act_heads) + self.act_heads.index(j) + 1)
                else:
                    eng.wait_ge(self.pT_dve, it * len(self.dve_heads) + self.dve_heads.index(j) + 1)

            def probabilities(self, eng, n):
                if self.clip:
                    eng.wait_ge(self.clip_done, n * 2)
                else:
                    eng.wait_ge(self.exp_done, n)

            def pT_of(self, j):
                if self.clip:
                    return pT[:, j, :].rearrange("p (k t) -> p k t", k=2)[:, :, 0:T]
                return pT[:, j, 0:len(self.blocks()) * P]

            def pT_from(self, j):
                if self.clip:
                    return bank[4 + j % 2].rearrange("p (k t) -> p k t", k=2)
                return bank[4 + j % 2][:, 0:len(self.blocks()) * P]

            def blocks(self):
                return [(0, 0), (0, 1), (1, 1)] if self.causal and not self.clip else [(0, 0), (0, 1), (1, 0), (1, 1)]

        att0 = Attention("att0", True, False, [1])
        att1 = Attention("att1", False, False, [1])
        att2 = Attention("att2", True, True, [0, 1, 2, 3])

        def family(tag, *names):
            return {n: sem(f"{tag}_{n}") for n in names}

        sx = family("x", "zT_psum", "zT_act", "zT_dve", "acur_ready", "q_psum", "q_high", "q_ready", "kv_high", "kv_split", "v_psum", "v_ready",
                    "score_psum", "max_ready", "exp_done", "pT_psum", "pT_act", "pT_dve", "y_psum", "rbc_ready",
                    "rb_psum", "rb_ready", "y_done", "out_psum")
        sf = family("f", "xin_ready", "zT_psum", "zT_act", "gate_psum", "gate_shifted", "gate_exp",
                    "route_ready", "routeT_psum", "routeT_ready", "bias_psum", "hid_psum", "gelu_done", "down_psum",
                    "mixed", "w_slot0", "w_slot1")
        sg = family("g", "zT_psum", "zT_act", "zT_dve", "proj_psum", "proj_act", "proj_dve", "score_psum",
                    "max_ready", "exp_done", "pT_psum", "pT_ready", "out_psum")
        sl = family("l", "zT_psum", "zT_act", "zT_dve", "low_psum", "low_ready", "gate_psum", "base_psum", "base_added", "gate_shifted",
                    "gate_exp", "route_ready", "routeT_psum", "routeT_ready", "wide_psum", "mixed", "out_psum")

        jobs = {}

        def job(key, src, dst, after):
            jobs[key] = (len(jobs), src, dst, after)

        def quarter(view, h):
            return view[:, 4 * h:4 * h + 4, :]

        for h in range(2):
            job(("n0", h), quarter(x, h), quarter(z, h), (loaded_x[h], 16))
        for c in range(4):
            job(("ctx", c), quarter(ctx_x, c), quarter(ctx_z, c), (loaded["ctx"], 16))
        def again(name, s, h):
            job((name, h), quarter(z, h), quarter(z2, h), (normed, jobs[(f"n{s}", h)][0] + 1))

        for s in range(1, 6):
            for h in range(2):
                job((f"n{s}", h), quarter(x, h), quarter(z, h), (x_done, 2 * s - 1 + h))
                if s == 2:
                    again("ln1", s, h)
            if s == 1:
                for h in range(2):
                    again("lat", s, h)
            if s == 2:
                for h in range(2):
                    job(("ln2", h), quarter(xin, h), quarter(z2, h), (sf["xin_ready"], h + 1))
        FIRST_JOBS = [("n0", 0), ("n0", 1)]
        CONTEXT_JOBS = [[("ctx", 0), ("ctx", 1)], [("ctx", 2), ("ctx", 3)]]

        def wait_normed(eng, name, h):
            eng.wait_ge(normed, jobs[(name, h)][0] + 1)

        block = ctx.enter_context(nc.Block())


        @block.sync
        def _(sp):
            for h in range(2):
                sp.dma_start(quarter(x, h), x_d[2 * h:2 * h + 2].rearrange("b (u p) c -> p (b u) c", p=P))\
                    .then_inc(loaded_x[h], 16)
            sp.dma_start(packs["a"][:, :], packs_d["a"]).then_inc(loaded["a"], 16)
            sp.dma_start(ctx_x[:, :, :], ctx_d.rearrange("b (u p) c -> p (b u) c", p=P)).then_inc(loaded["ctx"], 16)
            sp.dma_start(packs["b"][:, :], packs_d["b"]).then_inc(loaded["b"], 16)
            sp.dma_start(packs["q"][:, :], packs_d["q"]).then_inc(loaded["q"], 16)
            sp.dma_start(packs["v"][:, :], packs_d["v"]).then_inc(loaded["v"], 16)
            sp.dma_start(packs["f"][:, :], packs_d["f"]).then_inc(loaded["f"], 16)
            sp.dma_start(packs["l"][:, :], packs_d["l"]).then_inc(loaded["l"], 16)
            if stages > 2:
                def expert(e, slot):
                    sp.dma_start(w1b[:, slot, :], w1_d[e]).then_inc(sf[f"w_slot{slot}"], 16)
                    sp.dma_start(w2b[:, slot, :], w2_d[e]).then_inc(sf[f"w_slot{slot}"], 16)

                sp.wait_ge(sf["xin_ready"], 1)
                expert(0, 0)
                expert(1, 1)
                sp.wait_ge(sf["down_psum"], 2)
                expert(2, 0)
                with sp.Fori(1, E // 2) as i:
                    for k in range(2):
                        sp.wait_ge(sf["down_psum"], (i * 2 + k) * 2)
                        expert(i * 2 + k + 1, 1 - k)
            if stages > 4:
                sp.wait_ge(x_done, 8)
                sp.dma_start(maskx, mask_d[0].rearrange("(u p) k -> p u k", p=P)).then_inc(loaded["mask"], 16)
            for h in range(2):
                sp.wait_ge(x_done, 2 * stages - 1 + h)
                sp.dma_start(out_d[2 * h:2 * h + 2].rearrange("b (u p) c -> p (b u) c", p=P), quarter(x, h))\
                    .then_inc(stored, 16)
            sp.wait_ge(stored, 32)

        @block.tensor
        def _(pe):
            mm, transpose = nc.tensor.matmul, nc.tensor.transpose

            def transposes(name, src, h, done):
                wait_normed(pe, name, h)
                for t in range(4):
                    last = transpose(bank[h][:, t * P:(t + 1) * P], src[:, 4 * h + t, :], ident)
                last.then_inc(done, 1)

            def effective_weights():
                pe.wait_ge(loaded["a"], 16)
                mm(bank[0][:, 0:3 * D], col("a", "la0")[0:RL, :], col("a", "lb0")[0:RL, :], start=True, stop=True)\
                    .then_inc(prep_psum, 1)
                pe.wait_ge(prep_dve, 1)

            def effective_projection():
                pe.wait_ge(loaded["b"], 16)
                for g in range(G):
                    last = mm(bank[7][:, g * D:(g + 1) * D], col("b", "lap0")[0:RL, g * P:(g + 1) * P],
                              col("b", "lbp0")[0:RL, :], start=True, stop=True)
                last.then_inc(prep_psum, 1)

            def cross_operands():
                pe.wait_ge(loaded["q"], 16)
                for h in range(XH):
                    r = slice(XD * (h % 2), XD * (h % 2) + XD)
                    c = slice((h // 2) * D, (h // 2 + 1) * D)
                    bk, s = 2 + 2 * (h % 2) + h // 8, (h // 2) % 4
                    last = mm(bank[bk][:, s * P:(s + 1) * P], col("q", "wqT")[r, c], col("q", "wkT")[r, c],
                              start=True, stop=True)
                    if s == 3:
                        last.then_inc(prep_psum, 1)
                pe.wait_ge(loaded["ctx"], 16)
                for i in range(8):
                    c = i % 4
                    if i >= 4:
                        pe.wait_ge(normed, jobs[("ctx", c)][0] + 1)
                    if i >= 2:
                        pe.wait_ge(prep_act, i + 4)
                    src = ctx_x if i < 4 else ctx_z
                    for t in range(4):
                        last = transpose(bank[6 + c % 2][:, t * P:(t + 1) * P], src[:, 4 * c + t, :], ident)
                    last.then_inc(prep_psum, 1)
                for h in range(2):
                    transposes("lat", z2, h, sx["zT_psum"])

            def attention(a, src, name, w, wp, aside=None):
                for h in range(2):
                    transposes(name, src, h, a.zT_psum)
                    if h == 0 and aside:
                        aside()
                    pe.wait_ge(a.zT_act, h + 1)
                    cols = slice(h * BANK, (h + 1) * BANK)
                    mm(bank[2 + h][:, :], w[:, 0:D], zT[:, cols], start=True, stop=True).then_inc(a.qkv_psum, 1)
                    mm(bank[4 + h][:, :], w[:, D:2 * D], zT[:, cols], start=True, stop=True).then_inc(a.qkv_psum, 1)
                    if h and aside:
                        pe.wait_ge(prep_dve, 2)
                    for t in range(4):
                        last = mm(bank[6 + h][:, t * P:(t + 1) * P], zT[:, (4 * h + t) * P:(4 * h + t + 1) * P],
                                  w[:, 2 * D:3 * D], start=True, stop=True)
                    last.then_inc(a.qkv_psum, 1)
                pe.wait_ge(a.k_ready, 1)
                pe.wait_ge(a.qv_ready, 3)

                def scores(it, b, j, prev):
                    pe.wait_ge(a.qm_ready, it * HG + j + 1)
                    if prev:
                        pe.wait_ge(a.exp_done, it * HG + j - 3)
                    for u in range(2):
                        keys = P if a.causal and u == 0 else T
                        last = mm(bank[j][:, u * T:u * T + keys], qm[:, j, u * P:(u + 1) * P],
                                  kT[:, bass.ds(b * T, keys)], start=True, stop=not a.causal)
                        if a.causal:
                            last = mm(bank[j][:, u * T + keys - P:u * T + keys], identb[:, :], causalb[:, :],
                                      start=False, stop=True)
                    last.then_inc(a.score_psum, 1)

                def transposed(it, j, prev=True):
                    a.probabilities(pe, it * HG + j + 1)
                    if j >= 2:
                        a.evacuated(pe, it, j - 2)
                    elif j == 0 and prev:
                        a.evacuated(pe, it - 1, 2)
                    for i, (k, u) in enumerate(a.blocks()):
                        last = transpose(bank[4 + j % 2][:, i * P:(i + 1) * P], prob[:, j, u, k * P:(k + 1) * P], ident)
                    last.then_inc(a.pT_psum, 1)

                def weighted(group):
                    for j in range(HG):
                        a.evacuated(pe, group, j)
                    pe.wait_ge(a.v_aug_ready, group + 1)
                    pe.wait_ge(a.y_done, group + 1)
                    for k in range(2):
                        dst, keys = slice(0, T), slice(k * T, (k + 1) * T)
                        if a.clip:
                            dst, keys = slice(0, T + 1), slice(k * (T + 1), (k + 1) * (T + 1))
                        elif k and len(a.blocks()) == 3:
                            dst, keys = slice(P, T), slice(T, T + P)
                        for j in range(HG):
                            last = mm(bank[6][ROWS * j:ROWS * (j + 1), dst], v_aug[:, k, ROWS * j:ROWS * (j + 1)],
                                      pT[:, j, keys], start=(k == 0), stop=(k == 1))
                    last.then_inc(a.y_psum, 1)
                    pe.wait_ge(a.rbc_ready, group + 1)
                    for k in range(2 if a.clip else 1):
                        for u in range(2):
                            last = transpose(bank[7][:, k * T + u * P:k * T + (u + 1) * P], rbc[:, k, u, :], ident)
                    last.then_inc(a.rb_psum, 1)

                def body(it, b, cur=True, prev=True, prev2=True):
                    for j in range(HG):
                        if cur:
                            scores(it, b, j, prev)
                        if j == 1 and prev2:
                            weighted(it - 2)
                        if prev:
                            transposed(it - 1, j, prev2)

                body(0, 0, prev=False, prev2=False)
                pe.wait_ge(a.k_ready, 2)
                body(1, 0, prev2=False)
                with pe.Fori(2, H) as it:
                    body(it, it // G)

                def project(h):
                    for t in range(4 * h, 4 * h + 4):
                        for g in range(G):
                            last = mm(bank[h][:, (t % 4) * P:(t % 4 + 1) * P], yT[:, g, t * P:(t + 1) * P],
                                      wp[:, g * D:(g + 1) * D], start=(g == 0), stop=(g == G - 1))
                    last.then_inc(a.out_psum, 1)

                body(H, 0, cur=False)
                pe.wait_ge(a.y_done, H // 2 + 1)
                pe.wait_ge(a.exp_done, H * HG - 3)
                project(0)
                body(H + 1, 0, cur=False, prev=False)
                pe.wait_ge(a.y_done, H + 1)
                project(1)

            def cross():
                cross_operands()
                pe.wait_ge(sx["zT_act"], 1)
                pe.wait_ge(sx["zT_dve"], 1)
                pe.wait_ge(prep_act, 13)
                pe.wait_ge(loaded["v"], 16)
                wv, wo = col("v", "wv"), col("v", "wout")
                W = KEYS // 2

                def queries(it, u):
                    pe.wait_ge(sx["acur_ready"], it * 2 + u % 2 + 1)
                    mm(bank[6][:, T:2 * T], acur[:, u % 2, :], kvT[:, u // 2, S2:KEYS], start=True, stop=True)\
                        .then_inc(sx["q_psum"], 1)

                def values(it, b, half):
                    for k in range(3):
                        kt = 3 * half + k
                        last = mm(bank[7][:, k * P:(k + 1) * P], kvT[:, b, kt * P:(kt + 1) * P],
                                  wv[:, bass.ds(it * P, P)], start=True, stop=True)
                    last.then_inc(sx["v_psum"], 1)

                def scores(u, half):
                    for c in range(2):
                        out, tile, keys = bank[2 * half + c][:, 0:W], slice(half * P, (half + 1) * P), slice(c * W, (c + 1) * W)
                        mm(out, xq_high[:, u % 2, tile], kv_high[:, u // 2, keys], start=True, stop=False)
                        mm(out, xq_high[:, u % 2, tile], kv_low[:, u // 2, keys], start=False, stop=False)
                        last = mm(out, xq_low[:, u % 2, tile], kv_high[:, u // 2, keys], start=False, stop=True)
                    last.then_inc(sx["score_psum"], 1)

                def transposed(m, u, chunks, first=False):
                    pe.wait_ge(sx["exp_done"], m * 2 + 2)
                    for c in chunks:
                        if c == 2:
                            pe.wait_ge(sx["pT_act"], m * 2 + 1)
                        elif not first:
                            if c:
                                pe.wait_ge(sx["pT_act"], m * 2)
                            else:
                                pe.wait_ge(sx["pT_dve"], m)
                        for i in range(2):
                            kt = 2 * c + i
                            for h in range(2):
                                last = transpose(bank[4 + (3 * u + c) % 2][:, (2 * i + h) * P:(2 * i + h + 1) * P],
                                                 xprob[:, u % 2, h * KEYS + kt * P:h * KEYS + (kt + 1) * P], ident)
                        last.then_inc(sx["pT_psum"], 1)

                def weighted(p, b):
                    pe.wait_ge(sx["pT_dve"], p * 2 + 2)
                    pe.wait_ge(sx["pT_act"], p * 4 + 4)
                    pe.wait_ge(sx["y_done"], p + 1)
                    for kt in range(KT):
                        for a in range(2):
                            last = mm(bank[6][XD * a:XD * (a + 1), 0:T], xv[:, b, kt * P + XD * a:kt * P + XD * (a + 1)],
                                      xpT[:, b % 2, a, kt * T:(kt + 1) * T], start=(kt == 0), stop=(kt == KT - 1))
                    last.then_inc(sx["y_psum"], 1)

                def factors(p):
                    pe.wait_ge(sx["rbc_ready"], p + 1)
                    for u in range(2):
                        last = transpose(bank[6][:, T + u * P:T + (u + 1) * P], xrbc[:, u, :], ident)
                    last.then_inc(sx["rb_psum"], 1)

                queries(0, 0)
                for half in range(2):
                    if half:
                        pe.wait_ge(sx["v_ready"], 1)
                    values(0, 0, half)

                def body(it, prev, cur):
                    for u in range(8):
                        n, b, odd = it * 8 + u, u // 2, u % 2
                        weigh = odd and (prev or u > 1)
                        behind = (prev and u == 0) or (cur and u)
                        if cur:
                            pe.wait_ge(sx["q_ready"], n + 1)
                            if prev or u:
                                pe.wait_ge(sx["exp_done"], n * 2 - 1)
                            if not prev and not odd:
                                pe.wait_ge(sx["kv_split"], b + 1)
                            scores(u, 0)
                            if odd:
                                queries(it + (u + 1) // 8, (u + 1) % 8)
                            pe.wait_ge(sx["v_ready"], n + 2)
                            values(it + (b + 1) // 4, (b + 1) % 4, odd)
                        if behind:
                            transposed(n - 1, (u - 1) % 8, (0, 1), first=(not prev and u == 1))
                        if weigh:
                            if cur:
                                pe.wait_ge(sx["q_ready"], n + 2)
                            weighted(it * 4 + b - 1, (b - 1) % 4)
                        if cur:
                            if not odd:
                                if prev or u >= 4:
                                    pe.wait_ge(sx["rb_ready"], it * 4 + b - 1)
                                    pe.wait_ge(sx["y_done"], it * 4 + b)
                                queries(it, u + 1)
                            if prev or u:
                                pe.wait_ge(sx["exp_done"], n * 2)
                            scores(u, 1)
                        if behind:
                            transposed(n - 1, (u - 1) % 8, (2,))
                        if weigh:
                            factors(it * 4 + b - 1)
                        if not cur and u == 0:
                            pe.wait_ge(sx["y_done"], XP * B - 1)
                            pe.wait_ge(sx["exp_done"], XP * B * 4)
                            project(0)
                        if not cur and u == 1:
                            break

                def project(h):
                    for t in range(4 * h, 4 * h + 4):
                        for p in range(XP):
                            last = mm(bank[h][:, (t % 4) * P:(t % 4 + 1) * P], oT[:, p, t * P:(t + 1) * P],
                                      wo[:, p * D:(p + 1) * D], start=(p == 0), stop=(p == XP - 1))
                    last.then_inc(sx["out_psum"], 1)

                body(0, False, True)
                with pe.Fori(1, XP) as it:
                    body(it, True, True)
                body(XP, True, False)
                pe.wait_ge(sx["y_done"], XP * B + 1)
                project(1)

            def experts():
                def gate():
                    transposes("ln2", z2, 1, sf["zT_psum"])
                    pe.wait_ge(sf["zT_act"], 2)
                    for t in range(NT):
                        last = mm(bank[2][:, t * (E + 2):(t + 1) * (E + 2)], zT[:, t * P:(t + 1) * P], col("f", "gate"),
                                  start=True, stop=True)
                    last.then_inc(sf["gate_psum"], 1)

                def expert(e, slot, prev, cur):
                    for u in range(2 * FT):
                        n, c, t = e * (2 * FT) + u, u // FT, u % FT
                        if not prev and u == FT:
                            gate()
                        if cur:
                            if u == 0:
                                pe.wait_ge(sf[f"w_slot{slot}"], (e // 2) * 32 + 32)
                            if prev or u >= 4:
                                pe.wait_ge(sf["gelu_done"], n - 3)
                            mm(bank[4 + u % 4][:, :], w1b[:, slot, t * P:(t + 1) * P],
                               zT[:, c * BANK:(c + 1) * BANK], start=True, stop=True).then_inc(sf["hid_psum"], 1)
                        if prev if c == 0 else cur:
                            half, s = (1, 1 - slot) if c == 0 else (0, slot)
                            if t == 0:
                                pe.wait_ge(sf["gelu_done"], n)
                                if prev:
                                    pe.wait_ge(sf["mixed"], e * 2 + c)
                            for f in range(FT):
                                last = mm(bank[2 * s + half][:, t * P:(t + 1) * P], hid[:, FT * half + f, t * P:(t + 1) * P],
                                          w2b[:, s, f * D:(f + 1) * D], start=(f == 0), stop=(f == FT - 1))
                            if t == FT - 1:
                                last.then_inc(sf["down_psum"], 1)
                        if not cur and t == FT - 1:
                            break

                transposes("ln2", z2, 0, sf["zT_psum"])
                pe.wait_ge(sf["zT_act"], 1)
                expert(0, 0, False, True)
                pe.wait_ge(sf["route_ready"], 1)
                for t in range(NT):
                    last = transpose(bank[2 + t // 4][0:E + 1, (t % 4) * P:(t % 4 + 1) * P], route[:, t, :], ident)
                last.then_inc(sf["routeT_psum"], 1)
                pe.wait_ge(sf["routeT_ready"], 2)
                for t in range(NT):
                    last = mm(bank[2 + t // 4][:, (t % 4) * P:(t % 4 + 1) * P], routeT[0:E + 1, t * P:(t + 1) * P],
                              col("f", "b2")[0:E + 1, :], start=True, stop=True)
                    if t % 4 == 3:
                        last.then_inc(sf["bias_psum"], 1)
                with pe.Fori(0, E // 2) as i:
                    for k in range(2):
                        expert(i * 2 + k + 1, 1 - k, True, True)
                expert(E + 1, 1, True, False)

            def single():
                for c in range(4):
                    mm(bank[2 + c][:, :], col("l", "wk4"), ctxT[:, c * BANK:(c + 1) * BANK], start=True, stop=True)\
                        .then_inc(sg["proj_psum"], 1)
                for c in range(4):
                    bk = bank[(6, 7, 2, 3)[c]]
                    if c >= 2:
                        pe.wait_ge(sg["proj_act"], c - 1)
                    for t in range(4):
                        last = mm(bk[:, t * P:(t + 1) * P], ctxT[:, (4 * c + t) * P:(4 * c + t + 1) * P],
                                  col("l", "wv4"), start=True, stop=True)
                    last.then_inc(sg["proj_psum"], 1)
                for h in range(2):
                    transposes("n4", z, h, sg["zT_psum"])
                pe.wait_ge(sg["zT_act"], 1)
                pe.wait_ge(sg["zT_dve"], 1)
                for c in range(2):
                    pe.wait_ge(sg["proj_act"], 3 + c)
                    mm(bank[4 + c][:, :], col("l", "wq4"), zT[:, c * BANK:(c + 1) * BANK], start=True, stop=True)\
                        .then_inc(sg["proj_psum"], 1)
                pe.wait_ge(sg["proj_dve"], 6)
                for n in range(NT + 2):
                    if n < NT:
                        if n >= 2:
                            pe.wait_ge(sg["max_ready"], n - 1)
                        mm(bank[n % 2][:, :], qx[:, n * P:(n + 1) * P], kx[:, (n // 2) * S2:(n // 2 + 1) * S2],
                           start=True, stop=True).then_inc(sg["score_psum"], 1)
                    if 1 <= n <= NT:
                        m = n - 1
                        pe.wait_ge(sg["exp_done"], m + 1)
                        if m >= 2:
                            pe.wait_ge(sg["pT_ready"], m - 1)
                        for k in range(4):
                            last = transpose(bank[2 + m % 2][:, k * P:(k + 1) * P], px[:, m % 2, k * P:(k + 1) * P], ident)
                        last.then_inc(sg["pT_psum"], 1)
                    if n >= 2:
                        m = n - 2
                        pe.wait_ge(sg["pT_ready"], m + 1)
                        if m >= 2:
                            pe.wait_ge(x_parts, m - 1)
                        for k in range(4):
                            last = mm(bank[4 + m % 2][:, 0:D], pxT[:, m % 2, k * P:(k + 1) * P],
                                      vx[:, (m // 2) * 4 + k, :], start=(k == 0), stop=(k == 3))
                        last.then_inc(sg["out_psum"], 1)

            def mixture():
                for h in range(2):
                    transposes("n5", z, h, sl["zT_psum"])
                pe.wait_ge(sl["zT_act"], 1)
                pe.wait_ge(sl["zT_dve"], 1)
                for t in range(NT):
                    last = mm(bank[4][:, t * E2:(t + 1) * E2], zT[:, t * P:(t + 1) * P], col("l", "router"),
                              start=True, stop=True)
                last.then_inc(sl["gate_psum"], 1)
                for c in range(2):
                    mm(bank[2 + c][0:RU, :], col("l", "lowA"), zT[:, c * BANK:(c + 1) * BANK], start=True, stop=True)\
                        .then_inc(sl["low_psum"], 1)
                for t in range(NT):
                    out = bank[t // 4][:, (t % 4) * P:(t % 4 + 1) * P]
                    mm(out, zT[:, t * P:(t + 1) * P], col("l", "base"), start=True, stop=False)
                    last = mm(out, ones[0:1, 0:P], col("l", "base_b")[0:1, :], start=False, stop=True)
                    if t % 4 == 3:
                        last.then_inc(sl["base_psum"], 1)
                pe.wait_ge(sl["route_ready"], 1)
                for t in range(NT):
                    last = transpose(bank[5 + t // 4][0:E2 + 1, (t % 4) * P:(t % 4 + 1) * P], lw[:, t, :], ident)
                last.then_inc(sl["routeT_psum"], 1)
                pe.wait_ge(sl["routeT_ready"], 2)
                for c in range(2):
                    mm(bank[4 + 3 * c][0:RU, :], col("l", "sel7")[0:E2 + 1, :], lwT[0:E2 + 1, c * BANK:(c + 1) * BANK],
                       start=True, stop=True).then_inc(sl["wide_psum"], 1)
                pe.wait_ge(sl["low_ready"], 2)
                for t in range(NT):
                    if t % 4 == 0:
                        pe.wait_ge(sl["mixed"], t // 4 + 1)
                    last = mm(bank[2 + t // 4][:, (t % 4) * P:(t % 4 + 1) * P], lowTm[0:RU, t * P:(t + 1) * P],
                              col("l", "lowB")[0:RU, :], start=True, stop=True)
                    if t % 4 == 3:
                        last.then_inc(sl["out_psum"], 1)

            effective_weights()
            pe.wait_ge(constants, CONSTANTS)
            attention(att0, z, "n0", weff, wpeff, effective_projection)
            if stages > 1:
                cross()
            if stages > 2:
                pe.wait_ge(loaded["f"], 16)
                attention(att1, z2, "ln1", col("f", "w2"), col("f", "wp2"))
                experts()
            if stages > 3:
                pe.wait_ge(loaded["l"], 16)
                attention(att2, z, "n3", col("l", "w3"), col("l", "wp3"))
            if stages > 4:
                single()
            if stages > 5:
                mixture()

        @block.scalar
        def _(act):
            activation = nc.scalar.activation

            def square_jobs(keys):
                for key in keys:
                    k = jobs[key][0]
                    act.wait_ge(centred_ready, k + 1)
                    if k >= 2:
                        act.wait_ge(var_ready, k - 1)
                    activation(squares[:, k % 2, :, :], centred[:, k % 4, :, :], ACT.Square).then_inc(squared, 1)

            def affine(out, in_, g, b, done):
                activation(out, in_, ACT.Identity, bias=b, scale=g).then_inc(done, 1)

            def transposed(h, psum, done, g=None, b=None):
                act.wait_ge(psum, h + 1)
                if g is None:
                    activation(zT[:, h * BANK:(h + 1) * BANK], bank[h][:, :], ACT.Copy).then_inc(done, 1)
                else:
                    affine(zT[:, h * BANK:(h + 1) * BANK], bank[h][:, :], g, b, done)

            def attention(a, g, b, bias_k, asides=(), squares_between=((), ())):
                for h in range(2):
                    transposed(h, a.zT_psum, a.zT_act, g, b)
                    square_jobs(squares_between[0] if h == 0 else ())
                    act.wait_ge(a.qkv_psum, 3 * h + 2)
                    activation(kT[:, h * BANK:(h + 1) * BANK], bank[4 + h][:, :], ACT.Identity, bias=bias_k)\
                        .then_inc(a.k_ready, 1)
                    square_jobs(squares_between[1] if h == 0 else ())
                for keys in asides[:1]:
                    square_jobs(keys)

                def exponentials(it, j, prev):
                    n = it * HG + j
                    act.wait_ge(a.max_ready, n + 1)
                    if prev:
                        if a.clip:
                            a.probabilities(act, n - 3)
                        else:
                            act.wait_ge(a.pT_psum, n - 3)
                    if a.clip:
                        activation(low[:, j, :], negmax[:, j, :], ACT.Exp, bias=low_bias[:, :])
                    for u in range(2):
                        keys = P if a.causal and u == 0 else T
                        if a.clip:
                            last = activation(eraw[:, j, u, 0:keys], bank[j][:, u * T:u * T + keys], ACT.Exp,
                                              bias=negmax[:, j, u:u + 1])
                        else:
                            last = activation(prob[:, j, u, 0:keys], bank[j][:, u * T:u * T + keys], ACT.Exp,
                                              bias=negmax[:, j, u:u + 1], accum_out=sums[:, it, u * HG + j:u * HG + j + 1])
                    last.then_inc(a.exp_done, 1)

                def evacuate(it, j, prev):
                    if j in a.act_heads:
                        act.wait_ge(a.pT_psum, it * HG + j + 1)
                        if j == 0 and prev:
                            act.wait_ge(a.y_psum, it)
                        activation(a.pT_of(j), a.pT_from(j), ACT.Copy).then_inc(a.pT_act, 1)

                def body(it, cur=True, prev=True, prev2=True):
                    for j in range(HG):
                        if cur:
                            exponentials(it, j, prev)
                        if j == 1 and prev2:
                            act.wait_ge(a.rb_psum, it - 1)
                            w = 2 if a.clip else 1
                            activation(rb[:, 0:w, :], bank[7][:, 0:w * T].rearrange("p (k t) -> p k t", k=w), ACT.Copy)\
                                .then_inc(a.rb_ready, 1)
                        if prev:
                            for k in a.evacuations[j]:
                                evacuate(it - 1, k, prev2)

                body(0, prev=False, prev2=False)
                for keys in asides[1:]:
                    square_jobs(keys)
                body(1, prev2=False)
                with act.Fori(2, H) as it:
                    body(it)
                body(H, cur=False)
                body(H + 1, cur=False, prev=False)

            def cross():
                square_jobs([("n1", 0), ("n1", 1), ("lat", 0)])
                for i in range(4):
                    odd, late = i % 2, i // 2
                    act.wait_ge(prep_psum, 3 + i)
                    activation(A_all[:, 8 * late + odd:8 * late + odd + 7:2, :], tiles(bank[2 + 2 * odd + late][:, :]),
                               ACT.Copy, scale=XD ** -0.5).then_inc(prep_act, 1)
                activation(A_all[:, XH:XH + 2, :], psum[:, 2:5:2, 0:P], ACT.Copy, scale=XD ** -0.5)\
                    .then_inc(prep_act, 1)
                for i in range(8):
                    c = i % 4
                    if i == 0:
                        square_jobs([("lat", 1)])
                    act.wait_ge(prep_psum, 7 + i)
                    if i < 4:
                        activation(ctxT[:, c * BANK:(c + 1) * BANK], bank[6 + c % 2][:, :], ACT.Copy).then_inc(prep_act, 1)
                    else:
                        affine(kvT[:, c, 0:S2], bank[6 + c % 2][:, :], col("b", "lnm_g"), col("b", "lnm_b"), prep_act)
                act.wait_ge(sx["zT_psum"], 1)
                affine(kvT[:, 0:2, S2:KEYS], bank[0][:, :].rearrange("p (b t) -> p b t", b=2), col("b", "lnl_g"),
                       col("b", "lnl_b"), sx["zT_act"])
                act.wait_ge(sx["q_psum"], 1)
                activation(xq_high[:, 0, :], bank[6][:, T:2 * T], ACT.Copy).then_inc(sx["q_high"], 1)
                act.wait_ge(prep_act, 13)
                act.wait_ge(sx["zT_act"], 1)
                for b in range(B):
                    if b == 2:
                        act.wait_ge(sx["zT_dve"], 1)
                    activation(kv_high[:, b, :], kvT[:, b, :], ACT.Copy).then_inc(sx["kv_high"], 1)

            def cross_units():
                def body(it, prev, cur):
                    for u in range(8):
                        n, b, odd = it * 8 + u, u // 2, u % 2
                        behind = (prev and u == 0) or (cur and u)
                        if cur:
                            if odd:
                                queries(n, u)
                            exponentials(it, n, u, 0, prev)
                        if behind:
                            evacuate(n - 1, (u - 1) % 8, 0)
                        if cur:
                            if not odd:
                                queries(n, u)
                            exponentials(it, n, u, 1, prev)
                        if behind:
                            evacuate(n - 1, (u - 1) % 8, 2)
                        if odd and (prev or u > 1):
                            act.wait_ge(sx["rb_psum"], it * 4 + b)
                            activation(xrb[:, :], bank[6][:, T:2 * T], ACT.Copy).then_inc(sx["rb_ready"], 1)
                        if not cur and u == 1:
                            break

                def queries(n, u):
                    act.wait_ge(sx["q_psum"], n + 2)
                    activation(xq_high[:, (u + 1) % 2, :], bank[6][:, T:2 * T], ACT.Copy).then_inc(sx["q_high"], 1)

                def evacuate(m, mu, c):
                    act.wait_ge(sx["pT_psum"], m * 3 + c + 1)
                    activation(xpT[:, (mu // 2) % 2, mu % 2, 2 * c * T:2 * (c + 1) * T], bank[4 + (3 * mu + c) % 2][:, :],
                               ACT.Copy).then_inc(sx["pT_act"], 1)

                def exponentials(it, n, u, half, prev):
                    act.wait_ge(sx["max_ready"], n * 2 + half + 1)
                    if half == 0 and (prev or u >= 2):
                        act.wait_ge(sx["pT_psum"], n * 3 - 3)
                    src = banks_pair(half)
                    activation(xprob[:, u % 2, half * KEYS:(half + 1) * KEYS].rearrange("p (c w) -> p c w", c=2), src,
                               ACT.Exp, bias=xnegmax[:, u % 2, half:half + 1],
                               accum_out=xsums[:, (u // 2) % 2, half, u % 2:u % 2 + 1]).then_inc(sx["exp_done"], 1)

                body(0, False, True)
                with act.Fori(1, XP) as it:
                    body(it, True, True)
                body(XP, True, False)

            def experts():
                ln2 = col("f", "ln2_g"), col("f", "ln2_b")
                square_jobs([("ln2", 0)])
                transposed(0, sf["zT_psum"], sf["zT_act"], *ln2)
                square_jobs([("ln2", 1)])
                b1 = col("f", "b1")

                def expert(e, prev):
                    for u in range(2 * FT):
                        n = e * (2 * FT) + u
                        if not prev and u == FT:
                            transposed(1, sf["zT_psum"], sf["zT_act"], *ln2)
                        if not prev and u == 2 * FT - 1:
                            act.wait_ge(sf["gate_shifted"], 1)
                            activation(gates[:, :, :], gates[:, :, :], ACT.Exp).then_inc(sf["gate_exp"], 1)
                        act.wait_ge(sf["hid_psum"], n + 1)
                        if prev and u % FT == 0:
                            act.wait_ge(sf["down_psum"], e * 2 + u // FT - 1)
                        activation(hid[:, u, :], bank[4 + u % 4][:, :], ACT.Gelu,
                                   bias=b1[:, bass.ds(e * 2 * FT + u, 1)]).then_inc(sf["gelu_done"], 1)

                expert(0, False)
                act.wait_ge(sf["routeT_psum"], 1)
                activation(routeT[0:E + 1, 0:BANK], bank[2][0:E + 1, :], ACT.Copy).then_inc(sf["routeT_ready"], 1)
                with act.Fori(1, E + 1) as e:
                    expert(e, True)

            def single():
                square_jobs([("n4", 0), ("n4", 1)])
                for c in range(4):
                    act.wait_ge(sg["proj_psum"], c + 1)
                    activation(kx[:, c * BANK:(c + 1) * BANK], bank[2 + c][:, :], ACT.Identity, bias=col("l", "bk4"))\
                        .then_inc(sg["proj_act"], 1)
                act.wait_ge(sg["zT_psum"], 1)
                activation(zT[:, 0:BANK], bank[0][:, :], ACT.Copy).then_inc(sg["zT_act"], 1)
                for n in range(NT + 1):
                    if n < NT:
                        act.wait_ge(sg["max_ready"], n + 1)
                        if n >= 2:
                            act.wait_ge(sg["pT_psum"], n - 1)
                        activation(px[:, n % 2, :], sm[:, n % 2, :], ACT.Exp, bias=nm1[:, n:n + 1],
                                   accum_out=sm1[:, n:n + 1]).then_inc(sg["exp_done"], 1)
                    if n:
                        m = n - 1
                        act.wait_ge(sg["pT_psum"], m + 1)
                        if m >= 2:
                            act.wait_ge(sg["out_psum"], m - 1)
                        activation(pxT[:, m % 2, :], bank[2 + m % 2][:, :], ACT.Copy).then_inc(sg["pT_ready"], 1)
                    if n == 6 and stages > 5:
                        square_jobs([("n5", 0)])

            def mixture():
                square_jobs([("n5", 1)])
                act.wait_ge(sl["zT_psum"], 1)
                activation(zT[:, 0:BANK], bank[0][:, :], ACT.Copy).then_inc(sl["zT_act"], 1)
                for c in range(2):
                    act.wait_ge(sl["low_psum"], c + 1)
                    activation(lowT[0:RU, c * BANK:(c + 1) * BANK], bank[2 + c][0:RU, :], ACT.Copy)\
                        .then_inc(sl["low_ready"], 1)
                act.wait_ge(sl["gate_shifted"], 1)
                activation(lp, lg, ACT.Exp).then_inc(sl["gate_exp"], 1)
                act.wait_ge(sl["routeT_psum"], 1)
                activation(lwT[0:E2 + 1, 0:BANK], bank[5][0:E2 + 1, :], ACT.Copy).then_inc(sl["routeT_ready"], 1)

            square_jobs(FIRST_JOBS)
            act.wait_ge(loaded["a"], 16)
            activation(identb[:, :], ident, ACT.Copy).then_inc(constants, 1)
            activation(causalb[:, :], col("a", "causal"), ACT.Copy).then_inc(constants, 1)
            act.wait_ge(constants, CONSTANTS)
            attention(att0, None, None, col("a", "bk0"), CONTEXT_JOBS)
            if stages > 1:
                cross()
                cross_units()
            if stages > 2:
                act.wait_ge(loaded["f"], 16)
                square_jobs([("n2", 0), ("ln1", 0)])
                attention(att1, col("f", "ln1_g"), col("f", "ln1_b"), col("f", "bk2"),
                          squares_between=([("n2", 1)], [("ln1", 1)]))
                experts()
            if stages > 3:
                act.wait_ge(loaded["l"], 16)
                square_jobs([("n3", 0)])
                attention(att2, None, None, col("l", "zero"), squares_between=([("n3", 1)], ()))
            if stages > 4:
                single()
            if stages > 5:
                mixture()

        @block.vector
        def _(dve):
            v = nc.vector
            chain = Chain(dve_chain)

            def link(instruction):
                chain.did(instruction)
                chain.wait(dve)

            def centre(keys):
                for key in keys:
                    k, src, _, (after, value) = jobs[key]
                    dve.wait_ge(after, value)
                    link(v.tensor_reduce(stat[:, k % 4, 0, :], src, AX.X, ALU.add))
                    v.scalar_tensor_tensor(centred[:, k % 4, :, :], spread(stat[:, k % 4, 0, :], D), -1.0 / D, src,
                                           ALU.mult, ALU.add).then_inc(centred_ready, 1)

            def variances(keys):
                for key in keys:
                    k = jobs[key][0]
                    dve.wait_ge(squared, k + 1)
                    v.tensor_reduce(stat[:, k % 4, 1, :], squares[:, k % 2, :, :], AX.X, ALU.add).then_inc(var_ready, 1)

            def scale(keys):
                for key in keys:
                    k, _, dst, _ = jobs[key]
                    dve.wait_ge(rstd_ready, k + 1)
                    v.tensor_tensor(dst, centred[:, k % 4, :, :], spread(stat[:, k % 4, 3, :], D), ALU.mult)\
                        .then_inc(normed, 1)

            def normalise(keys):
                centre(keys)
                variances(keys)
                scale(keys)

            def add_to_x(psum, h, bk, done=x_done):
                dve.wait_ge(psum, h + 1)
                v.tensor_tensor(quarter(x, h), quarter(x, h), tiles(bank[bk][:, :]), ALU.add).then_inc(done, 1)

            def effective_weights():
                dve.wait_ge(prep_psum, 1)
                v.scalar_tensor_tensor(weff[:, :], bank[0][:, 0:3 * D], 0.5, col("a", "w0"), ALU.mult, ALU.add)\
                    .then_inc(prep_dve, 1)

            def effective_projection():
                dve.wait_ge(loaded["b"], 16)
                dve.wait_ge(prep_psum, 2)
                v.scalar_tensor_tensor(wpeff[:, :], bank[7][:, :], 0.5, col("b", "wp0"), ALU.mult, ALU.add)\
                    .then_inc(prep_dve, 1)

            def attention(a, bias_q, bias_v, asides=None):
                def aside(place):
                    if asides:
                        for work, *arguments in asides[place]:
                            work(*arguments)

                link(v.memset(v_aug, 0.0))
                link(v.memset(v_aug.rearrange("p k (j r) -> p k j r", j=HG)[:, :, :, HD:HD + 1], 1.0))
                if a.clip:
                    link(v.memset(eraw, 0.0))
                    link(v.memset(pT.rearrange("p j (k t) -> p (j k) t", k=2)[:, :, T:T + 1], 1.0))
                for h in range(2):
                    dve.wait_ge(a.qkv_psum, 3 * h + 1)
                    v.tensor_scalar(qT[:, h * BANK:(h + 1) * BANK], bank[2 + h][:, :], bias_q, HD ** -0.5,
                                    ALU.add, ALU.mult).then_inc(a.qv_ready, 1)
                    aside(h)
                    dve.wait_ge(a.qkv_psum, 3 * h + 3)
                    v.tensor_tensor(quarter(v_tok, h), tiles(bank[6 + h][:, :]),
                                    bias_v.unsqueeze(1).broadcast_to([P, 4, D]), ALU.add).then_inc(a.qv_ready, 1)
                    if h == 0:
                        aside(3)
                v.memset(vsum, 0.0).then_inc(a.y_done, 1)
                dve.wait_ge(a.qv_ready, 4)

                def maxima(it, j):
                    dve.wait_ge(a.score_psum, it * HG + j + 1)
                    if a.causal:
                        last = v.tensor_reduce(negmax[:, j, 0:1], bank[j][:, 0:P], AX.X, ALU.max, negate=True)
                        if a.clip:
                            chain.did(last)
                        last = v.tensor_reduce(negmax[:, j, 1:2], bank[j][:, T:2 * T], AX.X, ALU.max, negate=True)
                    else:
                        last = v.tensor_reduce(negmax[:, j, :], bank[j][:, :].rearrange("p (u k) -> p u k", u=2), AX.X,
                                               ALU.max, negate=True)
                    if a.clip:
                        chain.did(last)
                    else:
                        last.then_inc(a.max_ready, 1)

                def clipped_maxima(j):
                    chain.wait(dve)
                    v.tensor_scalar(negmax[:, j, :], negmax[:, j, :], -CLIP, CLIP, ALU.max, ALU.min)\
                        .then_inc(a.max_ready, 1)

                def clipped(it, j, u, prev):
                    if u == 0:
                        dve.wait_ge(a.exp_done, it * HG + j + 1)
                        if prev:
                            dve.wait_ge(a.pT_psum, it * HG + j - 3)
                    v.scalar_tensor_tensor(prob[:, j, u, :], eraw[:, j, u, :], low[:, j, u:u + 1], ones[:, :], ALU.max,
                                           ALU.min, accum_out=sums[:, it, u * HG + j:u * HG + j + 1])\
                        .then_inc(a.clip_done, 1)

                def evacuate(it, j, prev):
                    if j in a.dve_heads:
                        dve.wait_ge(a.pT_psum, it * HG + j + 1)
                        if j == 0 and prev:
                            dve.wait_ge(a.y_psum, it)
                        v.tensor_copy(a.pT_of(j), a.pT_from(j)).then_inc(a.pT_dve, 1)

                r, t, den, w = small[:, 0, :], small[:, 1, :], small[:, 2, :], small[:, 3, :]

                def over_rows(k, factor):
                    return v.tensor_copy(rbc[:, k, :, :].rearrange("p u (j r) -> p (u j) r", j=HG), spread(factor, ROWS))

                def factors(it):
                    dve.wait_ge(a.exp_done, it * HG + HG)
                    link(v.reciprocal(r, sums[:, it, :]))
                    over_rows(0, r).then_inc(a.rbc_ready, 1)

                def floored_factors(it, step):
                    if step == 0:
                        dve.wait_ge(a.clip_done, (it * HG + HG) * 2)
                        chain.did(v.tensor_scalar(t, sums[:, it, :], FLOOR, FLOOR * TINY, ALU.mult, ALU.add))
                    else:
                        chain.wait(dve)
                    if step == 1:
                        chain.did(v.scalar_tensor_tensor(den, t, float(T), sums[:, it, :], ALU.mult, ALU.add))
                    if step == 2:
                        chain.did(v.reciprocal(r, den))
                    if step == 3:
                        chain.did(v.tensor_tensor(w, t, r, ALU.mult))
                    if step == 4:
                        chain.did(over_rows(1, w))
                        over_rows(0, r).then_inc(a.rbc_ready, 1)

                def values(it, b, g):
                    v.tensor_copy(v_aug.rearrange("p k (j r) -> p k j r", j=HG)[:, :, :, 0:HD],
                                  v_tok[:, bass.ds(b * 2, 2), bass.ds(g * HG * HD, HG * HD)]
                                  .rearrange("p k (j r) -> p k j r", j=HG)).then_inc(a.v_aug_ready, 1)

                def results(group, b, g):
                    dve.wait_ge(a.rb_ready, group + 1)
                    out = yT[:, g, bass.ds(b * T, T)]
                    if a.clip:
                        chain.did(v.tensor_copy(vsum, bank[6][:, T:T + 1]))
                        link(v.tensor_tensor(ytmp, bank[6][:, 0:T], rb[:, 0, :], ALU.mult))
                        v.scalar_tensor_tensor(out, rb[:, 1, :], vsum, ytmp, ALU.mult, ALU.add).then_inc(a.y_done, 1)
                    else:
                        v.tensor_tensor(out, bank[6][:, 0:T], rb[:, 0, :], ALU.mult).then_inc(a.y_done, 1)

                def body(it, cur=True, prev=True, prev2=True):
                    for j in range(HG):
                        if cur:
                            maxima(it, j)
                        if a.clip:
                            behind = (it - 1, HG - 1, prev) if j == 0 else (it, j - 1, cur)
                            if j in (1, 2) and prev:
                                floored_factors(it - 1, 2 * j - 2)
                            if behind[2]:
                                clipped(behind[0], behind[1], 0, prev)
                            if cur:
                                clipped_maxima(j)
                            if behind[2]:
                                clipped(behind[0], behind[1], 1, prev)
                            if j in (1, 2) and prev:
                                floored_factors(it - 1, 2 * j - 1)
                        if prev:
                            for k in a.evacuations[j]:
                                evacuate(it - 1, k, prev2)
                        if j == 2 and prev2:
                            results(it - 2, (it - 2) // G, (it - 2) % G)
                        if prev:
                            if j == 2:
                                values(it - 1, (it - 1) // G, (it - 1) % G)
                                if not a.clip:
                                    factors(it - 1)
                            if j == 3 and a.clip:
                                floored_factors(it - 1, 4)

                body(0, prev=False, prev2=False)
                aside(2)
                body(1, prev2=False)
                each = 2 * HG + 5 + 2 if a.clip else 1
                with dve.Fori(2, H) as it:
                    chain.enter(it, 2, each)
                    body(it)
                    chain.leave(H - 2)
                body(H, cur=False)
                body(H + 1, cur=False, prev=False)

            def cross_latents():
                dve.wait_ge(sx["zT_psum"], 2)
                v.tensor_scalar(kvT[:, 2:4, S2:KEYS], bank[1][:, :].rearrange("p (b t) -> p b t", b=2),
                                col("b", "lnl_g"), col("b", "lnl_b"), ALU.mult, ALU.add).then_inc(sx["zT_dve"], 1)

            def cross_units():
                W3 = 3 * P

                def query_low(count, slot):
                    dve.wait_ge(sx["q_high"], count)
                    v.tensor_tensor(xq_low[:, slot, :], bank[6][:, T:2 * T], xq_high[:, slot, :].bitcast(f32), ALU.subtract)\
                        .then_inc(sx["q_ready"], 1)

                def key_low(b):
                    dve.wait_ge(sx["kv_high"], b + 1)
                    v.tensor_tensor(kv_low[:, b, :], kvT[:, b, :], kv_high[:, b, :].bitcast(f32), ALU.subtract)\
                        .then_inc(sx["kv_split"], 1)

                def maxima(n, u, half):
                    dve.wait_ge(sx["score_psum"], n * 2 + half + 1)
                    v.tensor_reduce(xnegmax[:, u % 2, half:half + 1], banks_pair(half), AX.XY, ALU.max, negate=True)\
                        .then_inc(sx["max_ready"], 1)

                def values(count, b, half):
                    dve.wait_ge(sx["v_psum"], count)
                    v.tensor_copy(xv[:, b, half * W3:(half + 1) * W3], bank[7][:, 0:W3]).then_inc(sx["v_ready"], 1)

                def results(p, hp, b):
                    dve.wait_ge(sx["rb_ready"], p + 1)
                    v.tensor_tensor(oT[:, hp, b * T:(b + 1) * T], bank[6][:, 0:T], xrb[:, :], ALU.mult)\
                        .then_inc(sx["y_done"], 1)

                def body(it, prev, cur):
                    for u in range(8):
                        n, b, odd = it * 8 + u, u // 2, u % 2
                        if cur:
                            maxima(n, u, 0)
                            if odd:
                                query_low(n + 2, (u + 1) % 2)
                            values(n + 3, (b + 1) % 4, odd)
                        if not odd and (prev or u >= 4):
                            results(it * 4 + b - 2, it - (u < 4), (b - 2) % 4)
                        if (prev and u == 0) or (cur and u):
                            m, mu = n - 1, (u - 1) % 8
                            dve.wait_ge(sx["pT_psum"], m * 3 + 2)
                            v.tensor_copy(xpT[:, (mu // 2) % 2, mu % 2, 2 * T:4 * T], bank[4 + (3 * mu + 1) % 2][:, :])\
                                .then_inc(sx["pT_dve"], 1)
                        if not odd and ((prev and u == 0) or (cur and u)):
                            dve.wait_ge(sx["exp_done"], n * 2)
                            link(v.reciprocal(xr[:, :], xsums[:, ((u - 2) % 8 // 2) % 2, :, :].rearrange("p h a -> p (h a)")))
                            v.tensor_copy(xrbc[:, :, :].rearrange("p h (a r) -> p (h a) r", a=2), spread(xr[:, :], XD))\
                                .then_inc(sx["rbc_ready"], 1)
                        if cur:
                            if not odd:
                                query_low(n + 2, (u + 1) % 2)
                            maxima(n, u, 1)
                        if not cur and u == 2:
                            break

                v.memset(xrb[:, 0:1], 0.0).then_inc(sx["y_done"], 1)
                query_low(1, 0)
                values(1, 0, 0)
                values(2, 0, 1)
                for b in range(B):
                    key_low(b)
                body(0, False, True)
                with dve.Fori(1, XP) as it:
                    chain.enter(it, 1, 4)
                    body(it, True, True)
                    chain.leave(XP - 1)
                body(XP, True, False)

            def top(src, out, value, key, shape_e, ramp):
                link(v.tensor_reduce(value, src, AX.X, ALU.max))
                link(v.tensor_tensor(out, src, spread(value, shape_e), ALU.is_equal))
                link(v.tensor_tensor(out, out, ramp.unsqueeze(1).broadcast_to([P, NT, shape_e]), ALU.mult))
                link(v.tensor_reduce(key, out, AX.X, ALU.max))
                link(v.tensor_tensor(out, out, spread(key, shape_e), ALU.is_equal))

            def experts():
                for h in range(2):
                    dve.wait_ge(att1.out_psum, h + 1)
                    v.tensor_tensor(quarter(xin, h), quarter(z, h), tiles(bank[h][:, :]), ALU.add)\
                        .then_inc(sf["xin_ready"], 1)
                    normalise([("ln2", h)])
                link(v.tensor_tensor(x[:, :, :], x[:, :, :], xin, ALU.add))
                dve.wait_ge(sf["gate_psum"], 1)
                link(v.tensor_copy(gates, bank[2][:, 0:NT * (E + 2)].rearrange("p (t e) -> p t e", t=NT)))
                ge, gc = gates[:, :, 0:E], gates[:, :, E:E + 2]
                link(v.tensor_tensor(gc, gc, col("f", "coef_b").unsqueeze(1).broadcast_to([P, NT, 2]), ALU.add))
                link(v.tensor_reduce(g1[:, 0, :], ge, AX.X, ALU.max))
                link(v.tensor_reduce(g1[:, 1, :], gc, AX.X, ALU.max))
                link(v.tensor_tensor(ge, ge, spread(g1[:, 0, :], E), ALU.subtract))
                v.tensor_tensor(gc, gc, spread(g1[:, 1, :], 2), ALU.subtract).then_inc(sf["gate_shifted"], 1)
                dve.wait_ge(sf["gate_exp"], 1)
                link(v.tensor_reduce(g1[:, 2, :], ge, AX.X, ALU.add))
                link(v.tensor_reduce(g1[:, 3, :], gc, AX.X, ALU.add))
                link(v.reciprocal(g1[:, 2:4, :], g1[:, 2:4, :]))
                link(v.tensor_tensor(probs, ge, spread(g1[:, 2, :], E), ALU.mult))
                link(v.tensor_tensor(coef, gc, spread(g1[:, 3, :], 2), ALU.mult))
                top(probs, pick, g1[:, 4, :], g1[:, 5, :], E, col("f", "ramp"))
                link(v.tensor_tensor(g1[:, 6, :], g1[:, 4, :], coef[:, :, 0:1].rearrange("p t a -> p (t a)"), ALU.mult))
                link(v.tensor_tensor(route[:, :, 0:E], pick, spread(g1[:, 6, :], E), ALU.mult))
                v.tensor_copy(route[:, :, E:E + 1], coef[:, :, 1:2]).then_inc(sf["route_ready"], 1)
                dve.wait_ge(sf["routeT_psum"], 1)
                v.tensor_copy(routeT[0:E + 1, BANK:2 * BANK], bank[3][0:E + 1, :]).then_inc(sf["routeT_ready"], 1)
                for h in range(2):
                    dve.wait_ge(sf["bias_psum"], h + 1)
                    v.tensor_tensor(quarter(x, h), quarter(x, h), tiles(bank[2 + h][:, :]), ALU.add)\
                        .then_inc(sf["mixed"], 1)

                def expert(e, slot, last=False):
                    for c in range(2):
                        dve.wait_ge(sf["down_psum"], e * 2 + c + 1)
                        dve.wait_ge(sf["mixed"], e * 2 + c + 1)
                        for t in range(4 * c, 4 * c + 4):
                            done = v.scalar_tensor_tensor(x[:, t, :], bank[2 * slot + c][:, (t % 4) * P:(t % 4 + 1) * P],
                                                          route[:, t, bass.ds(e, 1)], x[:, t, :], ALU.mult, ALU.add)
                        done.then_inc(x_done if last else sf["mixed"], 1)
                        if last and stages > 3:
                            normalise([("n3", c)])

                expert(0, 0)
                with dve.Fori(0, E // 2 - 1) as i:
                    for k in range(2):
                        expert(i * 2 + k + 1, 1 - k)
                expert(E - 1, 1)
                expert(E, 0, last=True)

            def single():
                for c in range(4):
                    dve.wait_ge(sg["proj_psum"], 5 + c)
                    v.tensor_tensor(quarter(vx, c), tiles(bank[(6, 7, 2, 3)[c]][:, :]),
                                    col("l", "bv4").unsqueeze(1).broadcast_to([P, 4, D]), ALU.add)\
                        .then_inc(sg["proj_dve"], 1)
                dve.wait_ge(sg["zT_psum"], 2)
                v.tensor_copy(zT[:, BANK:2 * BANK], bank[1][:, :]).then_inc(sg["zT_dve"], 1)
                for c in range(2):
                    dve.wait_ge(sg["proj_psum"], 9 + c)
                    v.tensor_scalar(qx[:, c * BANK:(c + 1) * BANK], bank[4 + c][:, :], col("l", "bq4"), D ** -0.5,
                                    ALU.add, ALU.mult).then_inc(sg["proj_dve"], 1)
                dve.wait_ge(loaded["mask"], 16)
                for n in range(NT + 2):
                    if n < NT:
                        dve.wait_ge(sg["score_psum"], n + 1)
                        if n >= 2:
                            dve.wait_ge(sg["exp_done"], n - 1)
                        link(v.tensor_tensor(sm[:, n % 2, :], bank[n % 2][:, :], maskx[:, n % 2, :], ALU.add))
                        v.tensor_reduce(nm1[:, n:n + 1], sm[:, n % 2, :], AX.X, ALU.max, negate=True)\
                            .then_inc(sg["max_ready"], 1)
                    if n >= 2:
                        m = n - 2
                        link(v.reciprocal(r1[:, m:m + 1], sm1[:, m:m + 1]))
                        dve.wait_ge(sg["out_psum"], m + 1)
                        last = v.scalar_tensor_tensor(x[:, m, :], bank[4 + m % 2][:, 0:D], r1[:, m:m + 1], x[:, m, :],
                                                      ALU.mult, ALU.add)
                        last.then_inc(x_parts, 1)
                        if m % 4 == 3:
                            dve.wait_ge(x_parts, m + 1)
                            dve.sem_inc(x_done, 1)
                    if stages > 5 and n >= 6 and n < 9:
                        (centre, variances, scale)[n - 6]([("n5", 0)])

            def mixture():
                normalise([("n5", 1)])
                dve.wait_ge(sl["zT_psum"], 2)
                v.tensor_copy(zT[:, BANK:2 * BANK], bank[1][:, :]).then_inc(sl["zT_dve"], 1)
                dve.wait_ge(sl["gate_psum"], 1)
                link(v.tensor_tensor(lg, bank[4][:, 0:NT * E2].rearrange("p (t e) -> p t e", t=NT),
                                     col("l", "router_b").unsqueeze(1).broadcast_to([P, NT, E2]), ALU.add))
                link(v.tensor_reduce(l1[:, 0, :], lg, AX.X, ALU.max))
                v.tensor_tensor(lg, lg, spread(l1[:, 0, :], E2), ALU.subtract).then_inc(sl["gate_shifted"], 1)
                for h in range(2):
                    add_to_x(sl["base_psum"], h, h, sl["base_added"])
                dve.wait_ge(sl["gate_exp"], 1)
                link(v.tensor_reduce(l1[:, 1, :], lp, AX.X, ALU.add))
                link(v.reciprocal(l1[:, 1, :], l1[:, 1, :]))
                link(v.tensor_tensor(lp, lp, spread(l1[:, 1, :], E2), ALU.mult))
                ramp = col("f", "ramp")[:, 0:E2]
                top(lp, lpick, l1[:, 2, :], l1[:, 3, :], E2, ramp)
                link(v.scalar_tensor_tensor(lg, lpick, -2.0, lp, ALU.mult, ALU.add))
                top(lg, lsel, l1[:, 4, :], l1[:, 5, :], E2, ramp)
                link(v.tensor_tensor(lsel, lsel, lpick, ALU.add))
                link(v.tensor_tensor(lsel, lsel, lp, ALU.mult))
                link(v.tensor_reduce(l1[:, 6, :], lsel, AX.X, ALU.add))
                link(v.tensor_scalar(l1[:, 6, :], l1[:, 6, :], TINY, None, ALU.add))
                link(v.reciprocal(l1[:, 6, :], l1[:, 6, :]))
                link(v.memset(lw[:, :, 0:1], 1.0))
                v.tensor_tensor(lw[:, :, 1:E2 + 1], lsel, spread(l1[:, 6, :], E2), ALU.mult).then_inc(sl["route_ready"], 1)
                dve.wait_ge(sl["routeT_psum"], 1)
                v.tensor_copy(lwT[0:E2 + 1, BANK:2 * BANK], bank[6][0:E2 + 1, :]).then_inc(sl["routeT_ready"], 1)
                dve.wait_ge(sl["low_ready"], 2)
                for c in range(2):
                    dve.wait_ge(sl["wide_psum"], c + 1)
                    v.tensor_tensor(lowTm[0:RU, c * BANK:(c + 1) * BANK], lowT[0:RU, c * BANK:(c + 1) * BANK],
                                    bank[4 + 3 * c][0:RU, :], ALU.mult).then_inc(sl["mixed"], 1)
                dve.wait_ge(sl["base_added"], 2)
                for h in range(2):
                    add_to_x(sl["out_psum"], h, 2 + h)

            v.memset(ones[:, :], 1.0).then_inc(constants, 1)
            v.memset(low_bias[:, :], -CLIP).then_inc(constants, 1)
            centre(FIRST_JOBS)
            variances(FIRST_JOBS)
            dve.wait_ge(loaded["a"], 16)
            effective_weights()
            scale(FIRST_JOBS)
            attention(att0, col("a", "bq0"), col("a", "bv0"),
                      [[(effective_projection,), (centre, CONTEXT_JOBS[0])], [(variances, CONTEXT_JOBS[0])],
                       [(scale, CONTEXT_JOBS[0]), (centre, CONTEXT_JOBS[1]), (variances, CONTEXT_JOBS[1])], []])
            scale(CONTEXT_JOBS[1])
            add_to_x(att0.out_psum, 0, 0)
            if stages > 1:
                centre([("n1", 0)])
                variances([("n1", 0)])
            add_to_x(att0.out_psum, 1, 1)
            if stages > 1:
                centre([("n1", 1)])
                scale([("n1", 0)])
                centre([("lat", 0)])
                variances([("n1", 1)])
                scale([("n1", 1)])
                variances([("lat", 0)])
                centre([("lat", 1)])
                scale([("lat", 0)])
                variances([("lat", 1)])
                scale([("lat", 1)])
                cross_latents()
                cross_units()
                for h in range(2):
                    add_to_x(sx["out_psum"], h, h)
                    if stages > 2:
                        normalise([("n2", h)])
                        if h == 0:
                            normalise([("ln1", 0)])
            if stages > 2:
                dve.wait_ge(loaded["f"], 16)
                attention(att1, col("f", "bq2"), col("f", "bv2"), [[], [], [], [(normalise, [("ln1", 1)])]])
                experts()
            if stages > 3:
                dve.wait_ge(loaded["l"], 16)
                attention(att2, col("l", "zero"), col("l", "zeros"))
                for h in range(2):
                    add_to_x(att2.out_psum, h, h)
                    if stages > 4:
                        normalise([("n4", h)])
            if stages > 4:
                single()
            if stages > 5:
                mixture()

        @block.gpsimd
        def _(pool):
            done = [0]

            def link(instruction):
                instruction.then_inc(pool_chain, 1)
                done[0] += 1
                pool.wait_ge(pool_chain, done[0])

            def rstd_jobs(keys):
                for key in keys:
                    k = jobs[key][0]
                    pool.wait_ge(var_ready, k + 1)
                    link(pool.tensor_scalar(stat[:, k % 4, 2, :], stat[:, k % 4, 1, :], 1.0 / D, EPS, ALU.mult, ALU.add))
                    pool.tensor_tensor(stat[:, k % 4, 3, :], stat[:, k % 4, 2, :], half[:, :], ALU.pow)\
                        .then_inc(rstd_ready, 1)

            def attention(a, asides=((), ())):
                pool.wait_ge(a.qv_ready, 1)
                headmask = col("a", "headmask")

                def body(it, b, g, prev):
                    for j in range(HG):
                        if prev:
                            pool.wait_ge(a.score_psum, it * HG + j - 3)
                        pool.tensor_tensor(qm[:, j, :], qT[:, bass.ds(b * T, T)],
                                           headmask[:, bass.ds(g * HG + j, 1)].broadcast_to([P, T]), ALU.mult)\
                            .then_inc(a.qm_ready, 1)

                body(0, 0, 0, False)
                rstd_jobs(asides[0])
                body(1, 0, 1, True)
                rstd_jobs(asides[1])
                pool.wait_ge(a.qv_ready, 3)
                with pool.Fori(2, H) as it:
                    body(it, it // G, it % G, True)

            def cross():
                def pair(it, prev):
                    for u in range(2):
                        if prev:
                            pool.wait_ge(sx["q_psum"], it * 8 - 1 + u)
                        pool.tensor_copy(acur[:, u, :], A_flat[:, bass.ds(it * 2 * P + u * P, P)])\
                            .then_inc(sx["acur_ready"], 1)

                pool.wait_ge(prep_act, 5)
                pair(0, False)
                with pool.Fori(1, XP + 1) as it:
                    pair(it, True)

            pool.memset(half[:, :], -0.5).then_inc(pool_chain, 1)
            done[0] += 1
            pool.wait_ge(pool_chain, 1)
            rstd_jobs(FIRST_JOBS)
            pool.wait_ge(loaded["a"], 16)
            attention(att0, CONTEXT_JOBS)
            if stages > 1:
                rstd_jobs([("n1", 0), ("n1", 1), ("lat", 0), ("lat", 1)])
                cross()
            if stages > 2:
                rstd_jobs([("n2", 0), ("ln1", 0), ("n2", 1), ("ln1", 1)])
                attention(att1)
                rstd_jobs([("ln2", 0), ("ln2", 1)])
            if stages > 3:
                rstd_jobs([("n3", 0), ("n3", 1)])
                attention(att2)
            if stages > 4:
                rstd_jobs([("n4", 0), ("n4", 1)])
            if stages > 5:
                rstd_jobs([("n5", 0), ("n5", 1)])


def _arrange(inputs):
    f = lambda n: np.asarray(inputs[n])

    def rows(a, n=P):
        out = np.zeros((n,) + a.shape[1:], np.float32)
        out[:a.shape[0]] = a
        return out

    def column(v):
        return np.ascontiguousarray(v).reshape(-1, 1)

    def repeated(v):
        return np.broadcast_to(v.reshape(1, -1), (P, v.size))

    def grouped(w, bias=None):
        out = np.zeros((HG, ROWS, G, w.shape[1]), np.float32)
        out[:, :HD] = w.reshape(G, HG, HD, -1).transpose(1, 2, 0, 3)
        if bias is not None:
            out[0, HD, 0] = bias
        return out.reshape(P, G * w.shape[1])

    qkv = f("L0_attn_b_attn").reshape(3, D)
    b2 = f("L0_ffn_bqkv").reshape(3, D)
    wx = f("L0_xattn_Wkv")
    wv = np.concatenate([wx[:, XH * XD:], wx[:, XH * XD:XH * XD + P]], 1)

    def pairs(w):
        return np.ascontiguousarray(w.T).reshape(XP, P, D).transpose(1, 0, 2).reshape(P, XP * D)

    low_rows = np.concatenate([f("L1_ffn_shared_A")[None], f("L1_ffn_routed_A")]).reshape(RU, D)
    low_cols = np.concatenate([f("L1_ffn_shared_B").T[None], f("L1_ffn_routed_B").transpose(0, 2, 1)]).reshape(RU, D)
    c = {
        "ident": np.eye(P, dtype=np.float32),
        "headmask": (np.arange(P)[:, None] // HD == np.arange(H)[None]).astype(np.float32),
        "causal": np.where(np.arange(P)[None] <= np.arange(P)[:, None], 0.0, MASKED).astype(np.float32),
        "la0": rows(f("L0_attn_la_attn")), "lb0": rows(f("L0_attn_lb_attn").T), "w0": f("L0_attn_w_attn").T,
        "bq0": column(qkv[0]), "bk0": column(qkv[1]), "bv0": repeated(qkv[2]),
        "lap0": rows(grouped(f("L0_attn_la_proj").T).reshape(P, G, RL).transpose(2, 1, 0).reshape(RL, G * P)),
        "lbp0": rows(f("L0_attn_lb_proj").T), "wp0": grouped(f("L0_attn_w_proj").T, f("L0_attn_b_proj")),
        "lnm_g": column(f("L0_xattn_ln_m_g")), "lnm_b": column(f("L0_xattn_ln_m_b")),
        "lnl_g": column(f("L0_xattn_ln_l_g")), "lnl_b": column(f("L0_xattn_ln_l_b")),
        "wqT": pairs(f("L0_xattn_Wq")), "wkT": pairs(wx[:, :XH * XD]), "wv": wv,
        "wout": f("L0_xattn_Wout").reshape(XP, P, D).transpose(1, 0, 2).reshape(P, XP * D),
        "ln1_g": column(f("L0_ffn_ln1_g")), "ln1_b": column(f("L0_ffn_ln1_b")), "w2": f("L0_ffn_Wqkv"),
        "bq2": column(b2[0]), "bk2": column(b2[1]), "bv2": repeated(b2[2]),
        "wp2": grouped(f("L0_ffn_Wo"), f("L0_ffn_bo")),
        "ln2_g": column(f("L0_ffn_ln2_g")), "ln2_b": column(f("L0_ffn_ln2_b")),
        "gate": np.concatenate([f("L0_ffn_gate_w"), f("L0_ffn_coef_w")], 1), "coef_b": repeated(f("L0_ffn_coef_b")),
        "ramp": np.broadcast_to(np.arange(E, 0, -1, dtype=np.float32), (P, E)),
        "b1": np.concatenate([f("L0_ffn_b1"), f("L0_ffn_rb1")[None]]).reshape(E + 1, 1, FT, P).repeat(2, 1)
        .reshape((E + 1) * 2 * FT, P).T,
        "b2": rows(np.concatenate([f("L0_ffn_b2"), f("L0_ffn_rb2")[None]])),
        "w3": f("L1_attn_w_qkv").T, "zero": np.zeros((P, 1), np.float32), "zeros": np.zeros((P, D), np.float32),
        "wp3": grouped(f("L1_attn_w_proj").T),
        "wq4": f("L1_xattn_kernel_q"), "wk4": f("L1_xattn_kernel_k"), "wv4": f("L1_xattn_kernel_v"),
        "bq4": column(f("L1_xattn_bias_q")), "bk4": column(f("L1_xattn_bias_k")), "bv4": repeated(f("L1_xattn_bias_v")),
        "base": f("L1_ffn_base_W").T, "lowA": low_rows.T, "lowB": rows(low_cols),
        "base_b": rows(f("L1_ffn_base_b").reshape(1, D)), "router": f("L1_ffn_router_W").T,
        "router_b": repeated(f("L1_ffn_router_b")),
        "sel7": rows((np.arange(E2 + 1)[:, None] == np.arange(RU)[None] // R2).astype(np.float32)),
    }
    arrays = {f"pack_{key}": np.concatenate([c[n] for n, _ in columns], 1) for key, columns in LAYOUT.items()}
    arrays["x"] = f("x")
    arrays["ctx"] = f("ctx_1024")
    arrays["mask"] = f("mask_1xSxS2_ff0")
    arrays["w1"] = np.concatenate([f("L0_ffn_W1"), f("L0_ffn_rW1")[None]])
    arrays["w2"] = np.concatenate([f("L0_ffn_W2"), f("L0_ffn_rW2")[None]]).reshape(E + 1, FT, P, D)\
        .transpose(0, 2, 1, 3).reshape(E + 1, P, FT * D)
    return arrays


def kernel(**inputs):
    import concourse.bacc as _bacc
    from concourse.bass_utils import run_bass_kernel_spmd as _run

    nc = _bacc.Bacc("TRN2", target_bir_lowering=False, num_devices=1)
    arrays = {f"in_{n}": np.ascontiguousarray(a) for n, a in _arrange(inputs).items()}
    d = {n[3:]: nc.dram_tensor(n, a.shape, mybir.dt.from_np(a.dtype), kind="ExternalInput").ap() for n, a in arrays.items()}
    out = nc.dram_tensor("out", (B, T, D), mybir.dt.float32, kind="ExternalOutput").ap()
    decoder(nc, d["x"], d["ctx"], d["mask"], {k: d[f"pack_{k}"] for k in LAYOUT}, d["w1"], d["w2"], out)
    return _run(nc, [arrays], core_ids=[0]).results[0]["out"]
```

```python
from contextlib import ExitStack

import numpy as np
import concourse.bass as bass
from concourse import mybir

P = 128
D = 128
B = 4
T = 256
S2 = 512
NT = B * T // P
NC = B * S2 // P
BANK = 512
EPS = 1e-5
BLOCKS = 6

H = 16
HD = D // H
G = 4
HG = H // G
ROWS = P // HG

XH = 16
XD = 64
XP = XH // 2
KEYS = S2 + T
KT = KEYS // P

E = 8
F = 512
FT = F // P
E2 = 6
R2 = 16
RU = (E2 + 1) * R2
RL = 32
MASKED = -1e30
CLIP = 100.0
TINY = 1e-6
FLOOR = 1e-8

LAYOUT = {
    "a": [("ident", P), ("headmask", H), ("causal", P), ("la0", D), ("lb0", 3 * D), ("w0", 3 * D),
          ("bq0", 1), ("bk0", 1), ("bv0", D)],
    "b": [("lap0", G * P), ("lbp0", D), ("wp0", G * D), ("lnm_g", 1), ("lnm_b", 1), ("lnl_g", 1), ("lnl_b", 1)],
    "q": [("wqT", XP * D), ("wkT", XP * D)],
    "v": [("wv", (XP + 1) * P), ("wout", XP * D)],
    "f": [("ln1_g", 1), ("ln1_b", 1), ("w2", 3 * D), ("bq2", 1), ("bk2", 1), ("bv2", D), ("wp2", G * D),
          ("ln2_g", 1), ("ln2_b", 1), ("gate", E + 2), ("coef_b", 2), ("ramp", E),
          ("b1", (E + 1) * 2 * FT), ("b2", D)],
    "l": [("w3", 3 * D), ("zero", 1), ("zeros", D), ("wp3", G * D), ("wq4", D), ("wk4", D), ("wv4", D), ("bq4", 1), ("bk4", 1),
          ("bv4", D), ("base", D), ("lowA", RU), ("lowB", D), ("base_b", D), ("router", E2), ("router_b", E2),
          ("sel7", RU)],
}


class Chain:

    def __init__(self, sem):
        self.sem, self.base, self.n = sem, 0, 0

    def did(self, instruction):
        instruction.then_inc(self.sem, 1)
        self.n += 1

    def wait(self, engine):
        engine.wait_ge(self.sem, self.base + self.n)

    def enter(self, iteration, first, each):
        self.start = self.n
        self.base, self.n, self.each = iteration * each + (self.start - first * each), 0, each

    def leave(self, iterations):
        assert self.n == self.each, (self.n, self.each)
        self.base, self.n = 0, self.start + iterations * self.each


def decoder(nc, x_d, ctx_d, mask_d, packs_d, w1_d, w2_d, out_d):
    f32, f32r, bf16 = mybir.dt.float32, mybir.dt.float32r, mybir.dt.bfloat16
    ALU, ACT, AX = mybir.AluOpType, mybir.ActivationFunctionType, mybir.AxisListType

    ctx = ExitStack()
    with ctx:
        def sb(name, shape, dt=f32):
            return ctx.enter_context(nc.sbuf_tensor(name, shape, dt))

        def sem(name):
            return ctx.enter_context(nc.semaphore(name))

        x = sb("x", [P, NT, D])
        z = sb("z", [P, NT, D])
        z2 = sb("z2", [P, NT, D])
        zT = sb("zT", [P, NT * P])
        with nc.sbuf_tensor("ctx_x", [P, NC, D], f32) as ctx_x, nc.sbuf_tensor("ctx_z", [P, NC, D], f32) as ctx_z, \
                nc.sbuf_tensor("centred", [P, 4, 4, D], f32) as centred, \
                nc.sbuf_tensor("squares", [P, 2, 4, D], f32) as squares:
            pass
        kv_high = sb("kv_high", [P, B, KEYS], f32r)
        kv_low = sb("kv_low", [P, B, KEYS], f32r)
        sb("behind_kv_low", [P, 2 * NC * D + 6 * 4 * D - 2 * B * KEYS])
        stat = sb("stat", [P, 4, 4, 4])
        half = sb("half", [P, 4])
        ctxT = sb("ctxT", [P, NC * P])
        with nc.sbuf_tensor("kvT", [P, B, KEYS], f32) as kvT, nc.sbuf_tensor("xv", [P, B, KT * P], f32) as xv:
            pass
        z_high, z_low = sb("z_high", [P, NT * P], f32r), sb("z_low", [P, NT * P], f32r)
        w1_high, w1_low = sb("w1_high", [P, 2, F], f32r), sb("w1_low", [P, 2, F], f32r)
        sb("behind_w1_low", [P, 2 * B * KEYS - 2 * NT * P - 4 * F])
        packs = {key: sb(f"pack_{key}", [P, sum(w for _, w in columns)]) for key, columns in LAYOUT.items()}
        identb = sb("identb", [P, P], bf16)
        causalb = sb("causalb", [P, P], bf16)
        ones = sb("ones_", [P, T])
        A_all = sb("A_all", [P, XH + 2, P])
        A_flat = A_all[:, :, :].rearrange("p h c -> p (h c)")
        low_bias = sb("low_bias", [P, 1])
        weff = sb("weff", [P, 3 * D])
        wpeff = sb("wpeff", [P, G * D])

        ARENA = 17920
        arena = sb("arena", [P, ARENA])

        class Area:
            def __init__(self):
                self.at = 0

            def __call__(self, *dims):
                n = int(np.prod(dims))
                view = arena[:, self.at:self.at + n]
                self.at += n
                assert self.at <= ARENA, self.at
                if len(dims) == 2:
                    return view.rearrange("p (a b) -> p a b", a=dims[0])
                if len(dims) == 3:
                    return view.rearrange("p (a b c) -> p a b c", a=dims[0], b=dims[1])
                return view

        area = Area()
        qT, kT = area(NT * P), area(NT * P)
        v_tok = area(NT, D)
        qm = area(HG, T)
        v_aug = area(2, HG * ROWS)
        prob = area(HG, 2, T)
        eraw = area(HG, 2, T)
        pT = area(2 * HG, 2 * (T + 1))
        yT = area(G, NT * P)
        sums = area(H, 2 * HG)
        negmax = area(HG, 2)
        low = area(HG, 2)
        small = area(8, 2 * HG)
        rbc = area(2, 2, P)
        rb = area(2, T)
        vsum = area(1)

        area = Area()
        oT = area(XP, NT * P)
        xpT = area(2, 2, KT * T)
        xprob = area(2, 2 * KEYS)

        xq_high = sb("xq_high", [P, 2, T], f32r)
        xq_low = sb("xq_low", [P, 2, T], f32r)
        acur = sb("acur", [P, 2, P])
        xnegmax = sb("xnegmax", [P, 2, 2])
        xsums = sb("xsums", [P, 2, 2, 2])
        xr = sb("xr", [P, 4])
        xrbc = sb("xrbc", [P, 2, P])
        xrb = sb("xrb", [P, T])
        ytmp = xrb[:, 0:T]

        area = Area()
        xin = area(NT, D)
        w1b = area(2, F)
        w2b = area(2, FT * D)
        hid = area(2 * FT, BANK)
        gates = area(NT, E + 2)
        probs = area(NT, E)
        pick = area(NT, E)
        coef = area(NT, 2)
        g1 = area(8, NT)
        route = area(NT, E + 1)
        routeT = area(NT * P)

        area = Area()
        qx = area(NT * P)
        kx = area(NC * P)
        vx = area(NC, D)
        maskx = area(2, S2)
        sm = area(2, S2)
        px = area(2, S2)
        pxT = area(2, S2)
        nm1, sm1, r1 = area(NT), area(NT), area(NT)

        area = Area()
        lowT = area(NT * P)
        lowTm = area(NT * P)
        lg, lp, lpick, lsel, lw = area(NT, E2), area(NT, E2), area(NT, E2), area(NT, E2), area(NT, E2 + 1)
        l1 = area(8, NT)
        lwT = area(NT * P)

        psum = ctx.enter_context(nc.psum_tensor("psum", [P, 8, BANK], f32))
        bank = [psum[:, i, :] for i in range(8)]

        def col(key, name):
            at = 0
            for n, w in LAYOUT[key]:
                if n == name:
                    return packs[key][:, at:at + w]
                at += w
            raise KeyError(name)

        ident = col("a", "ident")

        def banks_pair(half):
            return psum[:, 2 * half:2 * half + 2, 0:KEYS // 2]

        SINGLE_BANKS = (0, 6, 7, 1)

        def tiles(view):
            return view.rearrange("p (t c) -> p t c", c=D)

        def spread(view, n):
            return view.unsqueeze(2).broadcast_to([P, view.shape[1], n])

        factor, floor_factor = small[:, 0, :], small[:, 3, :]

        def over_rows(k):
            return rbc[:, k, :, :].rearrange("p u (j r) -> p (u j) r", j=HG)

        loaded = {k: sem(f"loaded_{k}") for k in ("ctx", "a", "b", "q", "v", "f", "l", "mask")}
        loaded_x = [sem("loaded_x0"), sem("loaded_x1")]
        stored = sem("stored")
        constants = sem("constants")
        dve_chain, pool_chain = sem("dve_chain"), sem("pool_chain")
        centred_ready, squared, rstd_ready = sem("centred_ready"), sem("squared"), sem("rstd_ready")
        normed = sem("normed")
        var_ready = sem("var_ready")
        prep_psum, prep_act, prep_dve = sem("prep_psum"), sem("prep_act"), sem("prep_dve")
        x_done, x_parts = sem("x_done"), sem("x_parts")
        CONSTANTS = 4

        class Attention:

            def __init__(self, tag, causal, clip, act_heads):
                self.causal, self.clip = causal, clip
                self.act_heads = act_heads
                self.dve_heads = [j for j in range(HG) if j not in act_heads]
                self.zT_psum = sem(f"{tag}_zT_psum")
                self.zT_act = sem(f"{tag}_zT_act")
                self.qkv_psum = sem(f"{tag}_qkv_psum")
                self.k_ready = sem(f"{tag}_k_ready")
                self.qv_ready = sem(f"{tag}_qv_ready")
                self.qm_ready = sem(f"{tag}_qm_ready")
                self.score_psum = sem(f"{tag}_score_psum")
                self.max_ready = sem(f"{tag}_max_ready")
                self.exp_done = sem(f"{tag}_exp_done")
                self.clip_done = sem(f"{tag}_clip_done") if clip else None
                self.pT_psum = sem(f"{tag}_pT_psum")
                self.pT_act = sem(f"{tag}_pT_act")
                self.pT_dve = sem(f"{tag}_pT_dve")
                self.v_aug_ready = sem(f"{tag}_v_aug_ready")
                self.rbc_ready = sem(f"{tag}_rbc_ready")
                self.factors_ready = sem(f"{tag}_factors_ready") if clip else None
                self.rb_psum = sem(f"{tag}_rb_psum")
                self.rb_ready = sem(f"{tag}_rb_ready")
                self.y_done = sem(f"{tag}_y_done")
                self.out_psum = sem(f"{tag}_out_psum")

            def evacuated(self, eng, it, j):
                if j in self.act_heads:
                    eng.wait_ge(self.pT_act, it * len(self.act_heads) + self.act_heads.index(j) + 1)
                else:
                    eng.wait_ge(self.pT_dve, it * len(self.dve_heads) + self.dve_heads.index(j) + 1)

            def probabilities(self, eng, n):
                if self.clip:
                    eng.wait_ge(self.clip_done, n * 2)
                else:
                    eng.wait_ge(self.exp_done, n)

            def pT_of(self, odd, j):
                if self.clip:
                    return pT[:, odd * HG + j, :].rearrange("p (k t) -> p k t", k=2)[:, :, 0:T]
                return pT[:, odd * HG + j, 0:len(self.blocks()) * P]

            def pT_from(self, j):
                if self.clip:
                    return bank[4 + j % 2].rearrange("p (k t) -> p k t", k=2)
                return bank[4 + j % 2][:, 0:len(self.blocks()) * P]

            def blocks(self):
                return [(0, 0), (0, 1), (1, 1)] if self.causal and not self.clip else [(0, 0), (0, 1), (1, 0), (1, 1)]

        att0 = Attention("att0", True, False, [1])
        att1 = Attention("att1", False, False, [1])
        att2 = Attention("att2", True, True, [0, 1, 2, 3])

        def family(tag, *names):
            return {n: sem(f"{tag}_{n}") for n in names}

        sx = family("x", "zT_psum", "zT_act", "zT_dve", "acur_ready", "q_psum", "q_high", "q_ready", "kv_high",
                    "kv_split", "v_psum", "v_ready",
                    "score_psum", "max_ready", "exp_done", "pT_psum", "pT_act", "pT_dve", "rbc_ready",
                    "rb_psum", "rb_ready", "y_done", "out_psum")
        sf = family("f", "xin_ready", "zT_psum", "zT_act", "gate_psum", "gate_shifted", "gate_exp",
                    "route_ready", "routeT_psum", "routeT_ready", "bias_psum", "hid_psum", "gelu_done", "down_psum",
                    "mixed", "w1_slot0", "w1_slot1", "w2_slot0", "w2_slot1", "w1_high", "w1_split", "z_high", "z_split")
        sg = family("g", "zT_psum", "zT_act", "proj_psum", "proj_act", "proj_dve", "score_psum",
                    "max_ready", "exp_done", "pT_psum", "pT_ready", "out_psum")
        sl = family("l", "zT_psum", "zT_act", "zT_dve", "low_psum", "low_ready", "gate_psum", "base_psum", "base_added",
                    "gate_shifted",
                    "gate_exp", "route_ready", "routeT_psum", "routeT_ready", "wide_psum", "mixed", "out_psum")

        jobs = {}

        def job(key, src, dst, after):
            jobs[key] = (len(jobs), src, dst, after)

        def quarter(view, h):
            return view[:, 4 * h:4 * h + 4, :]

        for h in range(2):
            job(("n0", h), quarter(x, h), quarter(z, h), (loaded_x[h], 16))
        for c in range(4):
            job(("ctx", c), quarter(ctx_x, c), quarter(ctx_z, c), (loaded["ctx"], 16))

        def again(name, s, h):
            job((name, h), quarter(z, h), quarter(z2, h), (normed, jobs[(f"n{s}", h)][0] + 1))

        for s in range(1, 6):
            for h in range(2):
                job((f"n{s}", h), quarter(x, h), quarter(z, h), (x_done, 2 * s - 1 + h))
                if s == 2:
                    again("ln1", s, h)
            if s == 1:
                for h in range(2):
                    again("lat", s, h)
            if s == 2:
                for h in range(2):
                    job(("ln2", h), quarter(xin, h), quarter(z2, h), (sf["xin_ready"], h + 1))
        FIRST_JOBS = [("n0", 0), ("n0", 1)]
        CONTEXT_JOBS = [[("ctx", 0), ("ctx", 1)], [("ctx", 2), ("ctx", 3)]]

        def wait_normed(eng, name, h):
            eng.wait_ge(normed, jobs[(name, h)][0] + 1)

        block = ctx.enter_context(nc.Block())

        @block.sync
        def _(sp):
            for h in range(2):
                sp.dma_start(quarter(x, h), x_d[2 * h:2 * h + 2].rearrange("b (u p) c -> p (b u) c", p=P))\
                    .then_inc(loaded_x[h], 16)
            sp.dma_start(packs["a"][:, :], packs_d["a"]).then_inc(loaded["a"], 16)
            sp.dma_start(ctx_x[:, :, :], ctx_d.rearrange("b (u p) c -> p (b u) c", p=P)).then_inc(loaded["ctx"], 16)
            sp.dma_start(packs["b"][:, :], packs_d["b"]).then_inc(loaded["b"], 16)
            sp.dma_start(packs["q"][:, :], packs_d["q"]).then_inc(loaded["q"], 16)
            sp.dma_start(packs["v"][:, :], packs_d["v"]).then_inc(loaded["v"], 16)
            sp.dma_start(packs["f"][:, :], packs_d["f"]).then_inc(loaded["f"], 16)
            sp.dma_start(packs["l"][:, :], packs_d["l"]).then_inc(loaded["l"], 16)
            def load_w1(e, slot):
                sp.dma_start(w1b[:, slot, :], w1_d[e]).then_inc(sf[f"w1_slot{slot}"], 16)

            def load_w2(e, slot):
                sp.dma_start(w2b[:, slot, :], w2_d[e]).then_inc(sf[f"w2_slot{slot}"], 16)

            sp.wait_ge(sf["xin_ready"], 1)
            for e in range(2):
                load_w1(e, e)
                load_w2(e, e)
            sp.wait_ge(sf["w1_split"], 1)
            load_w1(2, 0)
            sp.wait_ge(sf["down_psum"], 2)
            load_w2(2, 0)
            with sp.Fori(1, E // 2) as i:
                for k in range(2):
                    sp.wait_ge(sf["w1_split"], i * 2 + k)
                    load_w1(i * 2 + k + 1, 1 - k)
                    sp.wait_ge(sf["down_psum"], (i * 2 + k) * 2)
                    load_w2(i * 2 + k + 1, 1 - k)
            sp.wait_ge(x_done, 8)
            sp.dma_start(maskx, mask_d[0].rearrange("(u p) k -> p u k", p=P)).then_inc(loaded["mask"], 16)
            for h in range(2):
                sp.wait_ge(x_done, 2 * BLOCKS - 1 + h)
                sp.dma_start(out_d[2 * h:2 * h + 2].rearrange("b (u p) c -> p (b u) c", p=P), quarter(x, h))\
                    .then_inc(stored, 16)
            sp.wait_ge(stored, 32)

        @block.tensor
        def _(pe):
            mm, transpose = nc.tensor.matmul, nc.tensor.transpose

            def transposes(name, src, h, done):
                wait_normed(pe, name, h)
                for t in range(4):
                    last = transpose(bank[h][:, t * P:(t + 1) * P], src[:, 4 * h + t, :], ident)
                last.then_inc(done, 1)

            def effective_weights():
                pe.wait_ge(loaded["a"], 16)
                mm(bank[0][:, 0:3 * D], col("a", "la0")[0:RL, :], col("a", "lb0")[0:RL, :], start=True, stop=True)\
                    .then_inc(prep_psum, 1)
                pe.wait_ge(prep_dve, 1)

            def effective_projection():
                pe.wait_ge(loaded["b"], 16)
                for g in range(G):
                    last = mm(bank[7][:, g * D:(g + 1) * D], col("b", "lap0")[0:RL, g * P:(g + 1) * P],
                              col("b", "lbp0")[0:RL, :], start=True, stop=True)
                last.then_inc(prep_psum, 1)

            def cross_operands():
                pe.wait_ge(loaded["q"], 16)
                for h in range(XH):
                    r = slice(XD * (h % 2), XD * (h % 2) + XD)
                    c = slice((h // 2) * D, (h // 2 + 1) * D)
                    bk, s = 2 + 2 * (h % 2) + h // 8, (h // 2) % 4
                    last = mm(bank[bk][:, s * P:(s + 1) * P], col("q", "wqT")[r, c], col("q", "wkT")[r, c],
                              start=True, stop=True)
                    if s == 3:
                        last.then_inc(prep_psum, 1)
                pe.wait_ge(loaded["ctx"], 16)
                for i in range(8):
                    c = i % 4
                    if i >= 4:
                        pe.wait_ge(normed, jobs[("ctx", c)][0] + 1)
                    if i >= 2:
                        pe.wait_ge(prep_act, i + 4)
                    src = ctx_x if i < 4 else ctx_z
                    for t in range(4):
                        last = transpose(bank[6 + c % 2][:, t * P:(t + 1) * P], src[:, 4 * c + t, :], ident)
                    last.then_inc(prep_psum, 1)
                for h in range(2):
                    transposes("lat", z2, h, sx["zT_psum"])

            def attention(a, src, name, w, wp, aside=None):
                for h in range(2):
                    transposes(name, src, h, a.zT_psum)
                    if h == 0 and aside:
                        aside()
                    pe.wait_ge(a.zT_act, h + 1)
                    cols = slice(h * BANK, (h + 1) * BANK)
                    mm(bank[2 + h][:, :], w[:, 0:D], zT[:, cols], start=True, stop=True).then_inc(a.qkv_psum, 1)
                    mm(bank[4 + h][:, :], w[:, D:2 * D], zT[:, cols], start=True, stop=True).then_inc(a.qkv_psum, 1)
                    if h and aside:
                        pe.wait_ge(prep_dve, 2)
                    for t in range(4):
                        last = mm(bank[6 + h][:, t * P:(t + 1) * P], zT[:, (4 * h + t) * P:(4 * h + t + 1) * P],
                                  w[:, 2 * D:3 * D], start=True, stop=True)
                    last.then_inc(a.qkv_psum, 1)
                pe.wait_ge(a.k_ready, 1)
                pe.wait_ge(a.qv_ready, 3)

                def scores(it, b, j, prev):
                    pe.wait_ge(a.qm_ready, it * HG + j + 1)
                    if prev:
                        pe.wait_ge(a.exp_done, it * HG + j - 3)
                    for u in range(2):
                        keys = P if a.causal and u == 0 else T
                        last = mm(bank[j][:, u * T:u * T + keys], qm[:, j, u * P:(u + 1) * P],
                                  kT[:, bass.ds(b * T, keys)], start=True, stop=not a.causal)
                        if a.causal:
                            last = mm(bank[j][:, u * T + keys - P:u * T + keys], identb[:, :], causalb[:, :],
                                      start=False, stop=True)
                    last.then_inc(a.score_psum, 1)

                def transposed(it, j, prev=True):
                    a.probabilities(pe, it * HG + j + 1)
                    if j >= 2:
                        a.evacuated(pe, it, j - 2)
                    elif prev and j == 1:
                        a.evacuated(pe, it - 1, 3)
                    elif prev:
                        a.evacuated(pe, it - 1, 2)
                    for i, (k, u) in enumerate(a.blocks()):
                        last = transpose(bank[4 + j % 2][:, i * P:(i + 1) * P], prob[:, j, u, k * P:(k + 1) * P], ident)
                    last.then_inc(a.pT_psum, 1)

                def weighted(group, odd):
                    for j in range(HG):
                        a.evacuated(pe, group, j)
                    pe.wait_ge(a.v_aug_ready, group + 1)
                    pe.wait_ge(a.y_done, group + 1)
                    for k in range(2):
                        dst, keys = slice(0, T), slice(k * T, (k + 1) * T)
                        if a.clip:
                            dst, keys = slice(0, T + 1), slice(k * (T + 1), (k + 1) * (T + 1))
                        elif k and len(a.blocks()) == 3:
                            dst, keys = slice(P, T), slice(T, T + P)
                        for j in range(HG):
                            mm(bank[6][ROWS * j:ROWS * (j + 1), dst], v_aug[:, k, ROWS * j:ROWS * (j + 1)],
                               pT[:, odd * HG + j, keys], start=(k == 0), stop=(k == 1))
                    pe.wait_ge(a.rbc_ready, group + 1)
                    for k in range(2 if a.clip else 1):
                        for u in range(2):
                            last = transpose(bank[7][:, k * T + u * P:k * T + (u + 1) * P], rbc[:, k, u, :], ident)
                    last.then_inc(a.rb_psum, 1)

                def body(it, b, odd, cur=True, prev=True, prev2=True):
                    for j in range(HG):
                        if cur:
                            scores(it, b, j, prev)
                        if j == 2 and prev2:
                            weighted(it - 2, odd)
                        if prev:
                            transposed(it - 1, j, prev2)

                body(0, 0, 0, prev=False, prev2=False)
                pe.wait_ge(a.k_ready, 2)
                body(1, 0, 1, prev2=False)
                with pe.Fori(1, H // 2) as i:
                    for k in range(2):
                        body(i * 2 + k, (i * 2) // G, k)

                def project(h):
                    for t in range(4 * h, 4 * h + 4):
                        for g in range(G):
                            last = mm(bank[h][:, (t % 4) * P:(t % 4 + 1) * P], yT[:, g, t * P:(t + 1) * P],
                                      wp[:, g * D:(g + 1) * D], start=(g == 0), stop=(g == G - 1))
                    last.then_inc(a.out_psum, 1)

                body(H, 0, 0, cur=False)
                pe.wait_ge(a.y_done, H // 2 + 1)
                pe.wait_ge(a.exp_done, H * HG - 3)
                project(0)
                body(H + 1, 0, 1, cur=False, prev=False)
                pe.wait_ge(a.y_done, H + 1)
                project(1)

            def cross():
                cross_operands()
                pe.wait_ge(sx["zT_act"], 1)
                pe.wait_ge(sx["zT_dve"], 1)
                pe.wait_ge(prep_act, 13)
                pe.wait_ge(loaded["v"], 16)
                wv, wo = col("v", "wv"), col("v", "wout")
                W = KEYS // 2

                def queries(it, u):
                    pe.wait_ge(sx["acur_ready"], it * 2 + u % 2 + 1)
                    mm(bank[6][:, T:2 * T], acur[:, u % 2, :], kvT[:, u // 2, S2:KEYS], start=True, stop=True)\
                        .then_inc(sx["q_psum"], 1)

                def values(it, b, half):
                    for k in range(3):
                        kt = 3 * half + k
                        last = mm(bank[7][:, k * P:(k + 1) * P], kvT[:, b, kt * P:(kt + 1) * P],
                                  wv[:, bass.ds(it * P, P)], start=True, stop=True)
                    last.then_inc(sx["v_psum"], 1)

                def scores(u, half):
                    for c in range(2):
                        out, tile, keys = bank[2 * half + c][:, 0:W], slice(half * P, (half + 1) * P), slice(c * W, (c + 1) * W)
                        mm(out, xq_high[:, u % 2, tile], kv_high[:, u // 2, keys], start=True, stop=False)
                        mm(out, xq_high[:, u % 2, tile], kv_low[:, u // 2, keys], start=False, stop=False)
                        last = mm(out, xq_low[:, u % 2, tile], kv_high[:, u // 2, keys], start=False, stop=True)
                    last.then_inc(sx["score_psum"], 1)

                def transposed(m, u, chunks, first=False):
                    pe.wait_ge(sx["exp_done"], m * 2 + 2)
                    for c in chunks:
                        if c == 2:
                            pe.wait_ge(sx["pT_act"], m * 2 + 1)
                        elif not first:
                            if c:
                                pe.wait_ge(sx["pT_act"], m * 2)
                            else:
                                pe.wait_ge(sx["pT_dve"], m)
                        for i in range(2):
                            kt = 2 * c + i
                            for h in range(2):
                                last = transpose(bank[4 + (3 * u + c) % 2][:, (2 * i + h) * P:(2 * i + h + 1) * P],
                                                 xprob[:, u % 2, h * KEYS + kt * P:h * KEYS + (kt + 1) * P], ident)
                        last.then_inc(sx["pT_psum"], 1)

                def weighted(p, b):
                    pe.wait_ge(sx["pT_dve"], p * 2 + 2)
                    pe.wait_ge(sx["pT_act"], p * 4 + 4)
                    pe.wait_ge(sx["y_done"], p + 1)
                    for kt in range(KT):
                        for a in range(2):
                            mm(bank[6][XD * a:XD * (a + 1), 0:T], xv[:, b, kt * P + XD * a:kt * P + XD * (a + 1)],
                               xpT[:, b % 2, a, kt * T:(kt + 1) * T], start=(kt == 0), stop=(kt == KT - 1))

                def factors(p):
                    pe.wait_ge(sx["rbc_ready"], p + 1)
                    for u in range(2):
                        last = transpose(bank[6][:, T + u * P:T + (u + 1) * P], xrbc[:, u, :], ident)
                    last.then_inc(sx["rb_psum"], 1)

                queries(0, 0)
                for half in range(2):
                    if half:
                        pe.wait_ge(sx["v_ready"], 1)
                    values(0, 0, half)

                def body(it, prev, cur):
                    for u in range(8):
                        n, b, odd = it * 8 + u, u // 2, u % 2
                        weigh = odd and (prev or u > 1)
                        behind = (prev and u == 0) or (cur and u)
                        if cur:
                            pe.wait_ge(sx["q_ready"], n + 1)
                            if prev or u:
                                pe.wait_ge(sx["exp_done"], n * 2 - 1)
                            if not prev and not odd:
                                pe.wait_ge(sx["kv_split"], b + 1)
                            scores(u, 0)
                            if odd:
                                queries(it + (u + 1) // 8, (u + 1) % 8)
                            pe.wait_ge(sx["v_ready"], n + 2)
                            values(it + (b + 1) // 4, (b + 1) % 4, odd)
                        if behind:
                            transposed(n - 1, (u - 1) % 8, (0, 1), first=(not prev and u == 1))
                        if cur:
                            if not odd:
                                if prev or u >= 4:
                                    pe.wait_ge(sx["rb_ready"], it * 4 + b - 1)
                                    pe.wait_ge(sx["y_done"], it * 4 + b)
                                queries(it, u + 1)
                            if prev or u:
                                pe.wait_ge(sx["exp_done"], n * 2)
                            scores(u, 1)
                        if weigh:
                            if cur:
                                pe.wait_ge(sx["q_ready"], n + 2)
                            weighted(it * 4 + b - 1, (b - 1) % 4)
                        if behind:
                            transposed(n - 1, (u - 1) % 8, (2,))
                        if weigh:
                            factors(it * 4 + b - 1)
                        if not cur and u == 0:
                            pe.wait_ge(sx["y_done"], XP * B - 1)
                            pe.wait_ge(sx["exp_done"], XP * B * 4)
                            project(0)
                        if not cur and u == 1:
                            break

                def project(h):
                    for t in range(4 * h, 4 * h + 4):
                        for p in range(XP):
                            last = mm(bank[h][:, (t % 4) * P:(t % 4 + 1) * P], oT[:, p, t * P:(t + 1) * P],
                                      wo[:, p * D:(p + 1) * D], start=(p == 0), stop=(p == XP - 1))
                    last.then_inc(sx["out_psum"], 1)

                body(0, False, True)
                with pe.Fori(1, XP) as it:
                    body(it, True, True)
                body(XP, True, False)
                pe.wait_ge(sx["y_done"], XP * B + 1)
                project(1)

            def experts():
                def gate():
                    transposes("ln2", z2, 1, sf["zT_psum"])
                    pe.wait_ge(sf["zT_act"], 2)
                    for t in range(NT):
                        last = mm(bank[2][:, t * (E + 2):(t + 1) * (E + 2)], zT[:, t * P:(t + 1) * P], col("f", "gate"),
                                  start=True, stop=True)
                    last.then_inc(sf["gate_psum"], 1)

                def expert(e, slot, prev, cur):
                    for u in range(2 * FT):
                        n, c, t = e * (2 * FT) + u, u // FT, u % FT
                        if not prev and u == FT:
                            gate()
                        if cur:
                            if u == 0:
                                pe.wait_ge(sf["w1_split"], e + 1)
                            if prev or u >= 4:
                                pe.wait_ge(sf["gelu_done"], n - 3)
                            if not prev and t == 0:
                                pe.wait_ge(sf["z_split"], c + 1)
                            out, w, tokens = bank[4 + u % 4][:, :], slice(t * P, (t + 1) * P), slice(c * BANK, (c + 1) * BANK)
                            mm(out, w1_high[:, slot, w], z_high[:, tokens], start=True, stop=False)
                            mm(out, w1_high[:, slot, w], z_low[:, tokens], start=False, stop=False)
                            mm(out, w1_low[:, slot, w], z_high[:, tokens], start=False, stop=True)\
                                .then_inc(sf["hid_psum"], 1)
                        if prev if c == 0 else cur:
                            half, s = (1, 1 - slot) if c == 0 else (0, slot)
                            if t == 0:
                                if c:
                                    pe.wait_ge(sf[f"w2_slot{slot}"], (e // 2) * 16 + 16)
                                pe.wait_ge(sf["gelu_done"], n)
                                if prev:
                                    pe.wait_ge(sf["mixed"], e * 2 + c)
                            for f in range(FT):
                                last = mm(bank[2 * s + half][:, t * P:(t + 1) * P], hid[:, FT * half + f, t * P:(t + 1) * P],
                                          w2b[:, s, f * D:(f + 1) * D], start=(f == 0), stop=(f == FT - 1))
                            if t == FT - 1:
                                last.then_inc(sf["down_psum"], 1)
                        if not cur and t == FT - 1:
                            break

                transposes("ln2", z2, 0, sf["zT_psum"])
                pe.wait_ge(sf["zT_act"], 1)
                expert(0, 0, False, True)
                pe.wait_ge(sf["route_ready"], 1)
                for t in range(NT):
                    last = transpose(bank[2 + t // 4][0:E + 1, (t % 4) * P:(t % 4 + 1) * P], route[:, t, :], ident)
                last.then_inc(sf["routeT_psum"], 1)
                pe.wait_ge(sf["routeT_ready"], 2)
                for t in range(NT):
                    last = mm(bank[2 + t // 4][:, (t % 4) * P:(t % 4 + 1) * P], routeT[0:E + 1, t * P:(t + 1) * P],
                              col("f", "b2")[0:E + 1, :], start=True, stop=True)
                    if t % 4 == 3:
                        last.then_inc(sf["bias_psum"], 1)
                with pe.Fori(0, E // 2) as i:
                    for k in range(2):
                        expert(i * 2 + k + 1, 1 - k, True, True)
                expert(E + 1, 1, True, False)

            def single():
                for c in range(4):
                    mm(bank[2 + c][:, :], col("l", "wk4"), ctxT[:, c * BANK:(c + 1) * BANK], start=True, stop=True)\
                        .then_inc(sg["proj_psum"], 1)

                def values(c):
                    for t in range(4):
                        last = mm(bank[(6, 7, 2, 3)[c]][:, t * P:(t + 1) * P], ctxT[:, (4 * c + t) * P:(4 * c + t + 1) * P],
                                  col("l", "wv4"), start=True, stop=True)
                    last.then_inc(sg["proj_psum"], 1)

                def queries(c):
                    pe.wait_ge(sg["zT_act"], c + 1)
                    mm(bank[4 + c][:, :], col("l", "wq4"), zT[:, c * BANK:(c + 1) * BANK], start=True, stop=True)\
                        .then_inc(sg["proj_psum"], 1)

                def scores(n):
                    if n >= 4:
                        pe.wait_ge(sg["max_ready"], n - 3)
                    mm(bank[SINGLE_BANKS[n % 4]][:, :], qx[:, n * P:(n + 1) * P], kx[:, (n // 2) * S2:(n // 2 + 1) * S2],
                       start=True, stop=True).then_inc(sg["score_psum"], 1)

                values(0)
                values(1)
                transposes("n4", z, 0, sg["zT_psum"])
                pe.wait_ge(sg["proj_act"], 4)
                values(2)
                queries(0)
                values(3)
                transposes("n4", z, 1, sg["zT_psum"])
                pe.wait_ge(sg["proj_dve"], 3)
                scores(0)
                queries(1)
                for n in range(NT + 2):
                    if n + 1 == 4:
                        pe.wait_ge(sg["proj_dve"], 6)
                    if n + 1 < NT:
                        scores(n + 1)
                    if 1 <= n <= NT:
                        m = n - 1
                        if m == 0:
                            pe.wait_ge(sg["proj_dve"], 5)
                        pe.wait_ge(sg["exp_done"], m + 1)
                        if m >= 2:
                            pe.wait_ge(sg["pT_ready"], m - 1)
                        for k in range(4):
                            last = transpose(bank[2 + m % 2][:, k * P:(k + 1) * P], px[:, m % 2, k * P:(k + 1) * P], ident)
                        last.then_inc(sg["pT_psum"], 1)
                    if n >= 2:
                        m = n - 2
                        pe.wait_ge(sg["pT_ready"], m + 1)
                        if m >= 2:
                            pe.wait_ge(x_parts, m - 1)
                        for k in range(4):
                            last = mm(bank[4 + m % 2][:, 0:D], pxT[:, m % 2, k * P:(k + 1) * P],
                                      vx[:, (m // 2) * 4 + k, :], start=(k == 0), stop=(k == 3))
                        last.then_inc(sg["out_psum"], 1)

            def mixture():
                def gate(h):
                    for t in range(4 * h, 4 * h + 4):
                        last = mm(bank[4][:, t * E2:(t + 1) * E2], zT[:, t * P:(t + 1) * P], col("l", "router"),
                                  start=True, stop=True)
                    last.then_inc(sl["gate_psum"], 1)

                def base(h):
                    for t in range(4 * h, 4 * h + 4):
                        out = bank[h][:, (t % 4) * P:(t % 4 + 1) * P]
                        mm(out, zT[:, t * P:(t + 1) * P], col("l", "base"), start=True, stop=False)
                        last = mm(out, ones[0:1, 0:P], col("l", "base_b")[0:1, :], start=False, stop=True)
                    last.then_inc(sl["base_psum"], 1)

                transposes("n5", z, 0, sl["zT_psum"])
                pe.wait_ge(sl["zT_act"], 1)
                gate(0)
                base(0)
                transposes("n5", z, 1, sl["zT_psum"])
                pe.wait_ge(sl["zT_dve"], 1)
                gate(1)
                for c in range(2):
                    mm(bank[2 + c][0:RU, :], col("l", "lowA"), zT[:, c * BANK:(c + 1) * BANK], start=True, stop=True)\
                        .then_inc(sl["low_psum"], 1)
                base(1)
                pe.wait_ge(sl["route_ready"], 1)
                for t in range(NT):
                    last = transpose(bank[5 + t // 4][0:E2 + 1, (t % 4) * P:(t % 4 + 1) * P], lw[:, t, :], ident)
                    if t % 4 == 3:
                        last.then_inc(sl["routeT_psum"], 1)
                for c in range(2):
                    pe.wait_ge(sl["routeT_ready"], c + 1)
                    mm(bank[4 + 3 * c][0:RU, :], col("l", "sel7")[0:E2 + 1, :], lwT[0:E2 + 1, c * BANK:(c + 1) * BANK],
                       start=True, stop=True).then_inc(sl["wide_psum"], 1)
                pe.wait_ge(sl["low_ready"], 2)
                for t in range(NT):
                    if t % 4 == 0:
                        pe.wait_ge(sl["mixed"], t // 4 + 1)
                    last = mm(bank[2 + t // 4][:, (t % 4) * P:(t % 4 + 1) * P], lowTm[0:RU, t * P:(t + 1) * P],
                              col("l", "lowB")[0:RU, :], start=True, stop=True)
                    if t % 4 == 3:
                        last.then_inc(sl["out_psum"], 1)

            effective_weights()
            pe.wait_ge(constants, CONSTANTS)
            attention(att0, z, "n0", weff, wpeff, effective_projection)
            cross()
            pe.wait_ge(loaded["f"], 16)
            attention(att1, z2, "ln1", col("f", "w2"), col("f", "wp2"))
            experts()
            pe.wait_ge(loaded["l"], 16)
            attention(att2, z, "n3", col("l", "w3"), col("l", "wp3"))
            single()
            mixture()

        @block.scalar
        def _(act):
            activation = nc.scalar.activation

            def square_jobs(keys):
                for key in keys:
                    k = jobs[key][0]
                    act.wait_ge(centred_ready, k + 1)
                    if k >= 2:
                        act.wait_ge(var_ready, k - 1)
                    activation(squares[:, k % 2, :, :], centred[:, k % 4, :, :], ACT.Square).then_inc(squared, 1)

            def affine(out, in_, g, b, done):
                activation(out, in_, ACT.Identity, bias=b, scale=g).then_inc(done, 1)

            def transposed(h, psum, done, g=None, b=None):
                act.wait_ge(psum, h + 1)
                if g is None:
                    activation(zT[:, h * BANK:(h + 1) * BANK], bank[h][:, :], ACT.Copy).then_inc(done, 1)
                else:
                    affine(zT[:, h * BANK:(h + 1) * BANK], bank[h][:, :], g, b, done)

            def attention(a, g, b, bias_k, asides=(), squares_between=((), ())):
                for h in range(2):
                    transposed(h, a.zT_psum, a.zT_act, g, b)
                    square_jobs(squares_between[0] if h == 0 else ())
                    act.wait_ge(a.qkv_psum, 3 * h + 2)
                    activation(kT[:, h * BANK:(h + 1) * BANK], bank[4 + h][:, :], ACT.Identity, bias=bias_k)\
                        .then_inc(a.k_ready, 1)
                    square_jobs(squares_between[1] if h == 0 else ())
                for keys in asides[:1]:
                    square_jobs(keys)

                def exponentials(it, j, prev):
                    n = it * HG + j
                    act.wait_ge(a.max_ready, n + 1)
                    if prev:
                        if a.clip:
                            a.probabilities(act, n - 3)
                        else:
                            act.wait_ge(a.pT_psum, n - 3)
                    if a.clip:
                        activation(low[:, j, :], negmax[:, j, :], ACT.Exp, bias=low_bias[:, :])
                    for u in range(2):
                        keys = P if a.causal and u == 0 else T
                        if a.clip:
                            last = activation(eraw[:, j, u, 0:keys], bank[j][:, u * T:u * T + keys], ACT.Exp,
                                              bias=negmax[:, j, u:u + 1])
                        else:
                            last = activation(prob[:, j, u, 0:keys], bank[j][:, u * T:u * T + keys], ACT.Exp,
                                              bias=negmax[:, j, u:u + 1], accum_out=sums[:, it, u * HG + j:u * HG + j + 1])
                    last.then_inc(a.exp_done, 1)

                def evacuate(it, odd, j):
                    if j in a.act_heads:
                        act.wait_ge(a.pT_psum, it * HG + j + 1)
                        activation(a.pT_of(odd, j), a.pT_from(j), ACT.Copy).then_inc(a.pT_act, 1)

                def body(it, odd, cur=True, prev=True, prev2=True):
                    for j in range(HG):
                        if cur:
                            exponentials(it, j, prev)
                        if prev:
                            evacuate(it - 1, 1 - odd, j)
                        if j == 2 and prev2:
                            act.wait_ge(a.rb_psum, it - 1)
                            w = 2 if a.clip else 1
                            activation(rb[:, 0:w, :], bank[7][:, 0:w * T].rearrange("p (k t) -> p k t", k=w), ACT.Copy)\
                                .then_inc(a.rb_ready, 1)

                body(0, 0, prev=False, prev2=False)
                for keys in asides[1:]:
                    square_jobs(keys)
                body(1, 1, prev2=False)
                with act.Fori(1, H // 2) as i:
                    for k in range(2):
                        body(i * 2 + k, k)
                body(H, 0, cur=False)
                body(H + 1, 1, cur=False, prev=False)

            def cross():
                square_jobs([("n1", 0), ("n1", 1)])
                for i in range(4):
                    odd, late = i % 2, i // 2
                    if i == 2:
                        square_jobs([("lat", 0)])
                    act.wait_ge(prep_psum, 3 + i)
                    activation(A_all[:, 8 * late + odd:8 * late + odd + 7:2, :], tiles(bank[2 + 2 * odd + late][:, :]),
                               ACT.Copy, scale=XD ** -0.5).then_inc(prep_act, 1)
                activation(A_all[:, XH:XH + 2, :], psum[:, 2:5:2, 0:P], ACT.Copy, scale=XD ** -0.5)\
                    .then_inc(prep_act, 1)
                for i in range(8):
                    c = i % 4
                    if i == 4:
                        square_jobs([("lat", 1)])
                    act.wait_ge(prep_psum, 7 + i)
                    if i < 4:
                        activation(ctxT[:, c * BANK:(c + 1) * BANK], bank[6 + c % 2][:, :], ACT.Copy).then_inc(prep_act, 1)
                    else:
                        affine(kvT[:, c, 0:S2], bank[6 + c % 2][:, :], col("b", "lnm_g"), col("b", "lnm_b"), prep_act)
                act.wait_ge(sx["zT_psum"], 1)
                affine(kvT[:, 0:2, S2:KEYS], bank[0][:, :].rearrange("p (b t) -> p b t", b=2), col("b", "lnl_g"),
                       col("b", "lnl_b"), sx["zT_act"])
                act.wait_ge(sx["q_psum"], 1)
                activation(xq_high[:, 0, :], bank[6][:, T:2 * T], ACT.Copy).then_inc(sx["q_high"], 1)
                act.wait_ge(prep_act, 13)
                act.wait_ge(sx["zT_act"], 1)
                for b in range(B):
                    if b == 2:
                        act.wait_ge(sx["zT_dve"], 1)
                    activation(kv_high[:, b, :], kvT[:, b, :], ACT.Copy).then_inc(sx["kv_high"], 1)

            def cross_units():
                def body(it, prev, cur):
                    for u in range(8):
                        n, b, odd = it * 8 + u, u // 2, u % 2
                        behind = (prev and u == 0) or (cur and u)
                        if cur:
                            if odd:
                                queries(n, u)
                            exponentials(it, n, u, 0, prev)
                        if behind:
                            evacuate(n - 1, (u - 1) % 8, 0)
                        if cur:
                            if not odd:
                                queries(n, u)
                            exponentials(it, n, u, 1, prev)
                        if behind:
                            evacuate(n - 1, (u - 1) % 8, 2)
                        if odd and (prev or u > 1):
                            act.wait_ge(sx["rb_psum"], it * 4 + b)
                            activation(xrb[:, :], bank[6][:, T:2 * T], ACT.Copy).then_inc(sx["rb_ready"], 1)
                        if not cur and u == 1:
                            break

                def queries(n, u):
                    act.wait_ge(sx["q_psum"], n + 2)
                    activation(xq_high[:, (u + 1) % 2, :], bank[6][:, T:2 * T], ACT.Copy).then_inc(sx["q_high"], 1)

                def evacuate(m, mu, c):
                    act.wait_ge(sx["pT_psum"], m * 3 + c + 1)
                    activation(xpT[:, (mu // 2) % 2, mu % 2, 2 * c * T:2 * (c + 1) * T], bank[4 + (3 * mu + c) % 2][:, :],
                               ACT.Copy).then_inc(sx["pT_act"], 1)

                def exponentials(it, n, u, half, prev):
                    act.wait_ge(sx["max_ready"], n * 2 + half + 1)
                    if half == 0 and (prev or u >= 2):
                        act.wait_ge(sx["pT_psum"], n * 3 - 3)
                    src = banks_pair(half)
                    activation(xprob[:, u % 2, half * KEYS:(half + 1) * KEYS].rearrange("p (c w) -> p c w", c=2), src,
                               ACT.Exp, bias=xnegmax[:, u % 2, half:half + 1],
                               accum_out=xsums[:, (u // 2) % 2, half, u % 2:u % 2 + 1]).then_inc(sx["exp_done"], 1)

                body(0, False, True)
                with act.Fori(1, XP) as it:
                    body(it, True, True)
                body(XP, True, False)

            def experts():
                ln2 = col("f", "ln2_g"), col("f", "ln2_b")

                def z_halves(h):
                    transposed(h, sf["zT_psum"], sf["zT_act"], *ln2)
                    affine(z_high[:, h * BANK:(h + 1) * BANK], bank[h][:, :], *ln2, sf["z_high"])

                def weight_high(e, slot):
                    act.wait_ge(sf[f"w1_slot{slot}"], (e // 2) * 16 + 16)
                    activation(w1_high[:, slot, :], w1b[:, slot, :], ACT.Copy).then_inc(sf["w1_high"], 1)

                square_jobs([("ln2", 0)])
                weight_high(0, 0)
                z_halves(0)
                square_jobs([("ln2", 1)])
                b1 = col("f", "b1")

                def expert(e, slot, prev=True, last=False):
                    for u in range(2 * FT):
                        n = e * (2 * FT) + u
                        if not prev and u == FT:
                            z_halves(1)
                        if not last and u == 2 * FT - 2:
                            weight_high(e + 1, 1 - slot)
                        if not prev and u == FT + 1:
                            act.wait_ge(sf["gate_shifted"], 1)
                            activation(gates[:, :, :], gates[:, :, :], ACT.Exp).then_inc(sf["gate_exp"], 1)
                        act.wait_ge(sf["hid_psum"], n + 1)
                        if prev and u % FT == 0:
                            act.wait_ge(sf["down_psum"], e * 2 + u // FT - 1)
                        activation(hid[:, u, :], bank[4 + u % 4][:, :], ACT.Gelu,
                                   bias=b1[:, bass.ds(e * 2 * FT + u, 1)]).then_inc(sf["gelu_done"], 1)

                expert(0, 0, prev=False)
                act.wait_ge(sf["routeT_psum"], 1)
                activation(routeT[0:E + 1, 0:BANK], bank[2][0:E + 1, :], ACT.Copy).then_inc(sf["routeT_ready"], 1)
                with act.Fori(0, E // 2 - 1) as i:
                    for k in range(2):
                        expert(i * 2 + k + 1, 1 - k)
                expert(E - 1, 1)
                expert(E, 0, last=True)

            def single():
                square_jobs([("n4", 0)])
                for c in range(4):
                    act.wait_ge(sg["proj_psum"], c + 1)
                    activation(kx[:, c * BANK:(c + 1) * BANK], bank[2 + c][:, :], ACT.Identity, bias=col("l", "bk4"))\
                        .then_inc(sg["proj_act"], 1)
                square_jobs([("n4", 1)])
                for h in range(2):
                    transposed(h, sg["zT_psum"], sg["zT_act"])
                for n in range(NT + 1):
                    if n < NT:
                        act.wait_ge(sg["max_ready"], n + 1)
                        if n >= 2:
                            act.wait_ge(sg["pT_psum"], n - 1)
                        activation(px[:, n % 2, :], sm[:, n % 2, :], ACT.Exp, bias=nm1[:, n:n + 1],
                                   accum_out=sm1[:, n:n + 1]).then_inc(sg["exp_done"], 1)
                    if n:
                        m = n - 1
                        act.wait_ge(sg["pT_psum"], m + 1)
                        if m >= 2:
                            act.wait_ge(sg["out_psum"], m - 1)
                        activation(pxT[:, m % 2, :], bank[2 + m % 2][:, :], ACT.Copy).then_inc(sg["pT_ready"], 1)
                    if n == 6:
                        square_jobs([("n5", 0)])

            def mixture():
                act.wait_ge(sl["zT_psum"], 1)
                activation(zT[:, 0:BANK], bank[0][:, :], ACT.Copy).then_inc(sl["zT_act"], 1)
                square_jobs([("n5", 1)])
                act.wait_ge(sl["gate_shifted"], 1)
                activation(lp, lg, ACT.Exp).then_inc(sl["gate_exp"], 1)
                for c in range(2):
                    act.wait_ge(sl["low_psum"], c + 1)
                    activation(lowT[0:RU, c * BANK:(c + 1) * BANK], bank[2 + c][0:RU, :], ACT.Copy)\
                        .then_inc(sl["low_ready"], 1)
                for c in range(2):
                    act.wait_ge(sl["routeT_psum"], c + 1)
                    activation(lwT[0:E2 + 1, c * BANK:(c + 1) * BANK], bank[5 + c][0:E2 + 1, :], ACT.Copy)\
                        .then_inc(sl["routeT_ready"], 1)

            square_jobs(FIRST_JOBS)
            act.wait_ge(loaded["a"], 16)
            activation(identb[:, :], ident, ACT.Copy).then_inc(constants, 1)
            activation(causalb[:, :], col("a", "causal"), ACT.Copy).then_inc(constants, 1)
            act.wait_ge(constants, CONSTANTS)
            attention(att0, None, None, col("a", "bk0"), CONTEXT_JOBS)
            cross()
            cross_units()
            act.wait_ge(loaded["f"], 16)
            square_jobs([("n2", 0), ("ln1", 0), ("n2", 1)])
            attention(att1, col("f", "ln1_g"), col("f", "ln1_b"), col("f", "bk2"),
                      squares_between=([("ln1", 1)], ()))
            experts()
            act.wait_ge(loaded["l"], 16)
            square_jobs([("n3", 0)])
            attention(att2, None, None, col("l", "zero"), squares_between=([("n3", 1)], ()))
            single()
            mixture()

        @block.vector
        def _(dve):
            v = nc.vector
            chain = Chain(dve_chain)

            def link(instruction):
                chain.did(instruction)
                chain.wait(dve)

            def centre(keys):
                for key in keys:
                    k, src, _, (after, value) = jobs[key]
                    dve.wait_ge(after, value)
                    link(v.tensor_reduce(stat[:, k % 4, 0, :], src, AX.X, ALU.add))
                    v.scalar_tensor_tensor(centred[:, k % 4, :, :], spread(stat[:, k % 4, 0, :], D), -1.0 / D, src,
                                           ALU.mult, ALU.add).then_inc(centred_ready, 1)

            def variances(keys):
                for key in keys:
                    k = jobs[key][0]
                    dve.wait_ge(squared, k + 1)
                    v.tensor_reduce(stat[:, k % 4, 1, :], squares[:, k % 2, :, :], AX.X, ALU.add).then_inc(var_ready, 1)

            def scale(keys):
                for key in keys:
                    k, _, dst, _ = jobs[key]
                    dve.wait_ge(rstd_ready, k + 1)
                    v.tensor_tensor(dst, centred[:, k % 4, :, :], spread(stat[:, k % 4, 3, :], D), ALU.mult)\
                        .then_inc(normed, 1)

            def normalise(keys):
                centre(keys)
                variances(keys)
                scale(keys)

            def add_to_x(psum, h, bk, done=x_done):
                dve.wait_ge(psum, h + 1)
                v.tensor_tensor(quarter(x, h), quarter(x, h), tiles(bank[bk][:, :]), ALU.add).then_inc(done, 1)

            def effective_weights():
                dve.wait_ge(prep_psum, 1)
                v.scalar_tensor_tensor(weff[:, :], bank[0][:, 0:3 * D], 0.5, col("a", "w0"), ALU.mult, ALU.add)\
                    .then_inc(prep_dve, 1)

            def effective_projection():
                dve.wait_ge(loaded["b"], 16)
                dve.wait_ge(prep_psum, 2)
                v.scalar_tensor_tensor(wpeff[:, :], bank[7][:, :], 0.5, col("b", "wp0"), ALU.mult, ALU.add)\
                    .then_inc(prep_dve, 1)

            def attention(a, bias_q, bias_v, asides=None):
                def aside(place):
                    if asides:
                        for work, *arguments in asides[place]:
                            work(*arguments)

                link(v.memset(v_aug, 0.0))
                link(v.memset(v_aug.rearrange("p k (j r) -> p k j r", j=HG)[:, :, :, HD:HD + 1], 1.0))
                if a.clip:
                    link(v.memset(eraw, 0.0))
                    link(v.memset(pT.rearrange("p j (k t) -> p (j k) t", k=2)[:, :, T:T + 1], 1.0))
                for h in range(2):
                    dve.wait_ge(a.qkv_psum, 3 * h + 1)
                    v.tensor_scalar(qT[:, h * BANK:(h + 1) * BANK], bank[2 + h][:, :], bias_q, HD ** -0.5,
                                    ALU.add, ALU.mult).then_inc(a.qv_ready, 1)
                    aside(h)
                    dve.wait_ge(a.qkv_psum, 3 * h + 3)
                    v.tensor_tensor(quarter(v_tok, h), tiles(bank[6 + h][:, :]),
                                    bias_v.unsqueeze(1).broadcast_to([P, 4, D]), ALU.add).then_inc(a.qv_ready, 1)
                v.memset(vsum, 0.0).then_inc(a.y_done, 1)
                dve.wait_ge(a.qv_ready, 4)

                def maxima(it, j):
                    dve.wait_ge(a.score_psum, it * HG + j + 1)
                    if a.causal:
                        last = v.tensor_reduce(negmax[:, j, 0:1], bank[j][:, 0:P], AX.X, ALU.max, negate=True)
                        if a.clip:
                            chain.did(last)
                        last = v.tensor_reduce(negmax[:, j, 1:2], bank[j][:, T:2 * T], AX.X, ALU.max, negate=True)
                    else:
                        last = v.tensor_reduce(negmax[:, j, :], bank[j][:, :].rearrange("p (u k) -> p u k", u=2), AX.X,
                                               ALU.max, negate=True)
                    if a.clip:
                        chain.did(last)
                    else:
                        last.then_inc(a.max_ready, 1)

                def clipped_maxima(j):
                    chain.wait(dve)
                    v.tensor_scalar(negmax[:, j, :], negmax[:, j, :], -CLIP, CLIP, ALU.max, ALU.min)\
                        .then_inc(a.max_ready, 1)

                def clipped(it, j, u, prev):
                    if u == 0:
                        dve.wait_ge(a.exp_done, it * HG + j + 1)
                        if prev:
                            dve.wait_ge(a.pT_psum, it * HG + j - 3)
                    v.scalar_tensor_tensor(prob[:, j, u, :], eraw[:, j, u, :], low[:, j, u:u + 1], ones[:, :], ALU.max,
                                           ALU.min, accum_out=sums[:, it, u * HG + j:u * HG + j + 1])\
                        .then_inc(a.clip_done, 1)

                def evacuate(it, odd, j):
                    if j in a.dve_heads:
                        dve.wait_ge(a.pT_psum, it * HG + j + 1)
                        v.tensor_copy(a.pT_of(odd, j), a.pT_from(j)).then_inc(a.pT_dve, 1)

                r, t, den, w = factor, small[:, 1, :], small[:, 2, :], floor_factor

                def factors(it):
                    dve.wait_ge(a.exp_done, it * HG + HG)
                    link(v.reciprocal(r, sums[:, it, :]))
                    v.tensor_copy(over_rows(0), spread(r, ROWS)).then_inc(a.rbc_ready, 1)

                def floored_factors(it, step, prev):
                    if step == 0:
                        dve.wait_ge(a.clip_done, (it * HG + HG) * 2)
                        chain.did(v.tensor_scalar(t, sums[:, it, :], FLOOR, FLOOR * TINY, ALU.mult, ALU.add))
                    else:
                        chain.wait(dve)
                    if step == 1:
                        chain.did(v.scalar_tensor_tensor(den, t, float(T), sums[:, it, :], ALU.mult, ALU.add))
                    if step == 2:
                        if prev:
                            dve.wait_ge(a.rbc_ready, it)
                        chain.did(v.reciprocal(r, den))
                    if step == 3:
                        v.tensor_tensor(w, t, r, ALU.mult).then_inc(a.factors_ready, 1)

                def values(it, b, g):
                    v.tensor_copy(v_aug.rearrange("p k (j r) -> p k j r", j=HG)[:, :, :, 0:HD],
                                  v_tok[:, bass.ds(b * 2, 2), bass.ds(g * HG * HD, HG * HD)]
                                  .rearrange("p k (j r) -> p k j r", j=HG)).then_inc(a.v_aug_ready, 1)

                def result_of(group):
                    return yT[:, group % G, bass.ds(group // G * T, T)]

                def scaled(group):
                    dve.wait_ge(a.rb_ready, group + 1)
                    if a.clip:
                        chain.did(v.tensor_copy(vsum, bank[6][:, T:T + 1]))
                        chain.did(v.tensor_tensor(ytmp, bank[6][:, 0:T], rb[:, 0, :], ALU.mult))
                    else:
                        v.tensor_tensor(result_of(group), bank[6][:, 0:T], rb[:, 0, :], ALU.mult).then_inc(a.y_done, 1)

                def floor_added(group):
                    chain.wait(dve)
                    v.scalar_tensor_tensor(result_of(group), rb[:, 1, :], vsum, ytmp, ALU.mult, ALU.add)\
                        .then_inc(a.y_done, 1)

                def body(it, odd, cur=True, prev=True, prev2=True):
                    for j in range(HG):
                        if cur:
                            maxima(it, j)
                        if a.clip:
                            behind = (it - 1, j + 2, prev2, prev) if j < 2 else (it, j - 2, prev, cur)
                            if j >= 2 and prev:
                                floored_factors(it - 1, 2 * j - 4, prev2)
                            if behind[3]:
                                clipped(behind[0], behind[1], 0, behind[2])
                            if cur:
                                clipped_maxima(j)
                            if behind[3]:
                                clipped(behind[0], behind[1], 1, behind[2])
                            if j >= 2 and prev:
                                floored_factors(it - 1, 2 * j - 3, prev2)
                        if prev:
                            evacuate(it - 1, 1 - odd, j)
                    if prev2:
                        scaled(it - 2)
                    if prev:
                        values(it - 1, (it - 1) // G, (it - 1) % G)
                    if prev2 and a.clip:
                        floor_added(it - 2)
                    if prev and not a.clip:
                        factors(it - 1)

                body(0, 0, prev=False, prev2=False)
                aside(2)
                body(1, 1, prev2=False)
                each = 2 * HG + 3 + 2 if a.clip else 1
                with dve.Fori(1, H // 2) as i:
                    chain.enter(i, 1, 2 * each)
                    for k in range(2):
                        body(i * 2 + k, k)
                    chain.leave(H // 2 - 1)
                body(H, 0, cur=False)
                body(H + 1, 1, cur=False, prev=False)

            def cross_latents():
                dve.wait_ge(sx["zT_psum"], 2)
                v.tensor_scalar(kvT[:, 2:4, S2:KEYS], bank[1][:, :].rearrange("p (b t) -> p b t", b=2),
                                col("b", "lnl_g"), col("b", "lnl_b"), ALU.mult, ALU.add).then_inc(sx["zT_dve"], 1)

            def cross_units():
                W3 = 3 * P

                def query_low(count, slot):
                    dve.wait_ge(sx["q_high"], count)
                    v.tensor_tensor(xq_low[:, slot, :], bank[6][:, T:2 * T], xq_high[:, slot, :].bitcast(f32), ALU.subtract)\
                        .then_inc(sx["q_ready"], 1)

                def key_low(b):
                    dve.wait_ge(sx["kv_high"], b + 1)
                    v.tensor_tensor(kv_low[:, b, :], kvT[:, b, :], kv_high[:, b, :].bitcast(f32), ALU.subtract)\
                        .then_inc(sx["kv_split"], 1)

                def maxima(n, u, half):
                    dve.wait_ge(sx["score_psum"], n * 2 + half + 1)
                    v.tensor_reduce(xnegmax[:, u % 2, half:half + 1], banks_pair(half), AX.XY, ALU.max, negate=True)\
                        .then_inc(sx["max_ready"], 1)

                def values(count, b, half):
                    dve.wait_ge(sx["v_psum"], count)
                    v.tensor_copy(xv[:, b, half * W3:(half + 1) * W3], bank[7][:, 0:W3]).then_inc(sx["v_ready"], 1)

                def results(p, hp, b):
                    dve.wait_ge(sx["rb_ready"], p + 1)
                    v.tensor_tensor(oT[:, hp, b * T:(b + 1) * T], bank[6][:, 0:T], xrb[:, :], ALU.mult)\
                        .then_inc(sx["y_done"], 1)

                def body(it, prev, cur):
                    for u in range(8):
                        n, b, odd = it * 8 + u, u // 2, u % 2
                        if cur:
                            maxima(n, u, 0)
                            if odd:
                                query_low(n + 2, (u + 1) % 2)
                        if not odd and (prev or u >= 4):
                            results(it * 4 + b - 2, it - (u < 4), (b - 2) % 4)
                        if cur:
                            values(n + 3, (b + 1) % 4, odd)
                        if (prev and u == 0) or (cur and u):
                            m, mu = n - 1, (u - 1) % 8
                            dve.wait_ge(sx["pT_psum"], m * 3 + 2)
                            v.tensor_copy(xpT[:, (mu // 2) % 2, mu % 2, 2 * T:4 * T], bank[4 + (3 * mu + 1) % 2][:, :])\
                                .then_inc(sx["pT_dve"], 1)
                        if not odd and ((prev and u == 0) or (cur and u)):
                            dve.wait_ge(sx["exp_done"], n * 2)
                            link(v.reciprocal(xr[:, :], xsums[:, ((u - 2) % 8 // 2) % 2, :, :].rearrange("p h a -> p (h a)")))
                            v.tensor_copy(xrbc[:, :, :].rearrange("p h (a r) -> p (h a) r", a=2), spread(xr[:, :], XD))\
                                .then_inc(sx["rbc_ready"], 1)
                        if cur:
                            if not odd:
                                query_low(n + 2, (u + 1) % 2)
                            maxima(n, u, 1)
                        if not cur and u == 2:
                            break

                v.memset(xrb[:, 0:1], 0.0).then_inc(sx["y_done"], 1)
                query_low(1, 0)
                values(1, 0, 0)
                values(2, 0, 1)
                for b in range(B):
                    key_low(b)
                body(0, False, True)
                with dve.Fori(1, XP) as it:
                    chain.enter(it, 1, 4)
                    body(it, True, True)
                    chain.leave(XP - 1)
                body(XP, True, False)

            def top(src, out, value, key, shape_e, ramp):
                link(v.tensor_reduce(value, src, AX.X, ALU.max))
                link(v.tensor_tensor(out, src, spread(value, shape_e), ALU.is_equal))
                link(v.tensor_tensor(out, out, ramp.unsqueeze(1).broadcast_to([P, NT, shape_e]), ALU.mult))
                link(v.tensor_reduce(key, out, AX.X, ALU.max))
                link(v.tensor_tensor(out, out, spread(key, shape_e), ALU.is_equal))

            def experts():
                def z_low_half(h):
                    half_of = slice(h * BANK, (h + 1) * BANK)
                    dve.wait_ge(sf["z_high"], h + 1)
                    v.tensor_tensor(z_low[:, half_of], zT[:, half_of], z_high[:, half_of].bitcast(f32), ALU.subtract)\
                        .then_inc(sf["z_split"], 1)

                def weight_low(e, slot):
                    dve.wait_ge(sf["w1_high"], e + 1)
                    v.tensor_tensor(w1_low[:, slot, :], w1b[:, slot, :], w1_high[:, slot, :].bitcast(f32), ALU.subtract)\
                        .then_inc(sf["w1_split"], 1)

                for h in range(2):
                    dve.wait_ge(att1.out_psum, h + 1)
                    v.tensor_tensor(quarter(xin, h), quarter(z, h), tiles(bank[h][:, :]), ALU.add)\
                        .then_inc(sf["xin_ready"], 1)
                    centre([("ln2", h)])
                    if h:
                        z_low_half(0)
                    variances([("ln2", h)])
                    if h == 0:
                        weight_low(0, 0)
                    scale([("ln2", h)])
                link(v.tensor_tensor(x[:, :, :], x[:, :, :], xin, ALU.add))
                z_low_half(1)
                dve.wait_ge(sf["gate_psum"], 1)
                link(v.tensor_copy(gates, bank[2][:, 0:NT * (E + 2)].rearrange("p (t e) -> p t e", t=NT)))
                ge, gc = gates[:, :, 0:E], gates[:, :, E:E + 2]
                link(v.tensor_tensor(gc, gc, col("f", "coef_b").unsqueeze(1).broadcast_to([P, NT, 2]), ALU.add))
                link(v.tensor_reduce(g1[:, 0, :], ge, AX.X, ALU.max))
                link(v.tensor_reduce(g1[:, 1, :], gc, AX.X, ALU.max))
                link(v.tensor_tensor(ge, ge, spread(g1[:, 0, :], E), ALU.subtract))
                v.tensor_tensor(gc, gc, spread(g1[:, 1, :], 2), ALU.subtract).then_inc(sf["gate_shifted"], 1)
                dve.wait_ge(sf["gate_exp"], 1)
                link(v.tensor_reduce(g1[:, 2, :], ge, AX.X, ALU.add))
                link(v.tensor_reduce(g1[:, 3, :], gc, AX.X, ALU.add))
                link(v.reciprocal(g1[:, 2:4, :], g1[:, 2:4, :]))
                link(v.tensor_tensor(probs, ge, spread(g1[:, 2, :], E), ALU.mult))
                link(v.tensor_tensor(coef, gc, spread(g1[:, 3, :], 2), ALU.mult))
                top(probs, pick, g1[:, 4, :], g1[:, 5, :], E, col("f", "ramp"))
                link(v.tensor_tensor(g1[:, 6, :], g1[:, 4, :], coef[:, :, 0:1].rearrange("p t a -> p (t a)"), ALU.mult))
                link(v.tensor_tensor(route[:, :, 0:E], pick, spread(g1[:, 6, :], E), ALU.mult))
                v.tensor_copy(route[:, :, E:E + 1], coef[:, :, 1:2]).then_inc(sf["route_ready"], 1)
                weight_low(1, 1)
                dve.wait_ge(sf["routeT_psum"], 1)
                v.tensor_copy(routeT[0:E + 1, BANK:2 * BANK], bank[3][0:E + 1, :]).then_inc(sf["routeT_ready"], 1)
                for h in range(2):
                    dve.wait_ge(sf["bias_psum"], h + 1)
                    v.tensor_tensor(quarter(x, h), quarter(x, h), tiles(bank[2 + h][:, :]), ALU.add)\
                        .then_inc(sf["mixed"], 1)

                def expert(e, slot, split=True, last=False):
                    if split:
                        weight_low(e + 1, 1 - slot)
                    for c in range(2):
                        dve.wait_ge(sf["down_psum"], e * 2 + c + 1)
                        dve.wait_ge(sf["mixed"], e * 2 + c + 1)
                        for t in range(4 * c, 4 * c + 4):
                            done = v.scalar_tensor_tensor(x[:, t, :], bank[2 * slot + c][:, (t % 4) * P:(t % 4 + 1) * P],
                                                          route[:, t, bass.ds(e, 1)], x[:, t, :], ALU.mult, ALU.add)
                        done.then_inc(x_done if last else sf["mixed"], 1)
                        if last:
                            normalise([("n3", c)])

                expert(0, 0, split=False)
                with dve.Fori(0, E // 2 - 1) as i:
                    for k in range(2):
                        expert(i * 2 + k + 1, 1 - k)
                expert(E - 1, 1)
                expert(E, 0, split=False, last=True)

            def single():
                def values(c, count):
                    dve.wait_ge(sg["proj_psum"], count)
                    v.tensor_tensor(quarter(vx, c), tiles(bank[(6, 7, 2, 3)[c]][:, :]),
                                    col("l", "bv4").unsqueeze(1).broadcast_to([P, 4, D]), ALU.add)\
                        .then_inc(sg["proj_dve"], 1)

                def queries(c, count):
                    dve.wait_ge(sg["proj_psum"], count)
                    v.tensor_scalar(qx[:, c * BANK:(c + 1) * BANK], bank[4 + c][:, :], col("l", "bq4"), D ** -0.5,
                                    ALU.add, ALU.mult).then_inc(sg["proj_dve"], 1)

                centre([("n4", 1)])
                variances([("n4", 1)])
                values(0, 5)
                values(1, 6)
                scale([("n4", 1)])
                queries(0, 8)
                values(2, 7)
                values(3, 9)
                dve.wait_ge(loaded["mask"], 16)
                for n in range(NT + 2):
                    if n == 2:
                        queries(1, 10)
                    if n < NT:
                        dve.wait_ge(sg["score_psum"], n + 1)
                        if n >= 2:
                            dve.wait_ge(sg["exp_done"], n - 1)
                        chain.did(v.tensor_tensor(sm[:, n % 2, :], bank[SINGLE_BANKS[n % 4]][:, :], maskx[:, n % 2, :],
                                                  ALU.add))
                    if n >= 2:
                        m = n - 2
                        chain.did(v.reciprocal(r1[:, m:m + 1], sm1[:, m:m + 1]))
                    chain.wait(dve)
                    if n < NT:
                        v.tensor_reduce(nm1[:, n:n + 1], sm[:, n % 2, :], AX.X, ALU.max, negate=True)\
                            .then_inc(sg["max_ready"], 1)
                    if n >= 2:
                        dve.wait_ge(sg["out_psum"], m + 1)
                        last = v.scalar_tensor_tensor(x[:, m, :], bank[4 + m % 2][:, 0:D], r1[:, m:m + 1], x[:, m, :],
                                                      ALU.mult, ALU.add)
                        last.then_inc(x_parts, 1)
                        if m % 4 == 3:
                            dve.wait_ge(x_parts, m + 1)
                            dve.sem_inc(x_done, 1)
                    if 6 <= n < 9:
                        (centre, variances, scale)[n - 6]([("n5", 0)])

            def mixture():
                normalise([("n5", 1)])
                dve.wait_ge(sl["zT_psum"], 2)
                v.tensor_copy(zT[:, BANK:2 * BANK], bank[1][:, :]).then_inc(sl["zT_dve"], 1)
                dve.wait_ge(sl["gate_psum"], 2)
                link(v.tensor_tensor(lg, bank[4][:, 0:NT * E2].rearrange("p (t e) -> p t e", t=NT),
                                     col("l", "router_b").unsqueeze(1).broadcast_to([P, NT, E2]), ALU.add))
                link(v.tensor_reduce(l1[:, 0, :], lg, AX.X, ALU.max))
                v.tensor_tensor(lg, lg, spread(l1[:, 0, :], E2), ALU.subtract).then_inc(sl["gate_shifted"], 1)
                link(v.memset(lw[:, :, 0:1], 1.0))
                dve.wait_ge(sl["gate_exp"], 1)
                link(v.tensor_reduce(l1[:, 1, :], lp, AX.X, ALU.add))
                link(v.reciprocal(l1[:, 1, :], l1[:, 1, :]))
                link(v.tensor_tensor(lp, lp, spread(l1[:, 1, :], E2), ALU.mult))
                ramp = col("f", "ramp")[:, 0:E2]
                top(lp, lpick, l1[:, 2, :], l1[:, 3, :], E2, ramp)
                link(v.scalar_tensor_tensor(lg, lpick, -2.0, lp, ALU.mult, ALU.add))
                top(lg, lsel, l1[:, 4, :], l1[:, 5, :], E2, ramp)
                link(v.tensor_tensor(lsel, lsel, lpick, ALU.add))
                link(v.tensor_tensor(lsel, lsel, lp, ALU.mult))
                link(v.tensor_reduce(l1[:, 6, :], lsel, AX.X, ALU.add))
                link(v.tensor_scalar(l1[:, 6, :], l1[:, 6, :], TINY, None, ALU.add))
                link(v.reciprocal(l1[:, 6, :], l1[:, 6, :]))
                v.tensor_tensor(lw[:, :, 1:E2 + 1], lsel, spread(l1[:, 6, :], E2), ALU.mult).then_inc(sl["route_ready"], 1)
                for h in range(2):
                    add_to_x(sl["base_psum"], h, h, sl["base_added"])
                dve.wait_ge(sl["low_ready"], 2)
                for c in range(2):
                    dve.wait_ge(sl["wide_psum"], c + 1)
                    v.tensor_tensor(lowTm[0:RU, c * BANK:(c + 1) * BANK], lowT[0:RU, c * BANK:(c + 1) * BANK],
                                    bank[4 + 3 * c][0:RU, :], ALU.mult).then_inc(sl["mixed"], 1)
                dve.wait_ge(sl["base_added"], 2)
                for h in range(2):
                    add_to_x(sl["out_psum"], h, 2 + h)

            v.memset(ones[:, :], 1.0).then_inc(constants, 1)
            v.memset(low_bias[:, :], -CLIP).then_inc(constants, 1)
            centre(FIRST_JOBS)
            variances(FIRST_JOBS)
            dve.wait_ge(loaded["a"], 16)
            effective_weights()
            scale(FIRST_JOBS)
            attention(att0, col("a", "bq0"), col("a", "bv0"),
                      [[(effective_projection,), (centre, CONTEXT_JOBS[0])], [(variances, CONTEXT_JOBS[0])],
                       [(scale, CONTEXT_JOBS[0]), (centre, CONTEXT_JOBS[1]), (variances, CONTEXT_JOBS[1])]])
            scale(CONTEXT_JOBS[1])
            add_to_x(att0.out_psum, 0, 0)
            centre([("n1", 0)])
            variances([("n1", 0)])
            add_to_x(att0.out_psum, 1, 1)
            centre([("n1", 1)])
            scale([("n1", 0)])
            centre([("lat", 0)])
            variances([("n1", 1)])
            scale([("n1", 1)])
            variances([("lat", 0)])
            centre([("lat", 1)])
            scale([("lat", 0)])
            variances([("lat", 1)])
            scale([("lat", 1)])
            cross_latents()
            cross_units()
            add_to_x(sx["out_psum"], 0, 0)
            normalise([("n2", 0)])
            centre([("ln1", 0)])
            add_to_x(sx["out_psum"], 1, 1)
            variances([("ln1", 0)])
            centre([("n2", 1)])
            scale([("ln1", 0)])
            variances([("n2", 1)])
            scale([("n2", 1)])
            centre([("ln1", 1)])
            dve.wait_ge(loaded["f"], 16)
            attention(att1, col("f", "bq2"), col("f", "bv2"), [[(variances, [("ln1", 1)]), (scale, [("ln1", 1)])], [], []])
            experts()
            dve.wait_ge(loaded["l"], 16)
            attention(att2, col("l", "zero"), col("l", "zeros"))
            for h in range(2):
                add_to_x(att2.out_psum, h, h)
                if h == 0:
                    normalise([("n4", 0)])
            single()
            mixture()

        @block.gpsimd
        def _(pool):
            done = [0]

            def link(instruction):
                instruction.then_inc(pool_chain, 1)
                done[0] += 1
                pool.wait_ge(pool_chain, done[0])

            def rstd_jobs(keys):
                for key in keys:
                    k = jobs[key][0]
                    pool.wait_ge(var_ready, k + 1)
                    link(pool.tensor_scalar(stat[:, k % 4, 2, :], stat[:, k % 4, 1, :], 1.0 / D, EPS, ALU.mult, ALU.add))
                    pool.tensor_tensor(stat[:, k % 4, 3, :], stat[:, k % 4, 2, :], half[:, :], ALU.pow)\
                        .then_inc(rstd_ready, 1)

            def attention(a, asides=((), ())):
                pool.wait_ge(a.qv_ready, 1)
                headmask = col("a", "headmask")

                def body(it, b, g, prev):
                    for j in range(HG):
                        if prev:
                            pool.wait_ge(a.score_psum, it * HG + j - 3)
                        pool.tensor_tensor(qm[:, j, :], qT[:, bass.ds(b * T, T)],
                                           headmask[:, bass.ds(g * HG + j, 1)].broadcast_to([P, T]), ALU.mult)\
                            .then_inc(a.qm_ready, 1)

                def repeated(group):
                    pool.wait_ge(a.factors_ready, group + 1)
                    pool.wait_ge(a.y_done, group + 1)
                    once = ones[:, 0:2 * P].rearrange("p (j r) -> p j r", r=ROWS)
                    pool.tensor_tensor(over_rows(0), spread(factor, ROWS), once, ALU.mult)
                    pool.tensor_tensor(over_rows(1), spread(floor_factor, ROWS), once, ALU.mult)\
                        .then_inc(a.rbc_ready, 1)

                body(0, 0, 0, False)
                rstd_jobs(asides[0])
                body(1, 0, 1, True)
                rstd_jobs(asides[1])
                pool.wait_ge(a.qv_ready, 3)
                with pool.Fori(1, H // 2) as i:
                    for k in range(2):
                        it = i * 2 + k
                        body(it, it // G, it % G, True)
                        if a.clip:
                            repeated(it - 2)
                if a.clip:
                    repeated(H - 2)
                    repeated(H - 1)

            def cross():
                def pair(it, prev):
                    for u in range(2):
                        if prev:
                            pool.wait_ge(sx["q_psum"], it * 8 - 1 + u)
                        pool.tensor_copy(acur[:, u, :], A_flat[:, bass.ds(it * 2 * P + u * P, P)])\
                            .then_inc(sx["acur_ready"], 1)

                pool.wait_ge(prep_act, 5)
                pair(0, False)
                with pool.Fori(1, XP + 1) as it:
                    pair(it, True)

            pool.memset(half[:, :], -0.5).then_inc(pool_chain, 1)
            done[0] += 1
            pool.wait_ge(pool_chain, 1)
            rstd_jobs(FIRST_JOBS)
            pool.wait_ge(loaded["a"], 16)
            attention(att0, CONTEXT_JOBS)
            rstd_jobs([("n1", 0), ("n1", 1), ("lat", 0), ("lat", 1)])
            cross()
            rstd_jobs([("n2", 0), ("ln1", 0), ("n2", 1), ("ln1", 1)])
            attention(att1)
            rstd_jobs([("ln2", 0), ("ln2", 1)])
            rstd_jobs([("n3", 0), ("n3", 1)])
            attention(att2)
            rstd_jobs([("n4", 0), ("n4", 1)])
            rstd_jobs([("n5", 0), ("n5", 1)])


def _arrange(inputs):
    f = lambda n: np.asarray(inputs[n])

    def rows(a, n=P):
        out = np.zeros((n,) + a.shape[1:], np.float32)
        out[:a.shape[0]] = a
        return out

    def column(v):
        return np.ascontiguousarray(v).reshape(-1, 1)

    def repeated(v):
        return np.broadcast_to(v.reshape(1, -1), (P, v.size))

    def grouped(w, bias=None):
        out = np.zeros((HG, ROWS, G, w.shape[1]), np.float32)
        out[:, :HD] = w.reshape(G, HG, HD, -1).transpose(1, 2, 0, 3)
        if bias is not None:
            out[0, HD, 0] = bias
        return out.reshape(P, G * w.shape[1])

    qkv = f("L0_attn_b_attn").reshape(3, D)
    b2 = f("L0_ffn_bqkv").reshape(3, D)
    wx = f("L0_xattn_Wkv")
    wv = np.concatenate([wx[:, XH * XD:], wx[:, XH * XD:XH * XD + P]], 1)

    def pairs(w):
        return np.ascontiguousarray(w.T).reshape(XP, P, D).transpose(1, 0, 2).reshape(P, XP * D)

    low_rows = np.concatenate([f("L1_ffn_shared_A")[None], f("L1_ffn_routed_A")]).reshape(RU, D)
    low_cols = np.concatenate([f("L1_ffn_shared_B").T[None], f("L1_ffn_routed_B").transpose(0, 2, 1)]).reshape(RU, D)
    c = {
        "ident": np.eye(P, dtype=np.float32),
        "headmask": (np.arange(P)[:, None] // HD == np.arange(H)[None]).astype(np.float32),
        "causal": np.where(np.arange(P)[None] <= np.arange(P)[:, None], 0.0, MASKED).astype(np.float32),
        "la0": rows(f("L0_attn_la_attn")), "lb0": rows(f("L0_attn_lb_attn").T), "w0": f("L0_attn_w_attn").T,
        "bq0": column(qkv[0]), "bk0": column(qkv[1]), "bv0": repeated(qkv[2]),
        "lap0": rows(grouped(f("L0_attn_la_proj").T).reshape(P, G, RL).transpose(2, 1, 0).reshape(RL, G * P)),
        "lbp0": rows(f("L0_attn_lb_proj").T), "wp0": grouped(f("L0_attn_w_proj").T, f("L0_attn_b_proj")),
        "lnm_g": column(f("L0_xattn_ln_m_g")), "lnm_b": column(f("L0_xattn_ln_m_b")),
        "lnl_g": column(f("L0_xattn_ln_l_g")), "lnl_b": column(f("L0_xattn_ln_l_b")),
        "wqT": pairs(f("L0_xattn_Wq")), "wkT": pairs(wx[:, :XH * XD]), "wv": wv,
        "wout": f("L0_xattn_Wout").reshape(XP, P, D).transpose(1, 0, 2).reshape(P, XP * D),
        "ln1_g": column(f("L0_ffn_ln1_g")), "ln1_b": column(f("L0_ffn_ln1_b")), "w2": f("L0_ffn_Wqkv"),
        "bq2": column(b2[0]), "bk2": column(b2[1]), "bv2": repeated(b2[2]),
        "wp2": grouped(f("L0_ffn_Wo"), f("L0_ffn_bo")),
        "ln2_g": column(f("L0_ffn_ln2_g")), "ln2_b": column(f("L0_ffn_ln2_b")),
        "gate": np.concatenate([f("L0_ffn_gate_w"), f("L0_ffn_coef_w")], 1), "coef_b": repeated(f("L0_ffn_coef_b")),
        "ramp": np.broadcast_to(np.arange(E, 0, -1, dtype=np.float32), (P, E)),
        "b1": np.concatenate([f("L0_ffn_b1"), f("L0_ffn_rb1")[None]]).reshape(E + 1, 1, FT, P).repeat(2, 1)
        .reshape((E + 1) * 2 * FT, P).T,
        "b2": rows(np.concatenate([f("L0_ffn_b2"), f("L0_ffn_rb2")[None]])),
        "w3": f("L1_attn_w_qkv").T, "zero": np.zeros((P, 1), np.float32), "zeros": np.zeros((P, D), np.float32),
        "wp3": grouped(f("L1_attn_w_proj").T),
        "wq4": f("L1_xattn_kernel_q"), "wk4": f("L1_xattn_kernel_k"), "wv4": f("L1_xattn_kernel_v"),
        "bq4": column(f("L1_xattn_bias_q")), "bk4": column(f("L1_xattn_bias_k")), "bv4": repeated(f("L1_xattn_bias_v")),
        "base": f("L1_ffn_base_W").T, "lowA": low_rows.T, "lowB": rows(low_cols),
        "base_b": rows(f("L1_ffn_base_b").reshape(1, D)), "router": f("L1_ffn_router_W").T,
        "router_b": repeated(f("L1_ffn_router_b")),
        "sel7": rows((np.arange(E2 + 1)[:, None] == np.arange(RU)[None] // R2).astype(np.float32)),
    }
    arrays = {f"pack_{key}": np.concatenate([c[n] for n, _ in columns], 1) for key, columns in LAYOUT.items()}
    arrays["x"] = f("x")
    arrays["ctx"] = f("ctx_1024")
    arrays["mask"] = f("mask_1xSxS2_ff0")
    arrays["w1"] = np.concatenate([f("L0_ffn_W1"), f("L0_ffn_rW1")[None]])
    arrays["w2"] = np.concatenate([f("L0_ffn_W2"), f("L0_ffn_rW2")[None]]).reshape(E + 1, FT, P, D)\
        .transpose(0, 2, 1, 3).reshape(E + 1, P, FT * D)
    return arrays


def kernel(**inputs):
    import concourse.bacc as _bacc
    from concourse.bass_utils import run_bass_kernel_spmd as _run

    nc = _bacc.Bacc("TRN2", target_bir_lowering=False, num_devices=1)
    arrays = {f"in_{n}": np.ascontiguousarray(a) for n, a in _arrange(inputs).items()}
    d = {n[3:]: nc.dram_tensor(n, a.shape, mybir.dt.from_np(a.dtype), kind="ExternalInput").ap() for n, a in arrays.items()}
    out = nc.dram_tensor("out", (B, T, D), mybir.dt.float32, kind="ExternalOutput").ap()
    decoder(nc, d["x"], d["ctx"], d["mask"], {k: d[f"pack_{k}"] for k in LAYOUT}, d["w1"], d["w2"], out)
    return _run(nc, [arrays], core_ids=[0]).results[0]["out"]
```
